# Optimizing a Trainium2 kernel written in Bass

```python
import numpy as np
import jax
import jax.numpy as jnp

def _softmax(x, axis=-1):
    return jax.nn.softmax(x, axis=axis)

def _gelu(x):
    return jax.nn.gelu(x, approximate=True)

def _silu(x):
    return jax.nn.silu(x)

def _sigmoid(x):
    return jax.nn.sigmoid(x)

def _layernorm(x, axis=-1, eps=1e-05):
    m = jnp.mean(x, axis=axis, keepdims=True)
    v = jnp.var(x, axis=axis, keepdims=True)
    return (x - m) / jnp.sqrt(v + eps)

def _scatter_add(tgt, idx, src, axis=0):
    return tgt.at[idx].add(src)

def _segment_sum(src, seg, n):
    return jax.ops.segment_sum(src, seg, n)
kernel_name = 'mk_decoder_postln_d2_seqx_r8_c1ad85'

def setup_inputs(seed: int=0):
    np.random.seed(seed)
    _w = jnp.asarray

    def _rec_inputs():
        import jax
        import jax.numpy as jnp
        _rk = jax.random.key(seed)
        x = 7.22e-05 + 1 * jax.random.normal(jax.random.fold_in(_rk, 1), (16, 100, 256), jnp.float32)
        _lenS = 100 - jax.random.randint(jax.random.fold_in(_rk, 7), (16,), 0, max(1, 100 // 4) + 1, jnp.int32)
        _lenS2 = 1444 - jax.random.randint(jax.random.fold_in(_rk, 8), (16,), 0, max(1, 1444 // 4) + 1, jnp.int32)
        _ctx_2048P = jax.random.normal(jax.random.fold_in(_rk, 11), (16, 16, 256), jnp.float32)
        _ctx_2048c = jax.random.dirichlet(jax.random.fold_in(_rk, 511), 0.3 * jnp.ones((16,), jnp.float32), (16, 1444))
        _ctx_2048t = jnp.einsum('bsk,bkd->bsd', _ctx_2048c, _ctx_2048P)
        _ctx_2048t = _ctx_2048t * jax.lax.rsqrt(jnp.mean(jnp.square(_ctx_2048t)) + 1e-12) * 0.953939
        ctx_2048 = 4.13588e-05 + 0.999923 * (_ctx_2048t + 0.3 * jax.random.normal(jax.random.fold_in(_rk, 611), (16, 1444, 256), jnp.float32))
        _validS = jnp.arange(100)[None, :] < _lenS[:, None]
        _validS2 = jnp.arange(1444)[None, :] < _lenS2[:, None]
        _causal = jnp.tril(jnp.ones((100, 100), dtype=bool))
        mask_BxS2_ik0 = jnp.where(jnp.broadcast_to(_validS2[:, :], (16, 1444)), 0, 1).astype(jnp.int32)
        return (x, ctx_2048, mask_BxS2_ik0)
    x, ctx_2048, mask_BxS2_ik0 = _rec_inputs()

    def _L0_attn_setup():
        import jax, jax.numpy as jnp
        import numpy as np
        D_MODEL = 256
        N_HEADS = 16
        HEAD_DIM = D_MODEL // N_HEADS
        EPS = 1e-06

        def _rmsnorm(x, w):
            return x * jax.lax.rsqrt(jnp.mean(x * x, axis=-1, keepdims=True) + EPS) * w
        key = jax.random.key(seed)
        ks = jax.random.split(key, 9)
        B, T, D = (2, 256, D_MODEL)
        x = jax.random.normal(ks[0], (B, T, D), dtype=jnp.float32)
        lim = float(np.sqrt(6.0 / (D + D)))

        def xavier(k):
            return jax.random.uniform(k, (D, D), dtype=jnp.float32, minval=-lim, maxval=lim)
        return {'x': x, 'norm_w': jnp.ones((D,), dtype=jnp.float32), 'wq': xavier(ks[1]), 'bq': jnp.zeros((D,), jnp.float32), 'wk': xavier(ks[2]), 'bk': jnp.zeros((D,), jnp.float32), 'wv': xavier(ks[3]), 'bv': jnp.zeros((D,), jnp.float32), 'wo': xavier(ks[4]), 'bo': jnp.zeros((D,), jnp.float32)}
    _L0_attn_all = _L0_attn_setup()
    _L0_attn_in = {k: v for k, v in _L0_attn_all.items() if k in ('norm_w', 'wq', 'bq', 'wk', 'bk', 'wv', 'bv', 'wo', 'bo')}
    del _L0_attn_all

    def _L0_xattn_setup():
        import math
        import jax, jax.numpy as jnp
        import numpy as np
        HEADS = 16
        MASKED_BIAS = -10000.0

        def _mha(q, k, v):
            B, Sq, D = q.shape
            Sk = k.shape[-2]
            hd = D // HEADS
            qh = q.reshape(B, Sq, HEADS, hd).transpose(0, 2, 1, 3)
            kh = k.reshape(B, Sk, HEADS, hd).transpose(0, 2, 1, 3)
            vh = v.reshape(B, Sk, HEADS, hd).transpose(0, 2, 1, 3)
            scores = jnp.einsum('bhqd,bhkd->bhqk', qh, kh) / math.sqrt(hd)
            qi = jnp.arange(Sq)[:, None] + (Sk - Sq)
            ki = jnp.arange(Sk)[None, :]
            causal = ki <= qi
            scores = jnp.where(causal[None, None], scores, jnp.asarray(MASKED_BIAS, scores.dtype))
            attn = jax.nn.softmax(scores, axis=-1)
            out = jnp.einsum('bhqk,bhkd->bhqd', attn, vh)
            return out.transpose(0, 2, 1, 3).reshape(B, Sq, D)
        key = jax.random.key(seed)
        kq, kk, kv = jax.random.split(key, 3)
        B, S, D = (4, 128, 256)
        q = jax.random.normal(kq, (B, S, D), dtype=jnp.float32)
        k = jax.random.normal(kk, (B, S, D), dtype=jnp.float32)
        v = jax.random.normal(kv, (B, S, D), dtype=jnp.float32)
        return {'q': q, 'k': k, 'v': v}
    _L0_xattn_all = _L0_xattn_setup()
    _L0_xattn_in = {k: v for k, v in _L0_xattn_all.items() if k in ()}
    del _L0_xattn_all

    def _L0_ffn_setup():
        import jax, jax.numpy as jnp
        import numpy as np
        H = 256
        NH = 16
        NOPE = 128
        ROPE = 64
        VD = 128
        QHD = NOPE + ROPE
        E = 16
        I = 176
        TOPK = 4
        NSH = 2
        SHI = I * NSH
        EPS = 1e-06
        B, S = (2, 128)

        def rmsnorm(x, w):
            return x * jax.lax.rsqrt(jnp.mean(x * x, axis=-1, keepdims=True) + EPS) * w
        key = jax.random.key(seed)
        ks = jax.random.split(key, 12)
        sd = lambda fan_in: 1.0 / np.sqrt(fan_in)
        return {'hidden_states': jax.random.normal(ks[0], (B, S, H), jnp.float32), 'positions': jnp.broadcast_to(jnp.arange(S, dtype=jnp.int32), (B, S)), 'ln1_w': jnp.ones((H,), jnp.float32), 'ln2_w': jnp.ones((H,), jnp.float32), 'q_w': jax.random.normal(ks[1], (NH * QHD, H), jnp.float32) * sd(H), 'kv_w': jax.random.normal(ks[2], (NH * (NOPE + VD) + ROPE, H), jnp.float32) * sd(H), 'o_w': jax.random.normal(ks[3], (H, NH * VD), jnp.float32) * sd(NH * VD), 'gate_w': jax.random.normal(ks[4], (E, H), jnp.float32) * sd(H), 'w1': jax.random.normal(ks[5], (E, 2 * I, H), jnp.float32) * sd(H), 'w2': jax.random.normal(ks[6], (E, H, I), jnp.float32) * sd(I), 'sh_gu_w': jax.random.normal(ks[7], (2 * SHI, H), jnp.float32) * sd(H), 'sh_down_w': jax.random.normal(ks[8], (H, SHI), jnp.float32) * sd(SHI)}
    _L0_ffn_all = _L0_ffn_setup()
    _L0_ffn_in = {k: v for k, v in _L0_ffn_all.items() if k in ('positions', 'ln1_w', 'ln2_w', 'q_w', 'kv_w', 'o_w', 'gate_w', 'w1', 'w2', 'sh_gu_w', 'sh_down_w')}
    del _L0_ffn_all

    def _L1_attn_setup():
        import jax, jax.numpy as jnp
        import numpy as np
        NUM_HEADS = 16
        ROPE_BASE = 10000.0

        def _rope_tables(seq_len, head_dim, scaling_factor=1.0):
            inv_freq = 1.0 / ROPE_BASE ** (jnp.arange(0, head_dim, 2, dtype=jnp.float32) / head_dim)
            t = jnp.arange(seq_len, dtype=jnp.float32) * scaling_factor
            freqs = jnp.einsum('i,j->ij', t, inv_freq)
            c = jnp.sin(freqs)
            s = jnp.cos(freqs)
            return (c, s)

        def _apply_rope(x, c, s):
            x1, x2 = jnp.split(x, 2, axis=-1)
            c = c[None, None]
            s = s[None, None]
            return jnp.concatenate([x1 * c - x2 * s, x1 * s + x2 * c], axis=-1)
        key = jax.random.key(seed)
        ks = jax.random.split(key, 5)
        B, S, H = (4, 256, 256)
        x = jax.random.normal(ks[0], (B, S, H), dtype=jnp.float32)
        scale = 1.0 / np.sqrt(H)
        Wq = jax.random.normal(ks[1], (H, H), dtype=jnp.float32) * scale
        Wk = jax.random.normal(ks[2], (H, H), dtype=jnp.float32) * scale
        Wv = jax.random.normal(ks[3], (H, H), dtype=jnp.float32) * scale
        Wo = jax.random.normal(ks[4], (H, H), dtype=jnp.float32) * scale
        return {'x': x, 'Wq': Wq, 'Wk': Wk, 'Wv': Wv, 'Wo': Wo}
    _L1_attn_all = _L1_attn_setup()
    _L1_attn_in = {k: v for k, v in _L1_attn_all.items() if k in ('Wq', 'Wk', 'Wv', 'Wo')}
    del _L1_attn_all

    def _L1_xattn_setup():
        import jax, jax.numpy as jnp
        import numpy as np
        import math
        H = 256
        NH = 16
        HD = H // NH
        EPS_LN = 1e-05
        RES_SCALE_MAX = 0.3

        def _nan_clean(x, lim=10000.0):
            return jnp.nan_to_num(x, nan=0.0, posinf=lim, neginf=-lim)
        key = jax.random.key(seed)
        ks = jax.random.split(key, 12)
        B, S, T = (4, 256, 32)
        std = 1.0 / math.sqrt(H)
        return {'hidden_states': jax.random.normal(ks[0], (B, S, H), jnp.float32), 'audio_tokens': jax.random.normal(ks[1], (B, T, H), jnp.float32), 'attention_mask': jax.random.randint(ks[2], (B, T), 0, 2, jnp.int32), 'Wq': jax.random.normal(ks[3], (H, H), jnp.float32) * std, 'bq': jnp.zeros((H,), jnp.float32), 'Wk': jax.random.normal(ks[4], (H, H), jnp.float32) * std, 'bk': jnp.zeros((H,), jnp.float32), 'Wv': jax.random.normal(ks[5], (H, H), jnp.float32) * std, 'bv': jnp.zeros((H,), jnp.float32), 'Wo': jax.random.normal(ks[6], (H, H), jnp.float32) * std, 'bo': jnp.zeros((H,), jnp.float32), 'ln_gamma': jnp.ones((H,), jnp.float32), 'ln_beta': jnp.zeros((H,), jnp.float32), 'residual_scale': jnp.float32(0.05)}
    _L1_xattn_all = _L1_xattn_setup()
    _L1_xattn_in = {k: v for k, v in _L1_xattn_all.items() if k in ('Wq', 'bq', 'Wk', 'bk', 'Wv', 'bv', 'Wo', 'bo', 'ln_gamma', 'ln_beta', 'residual_scale')}
    del _L1_xattn_all

    def _L1_ffn_setup():
        import jax, jax.numpy as jnp
        import numpy as np
        CAPACITY_FACTOR = 1.0

        def _top1_gate(x, w_gate):
            S, E = (x.shape[0], w_gate.shape[1])
            capacity = int(CAPACITY_FACTOR * S / E)
            logits = x @ w_gate
            gates = jax.nn.softmax(logits, axis=-1)
            idx1 = jnp.argmax(gates, axis=-1)
            mask1 = jax.nn.one_hot(idx1, E, dtype=gates.dtype)
            locations1 = jnp.cumsum(mask1, axis=0) - mask1
            mask1 = mask1 * (locations1 < capacity)
            locations1_s = jnp.sum(locations1 * mask1, axis=1).astype(jnp.int32)
            gates_masked = gates * mask1
            loc_oh = jax.nn.one_hot(locations1_s, capacity, dtype=gates.dtype) * jnp.sum(mask1, axis=1, keepdims=True)
            combine_weights = jnp.einsum('se,sc->sec', gates_masked, loc_oh)
            dispatch_mask = (combine_weights > 0).astype(gates.dtype)
            return (combine_weights, dispatch_mask)
        key = jax.random.key(seed)
        k1, k2, k3, k4 = jax.random.split(key, 4)
        B, T, D, E, F = (4, 256, 256, 8, 1024)
        hidden_states = jax.random.normal(k1, (B, T, D), dtype=jnp.float32)
        w_gate = jax.random.normal(k2, (D, E), dtype=jnp.float32) * 0.02
        w1 = jax.random.normal(k3, (E, D, F), dtype=jnp.float32) * 0.02
        w2 = jax.random.normal(k4, (E, F, D), dtype=jnp.float32) * 0.02
        return {'hidden_states': hidden_states, 'w_gate': w_gate, 'w1': w1, 'w2': w2}
    _L1_ffn_all = _L1_ffn_setup()
    _L1_ffn_in = {k: v for k, v in _L1_ffn_all.items() if k in ('w_gate', 'w1', 'w2')}
    del _L1_ffn_all
    return {'x': x, 'ctx_2048': ctx_2048, 'mask_BxS2_ik0': mask_BxS2_ik0, 'L0_attn_norm_w': _L0_attn_in['norm_w'], 'L0_attn_wq': _L0_attn_in['wq'], 'L0_attn_bq': _L0_attn_in['bq'], 'L0_attn_wk': _L0_attn_in['wk'], 'L0_attn_bk': _L0_attn_in['bk'], 'L0_attn_wv': _L0_attn_in['wv'], 'L0_attn_bv': _L0_attn_in['bv'], 'L0_attn_wo': _L0_attn_in['wo'], 'L0_attn_bo': _L0_attn_in['bo'], 'L0_ffn_positions': _L0_ffn_in['positions'], 'L0_ffn_ln1_w': _L0_ffn_in['ln1_w'], 'L0_ffn_ln2_w': _L0_ffn_in['ln2_w'], 'L0_ffn_q_w': _L0_ffn_in['q_w'], 'L0_ffn_kv_w': _L0_ffn_in['kv_w'], 'L0_ffn_o_w': _L0_ffn_in['o_w'], 'L0_ffn_gate_w': _L0_ffn_in['gate_w'], 'L0_ffn_w1': _L0_ffn_in['w1'], 'L0_ffn_w2': _L0_ffn_in['w2'], 'L0_ffn_sh_gu_w': _L0_ffn_in['sh_gu_w'], 'L0_ffn_sh_down_w': _L0_ffn_in['sh_down_w'], 'L1_attn_Wq': _L1_attn_in['Wq'], 'L1_attn_Wk': _L1_attn_in['Wk'], 'L1_attn_Wv': _L1_attn_in['Wv'], 'L1_attn_Wo': _L1_attn_in['Wo'], 'L1_xattn_Wq': _L1_xattn_in['Wq'], 'L1_xattn_bq': _L1_xattn_in['bq'], 'L1_xattn_Wk': _L1_xattn_in['Wk'], 'L1_xattn_bk': _L1_xattn_in['bk'], 'L1_xattn_Wv': _L1_xattn_in['Wv'], 'L1_xattn_bv': _L1_xattn_in['bv'], 'L1_xattn_Wo': _L1_xattn_in['Wo'], 'L1_xattn_bo': _L1_xattn_in['bo'], 'L1_xattn_ln_gamma': _L1_xattn_in['ln_gamma'], 'L1_xattn_ln_beta': _L1_xattn_in['ln_beta'], 'L1_xattn_residual_scale': _L1_xattn_in['residual_scale'], 'L1_ffn_w_gate': _L1_ffn_in['w_gate'], 'L1_ffn_w1': _L1_ffn_in['w1'], 'L1_ffn_w2': _L1_ffn_in['w2']}

def reference(x, ctx_2048, mask_BxS2_ik0, L0_attn_norm_w, L0_attn_wq, L0_attn_bq, L0_attn_wk, L0_attn_bk, L0_attn_wv, L0_attn_bv, L0_attn_wo, L0_attn_bo, L0_ffn_positions, L0_ffn_ln1_w, L0_ffn_ln2_w, L0_ffn_q_w, L0_ffn_kv_w, L0_ffn_o_w, L0_ffn_gate_w, L0_ffn_w1, L0_ffn_w2, L0_ffn_sh_gu_w, L0_ffn_sh_down_w, L1_attn_Wq, L1_attn_Wk, L1_attn_Wv, L1_attn_Wo, L1_xattn_Wq, L1_xattn_bq, L1_xattn_Wk, L1_xattn_bk, L1_xattn_Wv, L1_xattn_bv, L1_xattn_Wo, L1_xattn_bo, L1_xattn_ln_gamma, L1_xattn_ln_beta, L1_xattn_residual_scale, L1_ffn_w_gate, L1_ffn_w1, L1_ffn_w2):
    import jax
    import jax.numpy as jnp

    def _L0_attn_ref(x, norm_w, wq, bq, wk, bk, wv, bv, wo, bo):
        import jax, jax.numpy as jnp
        import numpy as np
        D_MODEL = 256
        N_HEADS = 16
        HEAD_DIM = D_MODEL // N_HEADS
        EPS = 1e-06

        def _rmsnorm(x, w):
            return x * jax.lax.rsqrt(jnp.mean(x * x, axis=-1, keepdims=True) + EPS) * w
        B, T, D = x.shape
        H, Hd = (N_HEADS, HEAD_DIM)
        scale = Hd ** (-0.5)
        xn = _rmsnorm(x, norm_w)
        q = (xn @ wq.T + bq).reshape(B, T, H, Hd).transpose(0, 2, 1, 3)
        k = (xn @ wk.T + bk).reshape(B, T, H, Hd).transpose(0, 2, 1, 3)
        v = (xn @ wv.T + bv).reshape(B, T, H, Hd).transpose(0, 2, 1, 3)
        scores = jnp.einsum('bhqd,bhkd->bhqk', q, k) * scale
        causal = jnp.tril(jnp.ones((T, T), dtype=bool))
        scores = jnp.where(causal, scores, -jnp.inf)
        attn = jax.nn.softmax(scores, axis=-1)
        out = jnp.einsum('bhqk,bhkd->bhqd', attn, v)
        out = out.transpose(0, 2, 1, 3).reshape(B, T, D)
        out = out @ wo.T + bo
        return out

    def _L0_xattn_ref(q, k, v):
        import math
        import jax, jax.numpy as jnp
        import numpy as np
        HEADS = 16
        MASKED_BIAS = -10000.0

        def _mha(q, k, v):
            B, Sq, D = q.shape
            Sk = k.shape[-2]
            hd = D // HEADS
            qh = q.reshape(B, Sq, HEADS, hd).transpose(0, 2, 1, 3)
            kh = k.reshape(B, Sk, HEADS, hd).transpose(0, 2, 1, 3)
            vh = v.reshape(B, Sk, HEADS, hd).transpose(0, 2, 1, 3)
            scores = jnp.einsum('bhqd,bhkd->bhqk', qh, kh) / math.sqrt(hd)
            qi = jnp.arange(Sq)[:, None] + (Sk - Sq)
            ki = jnp.arange(Sk)[None, :]
            causal = ki <= qi
            scores = jnp.where(causal[None, None], scores, jnp.asarray(MASKED_BIAS, scores.dtype))
            attn = jax.nn.softmax(scores, axis=-1)
            out = jnp.einsum('bhqk,bhkd->bhqd', attn, vh)
            return out.transpose(0, 2, 1, 3).reshape(B, Sq, D)
        return _mha(q, k, v)

    def _L0_ffn_ref(hidden_states, positions, ln1_w, ln2_w, q_w, kv_w, o_w, gate_w, w1, w2, sh_gu_w, sh_down_w):
        import jax, jax.numpy as jnp
        import numpy as np
        H = 256
        NH = 16
        NOPE = 128
        ROPE = 64
        VD = 128
        QHD = NOPE + ROPE
        E = 16
        I = 176
        TOPK = 4
        NSH = 2
        SHI = I * NSH
        EPS = 1e-06
        B, S = (2, 128)

        def rmsnorm(x, w):
            return x * jax.lax.rsqrt(jnp.mean(x * x, axis=-1, keepdims=True) + EPS) * w
        b, s, h = hidden_states.shape
        x = rmsnorm(hidden_states, ln1_w)
        q = jnp.einsum('bsh,dh->bsd', x, q_w).reshape(b, s, NH, QHD)[..., :NOPE]
        kv = jnp.einsum('bsh,dh->bsd', x, kv_w)
        k = kv[..., :NH * NOPE].reshape(b, s, NH, NOPE)
        v = kv[..., NH * NOPE:NH * (NOPE + VD)].reshape(b, s, NH, VD)
        scale = QHD ** (-0.5)
        scores = jnp.einsum('bqnd,bknd->bnqk', q, k) * scale
        causal = jnp.tril(jnp.ones((s, s), bool))
        scores = jnp.where(causal, scores, -1000000000.0)
        p = jax.nn.softmax(scores, axis=-1)
        attn = jnp.einsum('bnqk,bknd->bqnd', p, v).reshape(b, s, NH * VD)
        attn_out = jnp.einsum('bsd,hd->bsh', attn, o_w)
        hid = hidden_states + attn_out
        x2 = rmsnorm(hid, ln2_w).reshape(-1, h)
        logits = x2 @ gate_w.T
        probs = jax.nn.softmax(logits, axis=-1)
        top_w, top_i = jax.lax.top_k(probs, TOPK)
        top_w = top_w / jnp.sum(top_w, axis=-1, keepdims=True)
        wfull = jnp.sum(jax.nn.one_hot(top_i, E, dtype=x2.dtype) * top_w[..., None], axis=1)
        gu = jnp.einsum('th,eih->tei', x2, w1)
        g, u = (gu[..., :I], gu[..., I:])
        act = jax.nn.silu(g) * u
        down = jnp.einsum('tei,ehi->teh', act, w2)
        routed = jnp.einsum('te,teh->th', wfull, down)
        sgu = x2 @ sh_gu_w.T
        sg, su = (sgu[..., :SHI], sgu[..., SHI:])
        shared = jax.nn.silu(sg) * su @ sh_down_w.T
        return hid + (routed + shared).reshape(b, s, h)

    def _L1_attn_ref(x, Wq, Wk, Wv, Wo):
        import jax, jax.numpy as jnp
        import numpy as np
        NUM_HEADS = 16
        ROPE_BASE = 10000.0

        def _rope_tables(seq_len, head_dim, scaling_factor=1.0):
            inv_freq = 1.0 / ROPE_BASE ** (jnp.arange(0, head_dim, 2, dtype=jnp.float32) / head_dim)
            t = jnp.arange(seq_len, dtype=jnp.float32) * scaling_factor
            freqs = jnp.einsum('i,j->ij', t, inv_freq)
            c = jnp.sin(freqs)
            s = jnp.cos(freqs)
            return (c, s)

        def _apply_rope(x, c, s):
            x1, x2 = jnp.split(x, 2, axis=-1)
            c = c[None, None]
            s = s[None, None]
            return jnp.concatenate([x1 * c - x2 * s, x1 * s + x2 * c], axis=-1)
        B, S, H = x.shape
        nh = NUM_HEADS
        hd = H // nh
        scale = hd ** (-0.5)

        def proj(W):
            y = jnp.einsum('bsi,oi->bso', x, W)
            return y.reshape(B, S, nh, hd).transpose(0, 2, 1, 3)
        Q = proj(Wq)
        K = proj(Wk)
        V = proj(Wv)
        c, s = _rope_tables(S, hd)
        Q = _apply_rope(Q, c, s)
        K = _apply_rope(K, c, s)
        scores = jnp.einsum('bhqd,bhkd->bhqk', Q, K) * scale
        mask = jnp.tril(jnp.ones((S, S), dtype=bool))
        scores = jnp.where(mask[None, None], scores, -jnp.inf)
        attn = jax.nn.softmax(scores, axis=-1)
        out = jnp.einsum('bhqk,bhkd->bhqd', attn, V)
        out = out.transpose(0, 2, 1, 3).reshape(B, S, H)
        return jnp.einsum('bsi,oi->bso', out, Wo)

    def _L1_xattn_ref(hidden_states, audio_tokens, attention_mask, Wq, bq, Wk, bk, Wv, bv, Wo, bo, ln_gamma, ln_beta, residual_scale):
        import jax, jax.numpy as jnp
        import numpy as np
        import math
        H = 256
        NH = 16
        HD = H // NH
        EPS_LN = 1e-05
        RES_SCALE_MAX = 0.3

        def _nan_clean(x, lim=10000.0):
            return jnp.nan_to_num(x, nan=0.0, posinf=lim, neginf=-lim)
        B, S, _ = hidden_states.shape
        T = audio_tokens.shape[1]
        hs = _nan_clean(hidden_states).astype(jnp.float32)
        at = _nan_clean(audio_tokens).astype(jnp.float32)

        def proj(x, W, b, L):
            y = x @ W.T + b
            return y.reshape(B, L, NH, HD).transpose(0, 2, 1, 3)
        q = _nan_clean(proj(hs, Wq, bq, S))
        k = _nan_clean(proj(at, Wk, bk, T))
        v = _nan_clean(proj(at, Wv, bv, T))
        scale = max(math.sqrt(HD), 1e-08)
        scores = jnp.einsum('bhsd,bhtd->bhst', q, k) / scale
        scores = jnp.clip(scores, -50.0, 50.0)
        scores = jnp.nan_to_num(scores, nan=0.0, posinf=50.0, neginf=-50.0)
        attend = (attention_mask.astype(jnp.float32) > 0.5)[:, None, None, :]
        scores = jnp.where(attend, scores, -10000.0)
        scores = jnp.clip(scores, -50.0, 50.0)
        probs = jax.nn.softmax(scores, axis=-1)
        probs = jnp.nan_to_num(probs, nan=0.0, posinf=1.0, neginf=0.0)
        probs = probs / (probs.sum(axis=-1, keepdims=True) + 1e-08)
        ctx = jnp.einsum('bhst,bhtd->bhsd', probs, v)
        ctx = ctx.transpose(0, 2, 1, 3).reshape(B, S, H)
        delta = _nan_clean(ctx @ Wo.T + bo)
        rs = jnp.clip(residual_scale, 0.0, RES_SCALE_MAX)
        delta = rs * delta
        mu = delta.mean(axis=-1, keepdims=True)
        var = jnp.mean((delta - mu) ** 2, axis=-1, keepdims=True)
        delta = (delta - mu) / jnp.sqrt(var + EPS_LN) * ln_gamma + ln_beta
        return delta

    def _L1_ffn_ref(hidden_states, w_gate, w1, w2):
        import jax, jax.numpy as jnp
        import numpy as np
        CAPACITY_FACTOR = 1.0

        def _top1_gate(x, w_gate):
            S, E = (x.shape[0], w_gate.shape[1])
            capacity = int(CAPACITY_FACTOR * S / E)
            logits = x @ w_gate
            gates = jax.nn.softmax(logits, axis=-1)
            idx1 = jnp.argmax(gates, axis=-1)
            mask1 = jax.nn.one_hot(idx1, E, dtype=gates.dtype)
            locations1 = jnp.cumsum(mask1, axis=0) - mask1
            mask1 = mask1 * (locations1 < capacity)
            locations1_s = jnp.sum(locations1 * mask1, axis=1).astype(jnp.int32)
            gates_masked = gates * mask1
            loc_oh = jax.nn.one_hot(locations1_s, capacity, dtype=gates.dtype) * jnp.sum(mask1, axis=1, keepdims=True)
            combine_weights = jnp.einsum('se,sc->sec', gates_masked, loc_oh)
            dispatch_mask = (combine_weights > 0).astype(gates.dtype)
            return (combine_weights, dispatch_mask)
        B, T, D = hidden_states.shape
        x = hidden_states.reshape(-1, D)
        combine_weights, dispatch_mask = _top1_gate(x, w_gate)
        dispatched = jnp.einsum('sec,sm->ecm', dispatch_mask, x)
        h = jax.nn.gelu(jnp.einsum('ecd,edf->ecf', dispatched, w1))
        expert_out = jnp.einsum('ecf,efd->ecd', h, w2)
        combined = jnp.einsum('sec,ecm->sm', combine_weights, expert_out)
        return combined.reshape(B, T, D)
    x = _layernorm(x + _L0_attn_ref(x, L0_attn_norm_w, L0_attn_wq, L0_attn_bq, L0_attn_wk, L0_attn_bk, L0_attn_wv, L0_attn_bv, L0_attn_wo, L0_attn_bo), axis=-1)
    x = _layernorm(x + _L0_xattn_ref(x, ctx_2048, ctx_2048), axis=-1)
    x = _layernorm(x + _L0_ffn_ref(x, L0_ffn_positions, L0_ffn_ln1_w, L0_ffn_ln2_w, L0_ffn_q_w, L0_ffn_kv_w, L0_ffn_o_w, L0_ffn_gate_w, L0_ffn_w1, L0_ffn_w2, L0_ffn_sh_gu_w, L0_ffn_sh_down_w), axis=-1)
    x = _layernorm(x + _L1_attn_ref(x, L1_attn_Wq, L1_attn_Wk, L1_attn_Wv, L1_attn_Wo), axis=-1)
    x = _layernorm(x + _L1_xattn_ref(x, ctx_2048, mask_BxS2_ik0, L1_xattn_Wq, L1_xattn_bq, L1_xattn_Wk, L1_xattn_bk, L1_xattn_Wv, L1_xattn_bv, L1_xattn_Wo, L1_xattn_bo, L1_xattn_ln_gamma, L1_xattn_ln_beta, L1_xattn_residual_scale), axis=-1)
    x = _layernorm(x + _L1_ffn_ref(x, L1_ffn_w_gate, L1_ffn_w1, L1_ffn_w2), axis=-1)
    return x

_drawn_inputs = setup_inputs


def setup_inputs(seed=0):
    import zlib

    import numpy as np

    out = dict(_drawn_inputs(seed))
    spreads = {'L0_attn_norm_w': (1.0, 0.2),
     'L0_attn_bq': (0.0, 0.336),
     'L0_attn_bk': (0.0, 0.8),
     'L0_attn_bv': (0.0, 0.1),
     'L0_attn_bo': (0.0, 0.1),
     'L0_ffn_ln1_w': (1.0, 0.2),
     'L0_ffn_ln2_w': (1.0, 0.2),
     'L1_xattn_bq': (0.0, 0.273),
     'L1_xattn_bk': (0.0, 0.8),
     'L1_xattn_bv': (0.0, 0.1),
     'L1_xattn_bo': (0.0, 0.1),
     'L1_xattn_ln_gamma': (1.0, 0.2),
     'L1_xattn_ln_beta': (0.0, 0.1)}
    factors = {'L1_ffn_w_gate': 3.204, 'L1_ffn_w1': 3.061, 'L1_ffn_w2': 3.008}
    for name, (base, spread) in spreads.items():
        noise = np.random.default_rng([zlib.crc32(name.encode()), seed]).standard_normal(out[name].shape)
        drawn = base * np.exp(spread * noise) if base else spread * noise
        out[name] = jnp.asarray(drawn.astype(out[name].dtype))
    for name, factor in factors.items():
        out[name] = (out[name] * factor).astype(out[name].dtype)
    return out
```

```python
from contextlib import ExitStack

import concourse.bass as bass
from concourse import mybir

F32 = mybir.dt.float32
BF16 = mybir.dt.bfloat16
I32 = mybir.dt.int32
ALU = mybir.AluOpType
ACT = mybir.ActivationFunctionType
AX_X = mybir.AxisListType.X

P = 128
B, T, D = 16, 100, 256
DC = D // P
H, HD = 16, 16
HH = 8
GB = 4
G = B // GB
GT = GB * T
N = B * T
S2 = 1444
KB, NKB = P, 12
S2P = KB * NKB
LASTKB = S2 - KB * (NKB - 1)
CUTS = (0, 482, 964, S2)
MASK0 = S2P - 2 * KB
PARTS = 3
STK = 6 * HD
E0, TOPK, I0 = 16, 4, 176
EC = E0 * I0 // P
SHI = 2 * I0
E1, F1 = 8, 1024
CAP = N // E1
NEG = -1.0e30


class Chain:

    def __init__(self, eng, sem):
        self.eng, self.sem, self.base, self.n = eng, sem, 0, 0

    def __call__(self, ins):
        self.n += 1
        ins.then_inc(self.sem, 1)
        self.eng.wait_ge(self.sem, self.base + self.n)

    def loop(self, i, per):
        self.start = self.n if isinstance(self.base, int) else self.start
        self.base, self.n, self.per = self.start + i * per, 0, per

    def end(self, steps):
        assert self.n == self.per, (self.n, self.per)
        self.base, self.n = 0, self.start + steps * self.per


def fixed(eng, value, name):
    reg = eng.alloc_register(name)
    eng.reg_mov(reg, value)
    return eng.snap(reg)


class Core:
    def __init__(self, nc, ctx):
        self.nc, self.ctx, self.stage = nc, ctx, ""
        self.sems = []

    def sem(self, name):
        self.sems.append(self.nc.alloc_semaphore(name=f"{self.stage}_{name}"))
        return self.sems[-1]

    def clear_sems(self):
        with self.nc.Block() as block:
            @block.sync
            def _(sp):
                for s in self.sems:
                    sp.sem_clear(s)
        for s in self.sems:
            self.nc.release_semaphore(s)
        self.sems = []

    def psum(self, ctx, name, shape, dt=F32):
        return ctx.enter_context(self.nc.psum_tensor(f"{self.stage}_{name}", shape, dt))

    def sb(self, ctx, name, shape, dt=F32):
        return ctx.enter_context(self.nc.sbuf_tensor(f"{self.stage}_{name}", shape, dt))


def statistics(dve, link, src, st, mv):
    for b in range(B):
        last = dve.bn_stats(st[:, b, :], src[:, b, :])
    link(last)
    for b in range(B):
        last = dve.bn_aggr(mv[:, b, :], st[:, b, :])
    link(last)


def layernorm(c, name, X, out=None, gamma=None, beta=None, add=None, eps=1e-5, scale=None):
    c.stage = name
    nc = c.nc
    out = X if out is None else out
    with ExitStack() as s:
        st, mv, rstd = (c.sb(s, n, [T, B, k]) for n, k in (("st", 6), ("mv", 2), ("rstd", 1)))
        chain, have_var, have_rstd = c.sem("chain"), c.sem("have_var"), c.sem("have_rstd")
        with nc.Block() as block:
            @block.vector
            def _(dve):
                link = Chain(dve, chain)
                if scale is not None:
                    link(dve.tensor_scalar(X[:, :, :], X[:, :, :], scale, None, ALU.mult))
                statistics(dve, link, X, st, mv)
                dve.tensor_scalar(rstd[:, :, :], mv[:, :, 1:2], eps, None, ALU.add).then_inc(have_var, 1)
                dve.wait_ge(have_rstd, 1)
                link(dve.reciprocal(rstd[:, :, :], rstd[:, :, :]))
                for b in range(B):
                    last = dve.tensor_scalar(out[:, b, :], X[:, b, :], mv[:, b, 0:1], rstd[:, b, :],
                                             ALU.subtract, ALU.mult)
                link(last)
                if gamma is not None:
                    link(dve.tensor_tensor(out[:, :, :], out[:, :, :], over_seqs(gamma), ALU.mult))
                    link(dve.tensor_tensor(out[:, :, :], out[:, :, :], over_seqs(beta), ALU.add))
                if add is not None:
                    link(dve.tensor_tensor(out[:, :, :], out[:, :, :], add[:, :, :], ALU.add))

            @block.scalar
            def _(act):
                act.wait_ge(have_var, 1)
                act.activation(rstd[:, :, :], rstd[:, :, :], ACT.Sqrt).then_inc(have_rstd, 1)


def over_seqs(row):
    return row.unsqueeze(1).to_broadcast([T, B, D])


def features_first(c, name, X, XT, ident, rms=False, weight=None, nseq=B):
    c.stage = name
    nc = c.nc
    with ExitStack() as s:
        st, mv, ms = (c.sb(s, n, [T, B, k]) for n, k in (("st", 6), ("mv", 2), ("ms", 1)))
        xn = c.sb(s, "xn", [T, B, D]) if rms else X
        banks = c.psum(s, "banks", [P, 8, 512])
        chain, have_ms, have_rms, have_xn = (c.sem(n) for n in ("chain", "have_ms", "have_rms", "have_xn"))
        turned = c.sem("turned")
        with nc.Block() as block:
            if rms:
                @block.vector
                def _(dve):
                    link = Chain(dve, chain)
                    statistics(dve, link, X, st, mv)
                    link(dve.tensor_tensor(ms[:, :, :], mv[:, :, 0:1], mv[:, :, 0:1], ALU.mult))
                    link(dve.tensor_tensor(ms[:, :, :], ms[:, :, :], mv[:, :, 1:2], ALU.add))
                    dve.tensor_scalar(ms[:, :, :], ms[:, :, :], 1e-6, None, ALU.add).then_inc(have_ms, 1)
                    dve.wait_ge(have_rms, 1)
                    link(dve.reciprocal(ms[:, :, :], ms[:, :, :]))
                    for b in range(B):
                        dve.tensor_scalar(xn[:, b, :], X[:, b, :], ms[:, b, :], None, ALU.mult).then_inc(have_xn, 1)

            @block.tensor
            def _(pe):
                for g in range(G):
                    if rms:
                        pe.wait_ge(have_xn, GB * (g + 1))
                    for ch in range(DC):
                        for j in range(GB):
                            last = pe.transpose(banks[:, g * DC + ch, j * T:(j + 1) * T],
                                                xn[:, g * GB + j, ch * P:(ch + 1) * P], ident[0:T, 0:T])
                        last.then_inc(turned, 1)

            @block.scalar
            def _(act):
                if rms:
                    act.wait_ge(have_ms, 1)
                    act.activation(ms[:, :, :], ms[:, :, :], ACT.Sqrt).then_inc(have_rms, 1)
                for g in range(G):
                    for ch in range(DC):
                        act.wait_ge(turned, g * DC + ch + 1)
                        act.activation(XT[:, ch, g * GT:(g + 1) * GT], banks[:, g * DC + ch, 0:GT], ACT.Copy,
                                       scale=1.0 if weight is None else weight[:, ch:ch + 1])


def load(c, name, pairs):
    c.stage = name
    landed = c.sem("landed")
    with c.nc.Block() as block:
        @block.sync
        def _(sp):
            for dst, src in pairs[0::2]:
                sp.dma_start(dst, src).then_inc(landed, 16)
            sp.wait_ge(landed, 16 * len(pairs))

        @block.scalar
        def _(act):
            for dst, src in pairs[1::2]:
                act.dma_start(dst, src).then_inc(landed, 16)


def narrow_attention(c, name, X, XT, K, w, scale, rope=None, bias=None):
    c.stage = name
    nc = c.nc
    with ExitStack() as s:
        xg = c.sb(s, "xg", [P, DC, GT])
        qT, kT = c.sb(s, "qT", [P, DC, GT]), c.sb(s, "kT", [P, DC, GT])
        rot = c.sb(s, "rot", [P, 4, GT]) if rope else None
        kD = c.sb(s, "kD", [P, 2, DC, HH, T])
        V = c.sb(s, "V", [T, GB, H, 32])
        Pm = c.sb(s, "Pm", [T, 2, H, T])
        mx, sm = c.sb(s, "mx", [T, H, 1]), c.sb(s, "sm", [T, H, 1])
        PT = c.sb(s, "PT", [T, H, T])
        OT = c.sb(s, "OT", [P, 4, T])
        SB, TB = c.psum(s, "SB", [P, 4, 512]), c.psum(s, "TB", [P, 4, 512])
        (chain, xg_ready, zeroed, proj_ready, qk_done, v_ready, v_taken, spread, scores_ready,
         shifted, exp_done, sums, scaled, turned, turned_sb, mixed, mixed_sb, out_ready, out_added) = (
            c.sem(n) for n in (
                "chain", "xg_ready", "zeroed", "proj_ready", "qk_done", "v_ready", "v_taken",
                "spread", "scores_ready", "shifted", "exp_done", "sums", "scaled", "turned", "turned_sb",
                "mixed", "mixed_sb", "out_ready", "out_added"))
        Sv = SB[0:T, :, 0:GT].rearrange("q j (i k) -> q j i k", k=T)
        NPROJ = 8 if rope else 4
        QK = 1 if rope else 4

        with nc.Block() as block:
            @block.gpsimd
            def _(pool):
                pool.memset(V[:, :, :, :], 0.0).then_inc(zeroed, 1)

                def spread_keys(g, u):
                    if u == 0:
                        pool.wait_ge(qk_done, QK * (g + 1))
                    if u >= 2:
                        pool.wait_ge(scores_ready, g * GB + u - 1)
                    for m in range(DC):
                        pool.tensor_tensor(kD[:, u % 2, m, :, :],
                                           kT[:, m, u * T:(u + 1) * T].unsqueeze(1).to_broadcast([P, HH, T]),
                                           K["headrows"][:, :].unsqueeze(2).to_broadcast([P, HH, T]),
                                           ALU.mult).then_inc(spread, 1)

                with pool.Fori(0, G) as g:
                    spread_keys(g, 0)
                    for u in range(GB):
                        if u + 1 < GB:
                            spread_keys(g, u + 1)
                        pool.wait_ge(sums, g * GB + u + 1)
                        pool.tensor_tensor(Pm[:, u % 2, :, :], Pm[:, u % 2, :, :],
                                           sm[:, :, :].to_broadcast([T, H, T]), ALU.mult).then_inc(scaled, 1)

            @block.tensor
            def _(pe):
                def project(g):
                    pe.wait_ge(shifted, g * GB)
                    if rope:
                        pe.wait_ge(out_added, g * GB)
                    n = 0
                    for banks, mats in ((SB, ("wq", "wk")), (TB, ("wqs", "wks")))[:2 if rope else 1]:
                        for j in range(4):
                            for ch in range(DC):
                                m = j % 2
                                last = pe.matmul(banks[:, j, 0:GT], w[mats[j // 2]][:, ch, m * P:(m + 1) * P],
                                                 xg[:, ch, :], start=(ch == 0), stop=(ch == DC - 1))
                            last.then_inc(proj_ready, 1)

                def values(g):
                    pe.wait_ge(out_added, g * GB)
                    if rope:
                        pe.wait_ge(qk_done, QK * (g + 1))
                    for b in range(GB):
                        for ch in range(DC):
                            last = pe.matmul(TB[0:T, b, 0:D], xg[:, ch, b * T:(b + 1) * T], w["wv"][:, ch, :],
                                             start=(ch == 0), stop=(ch == DC - 1 and not bias))
                        if bias:
                            last = pe.matmul(TB[0:T, b, 0:D], K["ones"][0:1, 0:T], w["bv"][:, :],
                                             start=False, stop=True)
                        last.then_inc(v_ready, 1)

                def scores(g, u):
                    pe.wait_ge(shifted, g * GB + u)
                    pe.wait_ge(qk_done, QK * (g + 1))
                    pe.wait_ge(spread, 2 * (g * GB + u + 1))
                    for j in range(4):
                        pe.matmul(SB[0:T, j, 0:GT], K["identb"][0:T, 0:T], K["causal"][:, :],
                                  start=True, stop=False, skip_group_check=True)
                        h = 4 * (j % 2)
                        last = pe.matmul(SB[0:T, j, 0:GT], qT[:, j // 2, u * T:(u + 1) * T],
                                         kD[:, u % 2, j // 2, h:h + 4, :].rearrange("p h k -> p (h k)"),
                                         start=False, stop=True, skip_group_check=True)
                    last.then_inc(scores_ready, 1)

                def mix(g, u):
                    U = g * GB + u
                    pe.wait_ge(scaled, U + 1)
                    pe.wait_ge(out_added, U)
                    pe.wait_ge(v_taken, 4 * (g + 1))
                    for j in range(4):
                        for i in range(4):
                            last = pe.transpose(TB[0:T, j, i * T:(i + 1) * T], Pm[:, u % 2, 4 * j + i, :],
                                                K["ident"][0:T, 0:T])
                        last.then_inc(turned, 1)
                    pe.wait_ge(turned_sb, 2 * (U + 1))
                    for q in range(4):
                        for j in range(4):
                            last = pe.matmul(TB[32 * j:32 * j + 32, 0, q * T:(q + 1) * T], V[:, u, 4 * q + j, :],
                                             PT[:, 4 * q + j, :], start=(q == 0), stop=True,
                                             skip_group_check=True)
                    last.then_inc(mixed, 1)
                    pe.wait_ge(mixed_sb, U + 1)
                    for q in range(4):
                        last = pe.matmul(TB[0:T, 1, 0:D], OT[:, q, :], w["wo"][:, q, :],
                                         start=(q == 0), stop=(q == 3 and not bias))
                    if bias:
                        last = pe.matmul(TB[0:T, 1, 0:D], K["ones"][0:1, 0:T], w["bo"][:, :],
                                         start=False, stop=True)
                    last.then_inc(out_ready, 1)

                with pe.Fori(0, G) as g:
                    pe.wait_ge(xg_ready, g + 1)
                    project(g)
                    values(g)
                    scores(g, 0)
                    for u in range(GB):
                        if u + 1 < GB:
                            scores(g, u + 1)
                        mix(g, u)

            @block.scalar
            def _(act):
                def exponentials(g, u):
                    act.wait_ge(shifted, g * GB + u + 1)
                    act.activation(Pm[:, u % 2, :, :], Pm[:, u % 2, :, :], ACT.Exp,
                                   scale=scale).then_inc(exp_done, 1)

                act.wait_ge(zeroed, 1)
                with act.Fori(0, G) as g:
                    act.wait_ge(out_ready, g * GB)
                    act.activation(xg[:, :, :], XT[:, :, bass.ds(g * GT, GT)], ACT.Copy).then_inc(xg_ready, 1)
                    if not rope:
                        act.wait_ge(scores_ready, g * GB)
                        act.wait_ge(spread, 2 * g * GB)
                        for j in range(4):
                            act.wait_ge(proj_ready, 4 * g + j + 1)
                            act.activation((qT if j < 2 else kT)[:, j % 2, :], SB[:, j, 0:GT], ACT.Identity,
                                           bias=w["bq" if j < 2 else "bk"][:, j % 2:j % 2 + 1]).then_inc(qk_done, 1)
                    act.wait_ge(mixed, g * GB)
                    for b in range(GB):
                        act.wait_ge(v_ready, 4 * g + b + 1)
                        act.activation(V[:, b, :, 0:HD], TB[0:T, b, 0:D].rearrange("t (h d) -> t h d", d=HD),
                                       ACT.Copy).then_inc(v_taken, 1)
                    exponentials(g, 0)
                    for u in range(GB):
                        U = g * GB + u
                        if u + 1 < GB:
                            exponentials(g, u + 1)
                        act.wait_ge(turned, 4 * U + 2)
                        act.wait_ge(mixed, U)
                        act.activation(PT[:, 0:8, :].rearrange("k (j i) q -> k j (i q)", j=2),
                                       TB[0:T, 0:2, 0:GT], ACT.Copy).then_inc(turned_sb, 1)
                        act.wait_ge(mixed, U + 1)
                        act.wait_ge(out_ready, U)
                        act.activation(OT[:, :, :].rearrange("p q t -> p (q t)"), TB[:, 0, 0:GT],
                                       ACT.Copy).then_inc(mixed_sb, 1)

            @block.vector
            def _(dve):
                link = Chain(dve, chain)

                def rotate(g):
                    dve.wait_ge(proj_ready, (g + 1) * NPROJ)
                    dve.wait_ge(scores_ready, g * GB)
                    dve.wait_ge(spread, 2 * g * GB)
                    tab = [rope[:, t, :].unsqueeze(1).to_broadcast([P, GB, T]) for t in range(2)]
                    cut = lambda a: a.rearrange("p (b t) -> p b t", t=T)
                    for j in range(4):
                        dst = (qT if j < 2 else kT)[:, j % 2, :]
                        dve.tensor_tensor(cut(dst), cut(SB[:, j, 0:GT]), tab[0], ALU.mult)
                        last = dve.tensor_tensor(cut(rot[:, j, :]), cut(TB[:, j, 0:GT]), tab[1], ALU.mult)
                    link(last)
                    dve.tensor_tensor(qT[:, :, :], qT[:, :, :], rot[:, 0:2, :], ALU.add)
                    dve.tensor_tensor(kT[:, :, :], kT[:, :, :], rot[:, 2:4, :], ALU.add).then_inc(qk_done, 1)

                def shift(g, u):
                    dve.wait_ge(scores_ready, g * GB + u + 1)
                    link(dve.tensor_reduce(mx[:, :, :].rearrange("q (j i) o -> q j (i o)", j=4), Sv, AX_X, ALU.max))
                    dve.tensor_tensor(Pm[:, u % 2, :, :].rearrange("q (j i) k -> q j i k", j=4), Sv,
                                      mx[:, :, :].rearrange("q (j i) o -> q j i o", j=4).to_broadcast([T, 4, 4, T]),
                                      ALU.subtract).then_inc(shifted, 1)

                with dve.Fori(0, G) as g:
                    link.loop(g, (1 if rope else 0) + 2 * GB)
                    if rope:
                        rotate(g)
                    shift(g, 0)
                    for u in range(GB):
                        U = g * GB + u
                        dve.wait_ge(exp_done, U + 1)
                        dve.wait_ge(scaled, U)
                        link(dve.tensor_reduce(sm[:, :, :].rearrange("q h o -> q (h o)"), Pm[:, u % 2, :, :],
                                               AX_X, ALU.add))
                        dve.reciprocal(sm[:, :, :], sm[:, :, :]).then_inc(sums, 1)
                        if u + 1 < GB:
                            shift(g, u + 1)
                        dve.wait_ge(turned, 4 * U + 4)
                        dve.wait_ge(mixed, U)
                        dve.tensor_copy(PT[:, 8:16, :].rearrange("k (j i) q -> k j (i q)", j=2),
                                        TB[0:T, 2:4, 0:GT]).then_inc(turned_sb, 1)
                        dve.wait_ge(out_ready, U + 1)
                        xb = X[:, bass.ds(g * GB + u, 1), :]
                        dve.tensor_tensor(xb, xb, TB[0:T, 1:2, 0:D], ALU.add).then_inc(out_added, 1)
                link.end(G)


def latent_attention(c, name, A, XT, K, w, scale):
    c.stage = name
    nc = c.nc
    with ExitStack() as s:
        xg = c.sb(s, "xg", [P, DC, GT])
        qT, kT = c.sb(s, "qT", [P, 4, GT]), c.sb(s, "kT", [P, 4, GT])
        V = c.sb(s, "V", [T, GB, 4, P])
        Pm = c.sb(s, "Pm", [T, 16, T])
        mx, sm = c.sb(s, "mx", [T, 16, 1]), c.sb(s, "sm", [T, 16, 1])
        PT = c.sb(s, "PT", [T, 16, T])
        OT = c.sb(s, "OT", [P, 4, GT])
        SB, TB = c.psum(s, "SB", [P, 4, 512]), c.psum(s, "TB", [P, 4, 512])
        (chain, xg_ready, proj_ready, qk_done, v_ready, v_taken, scores_ready, shifted, exp_done,
         sums, scaled, turned, turned_sb, mixed, mixed_sb, out_ready, out_added) = (
            c.sem(n) for n in (
                "chain", "xg_ready", "proj_ready", "qk_done", "v_ready", "v_taken",
                "scores_ready", "shifted", "exp_done", "sums", "scaled", "turned", "turned_sb", "mixed",
                "mixed_sb", "out_ready", "out_added"))
        Sv = SB[0:T, :, 0:GT].rearrange("q j (i k) -> q j i k", k=T)
        HQ = 4

        with nc.Block() as block:
            @block.gpsimd
            def _(pool):
                with pool.Fori(0, G) as g:
                    for u in range(HQ):
                        pool.wait_ge(sums, g * HQ + u + 1)
                        pool.tensor_tensor(Pm[:, :, :], Pm[:, :, :], sm[:, :, :].to_broadcast([T, 16, T]),
                                           ALU.mult).then_inc(scaled, 1)

            @block.tensor
            def _(pe):
                def project(g, u):
                    U = g * HQ + u
                    pe.wait_ge(shifted, U)
                    for n in range(8):
                        if n >= 4:
                            pe.wait_ge(qk_done, 8 * U + n - 3)
                        wm = w["wq" if n < 4 else "wk"]
                        h = 4 * u + n % 4
                        for ch in range(DC):
                            last = pe.matmul(SB[:, n % 4, 0:GT], wm[:, ch, h * P:(h + 1) * P], xg[:, ch, :],
                                             start=(ch == 0), stop=(ch == DC - 1))
                        last.then_inc(proj_ready, 1)

                def values(g, u):
                    pe.wait_ge(out_added, g * HQ + u)
                    for b in range(GB):
                        for ch in range(DC):
                            last = pe.matmul(TB[0:T, b, :], xg[:, ch, b * T:(b + 1) * T],
                                             w["wv"][:, ch, 4 * u * P:4 * (u + 1) * P],
                                             start=(ch == 0), stop=(ch == DC - 1))
                        last.then_inc(v_ready, 1)

                def scores(g, u):
                    U = g * HQ + u
                    pe.wait_ge(qk_done, 8 * (U + 1))
                    for j in range(4):
                        pe.matmul(SB[0:T, j, 0:GT], K["identb"][0:T, 0:T], K["causal"][:, :],
                                  start=True, stop=False, skip_group_check=True)
                        for b in range(GB):
                            t = slice(b * T, (b + 1) * T)
                            last = pe.matmul(SB[0:T, j, t], qT[:, j, t], kT[:, j, t], start=False,
                                             stop=(b == GB - 1), skip_group_check=True)
                    last.then_inc(scores_ready, 1)

                def mix(g, u):
                    U = g * HQ + u
                    pe.wait_ge(scaled, U + 1)
                    pe.wait_ge(v_taken, 4 * (U + 1))
                    for j in range(4):
                        for b in range(GB):
                            last = pe.transpose(TB[0:T, j, b * T:(b + 1) * T], Pm[:, 4 * j + b, :],
                                                K["ident"][0:T, 0:T])
                        last.then_inc(turned, 1)
                    pe.wait_ge(turned_sb, 2 * (U + 1))
                    for j in range(4):
                        for b in range(GB):
                            last = pe.matmul(TB[:, j, b * T:(b + 1) * T], V[:, b, j, :], PT[:, 4 * j + b, :],
                                             start=True, stop=True)
                        last.then_inc(mixed, 1)
                    pe.wait_ge(mixed_sb, 4 * (U + 1))
                    for b in range(GB):
                        for j in range(4):
                            last = pe.matmul(TB[0:T, b, 0:D], OT[:, j, b * T:(b + 1) * T],
                                             w["wo"][:, 4 * u + j, :], start=(j == 0), stop=(j == 3))
                    last.then_inc(out_ready, 1)

                with pe.Fori(0, G) as g:
                    pe.wait_ge(xg_ready, g + 1)
                    project(g, 0)
                    values(g, 0)
                    scores(g, 0)
                    for u in range(HQ):
                        if u + 1 < HQ:
                            project(g, u + 1)
                        mix(g, u)
                        if u + 1 < HQ:
                            values(g, u + 1)
                            scores(g, u + 1)

            @block.scalar
            def _(act):
                def take_projections(g, u):
                    U = g * HQ + u
                    act.wait_ge(scores_ready, U)
                    for n in range(8):
                        act.wait_ge(proj_ready, 8 * U + n + 1)
                        act.activation((qT if n < 4 else kT)[:, n % 4, :], SB[:, n % 4, 0:GT],
                                       ACT.Copy).then_inc(qk_done, 1)

                def take_values(g, u):
                    U = g * HQ + u
                    act.wait_ge(mixed, 4 * U)
                    for b in range(GB):
                        act.wait_ge(v_ready, 4 * U + b + 1)
                        act.activation(V[:, b, :, :].rearrange("t h d -> t (h d)"), TB[0:T, b, :],
                                       ACT.Copy).then_inc(v_taken, 1)

                with act.Fori(0, G) as g:
                    act.wait_ge(out_ready, g * GB)
                    act.activation(xg[:, :, :], XT[:, :, bass.ds(g * GT, GT)], ACT.Copy).then_inc(xg_ready, 1)
                    take_projections(g, 0)
                    take_values(g, 0)
                    for u in range(HQ):
                        U = g * HQ + u
                        act.wait_ge(shifted, U + 1)
                        act.activation(Pm[:, :, :], Pm[:, :, :], ACT.Exp, scale=scale).then_inc(exp_done, 1)
                        if u + 1 < HQ:
                            take_projections(g, u + 1)
                        act.wait_ge(turned, 4 * U + 2)
                        act.wait_ge(mixed, 4 * U)
                        act.activation(PT[:, 0:8, :].rearrange("k (j i) q -> k j (i q)", j=2),
                                       TB[0:T, 0:2, 0:GT], ACT.Copy).then_inc(turned_sb, 1)
                        for j in range(4):
                            act.wait_ge(mixed, 4 * U + j + 1)
                            if j == 0:
                                act.wait_ge(out_ready, U)
                            act.activation(OT[:, j, :], TB[:, j, 0:GT], ACT.Copy).then_inc(mixed_sb, 1)
                        if u + 1 < HQ:
                            take_values(g, u + 1)

            @block.vector
            def _(dve):
                link = Chain(dve, chain)
                with dve.Fori(0, G) as g:
                    link.loop(g, 2 * HQ)
                    for u in range(HQ):
                        U = g * HQ + u
                        dve.wait_ge(scores_ready, U + 1)
                        link(dve.tensor_reduce(mx[:, :, :].rearrange("q (j i) o -> q j (i o)", j=4), Sv,
                                               AX_X, ALU.max))
                        dve.tensor_tensor(Pm[:, :, :].rearrange("q (j i) k -> q j i k", j=4), Sv,
                                          mx[:, :, :].rearrange("q (j i) o -> q j i o", j=4)
                                          .to_broadcast([T, 4, 4, T]), ALU.subtract).then_inc(shifted, 1)
                        dve.wait_ge(exp_done, U + 1)
                        link(dve.tensor_reduce(sm[:, :, :].rearrange("q h o -> q (h o)"), Pm[:, :, :],
                                               AX_X, ALU.add))
                        dve.reciprocal(sm[:, :, :], sm[:, :, :]).then_inc(sums, 1)
                        dve.wait_ge(turned, 4 * U + 4)
                        dve.wait_ge(mixed, 4 * U)
                        dve.tensor_copy(PT[:, 8:16, :].rearrange("k (j i) q -> k j (i q)", j=2),
                                        TB[0:T, 2:4, 0:GT]).then_inc(turned_sb, 1)
                        dve.wait_ge(out_ready, U + 1)
                        ag = A[:, bass.ds(g * GB, GB), :]
                        dve.tensor_tensor(ag, ag, TB[0:T, 0:GB, 0:D], ALU.add).then_inc(out_added, 1)
                        dve.wait_ge(out_added, U + 1)
                link.end(G)



NQ = 4
ROWS = STK + PARTS
SETS = 8
HKB = NKB // 2


def quad_rows(kp, part, q):
    return kp[64 * (q % 2):64 * (q % 2) + 64, q // 2, part, :]


def cross_attention_0(c, name, X, K, a):
    c.stage = name
    nc = c.nc
    STEPS = B * NQ
    with ExitStack() as s:
        mask = c.sb(s, "mask", [T, 2 * KB], BF16)
        QP = c.sb(s, "QP", [T, PARTS, B, D], BF16)
        tmp = c.sb(s, "tmp", [T, B, D])
        kf = c.sb(s, "kf", [P, 2, S2P])
        kp = c.sb(s, "kp", [P, 2, PARTS, S2P], BF16)
        KS = c.sb(s, "KS", [ROWS, NQ, 4, S2P], BF16)
        QS = c.sb(s, "QS", [ROWS, NQ, 4, T], BF16)
        QR = c.sb(s, "QR", [T, 2, 4, STK], BF16)
        V = c.sb(s, "V", [KB, NQ, NKB, 4, HD + 1])
        Pb = c.sb(s, "Pb", [KB, 2, 4, HKB * T])
        mx3, mx = c.sb(s, "mx3", [T, 2, 4, 3]), c.sb(s, "mx", [T, 4])
        nm, zero = c.sb(s, "nm", [T, 2, 4, PARTS], BF16), c.sb(s, "zero", [T, 4])
        OT, rz, on = c.sb(s, "OT", [P, T]), c.sb(s, "rz", [T, 4, 1]), c.sb(s, "on", [T, 4, HD])
        SB = c.psum(s, "SB", [P, 2, 512])
        ST = c.psum(s, "ST", [P, 2, 2, 512])
        OB = c.psum(s, "OB", [P, 512])
        TB = c.psum(s, "TB", [P, 512])
        TQ, TO = TB[:, 0:3 * P].bitcast(BF16), TB[:, 3 * P:4 * P]
        names = ("chain pchain q_in parts_ready kf_in k1_done r_done k2_done k3_done stack_in v_in q_built "
                 "q_turned q_stacked scores_ready maxed max_done neg_done neg_turned neg_stacked st_ready "
                 "exp_done pv_done ot_sb ot_turned normed added zeroed").split()
        S = {n: c.sem(n) for n in names if n not in ("stack_in", "v_in", "kf_in")}
        stack_in = [c.sem(f"stack_in{q}") for q in range(NQ)]
        v_in = [c.sem(f"v_in{q}") for q in range(NQ)]
        kf_in = [c.sem(f"kf_in{h}") for h in range(2)]
        mask_in = c.sem("mask_in")
        parts_in = S["parts_ready"]

        with nc.Block() as block:
            @block.sync
            def _(sp):
                sp.dma_start(mask[:, :], a["k_mask0"]).then_inc(mask_in, 16)

                def load_keys(b, hf):
                    sp.dma_start(kf[:, hf, :], a["ctxT0"][bass.ds(b, 1), hf, :, :]
                                 .rearrange("o p k -> (o p) k")).then_inc(kf_in[hf], 16)

                def load_values(b, q):
                    sp.dma_start(V[:, q, :, :, :].rearrange("k n h d -> k (n h d)"),
                                 a["ctxV0"][bass.ds(b, 1), q, :, :].rearrange("o k n -> (o k) n")
                                 ).then_inc(v_in[q], 16)

                def stack(parts, q):
                    sp.wait_ge(S["k3_done"], parts)
                    for r, part in enumerate((0, 1, 2, 0, 1, 0)):
                        sp.dma_start(KS[HD * r:HD * (r + 1), q, :, :], quad_rows(kp, part, q)
                                     ).then_inc(stack_in[q], 16)

                def prepare(b, known):
                    b2 = sp.snap(b + 2) if known == 0 else None
                    b1 = sp.snap(b + 1) if known == 0 else b + 1
                    for q in range(NQ):
                        parts = 2 * b + q // 2 + 3 if known else fixed(sp, 2 * b + q // 2 + 3, f"{name}_parts{q}")
                        sp.wait_ge(S["st_ready"], SETS * (NQ * b + q + 1))
                        stack(parts, q)
                        if q % 2 == 1 and known + 2 != B + 1:
                            load_keys(b2, q // 2)
                        sp.wait_ge(S["pv_done"], 2 * (NQ * b + q + 1))
                        load_values(b1, q)

                for hf in range(2):
                    load_keys(0, hf)
                for q in range(NQ):
                    load_values(0, q)
                for hf in range(2):
                    for q in (2 * hf, 2 * hf + 1):
                        stack(hf + 1, q)
                    load_keys(1, hf)
                with sp.Fori(0, B - 2) as b:
                    prepare(b, 0)
                prepare(B - 2, B - 1)

            @block.gpsimd
            def _(pool):
                link = Chain(pool, S["pchain"])
                def rest(b, hf):
                    pool.wait_ge(S["k1_done"], 2 * b + hf + 1)
                    pool.tensor_tensor(kf[:, hf, :], kf[:, hf, :], kp[:, hf, 0, :],
                                       ALU.subtract).then_inc(S["r_done"], 1)

                def third(b, hf):
                    pool.wait_ge(S["k2_done"], 2 * b + hf + 1)
                    pool.tensor_tensor(kp[:, hf, 2, :], kf[:, hf, :], kp[:, hf, 1, :],
                                       ALU.subtract).then_inc(S["k3_done"], 1)

                def build_queries(b, q):
                    n = NQ * b + q
                    if not (isinstance(n, int) and n < 2):
                        pool.wait_ge(S["q_turned"], n - 1)
                    pool.wait_ge(parts_in, 1)
                    at = 0
                    for part, times in ((0, 3), (1, 2), (2, 1)):
                        src = QP[:, part, bass.ds(b, 1), 4 * HD * q:4 * HD * (q + 1)].rearrange(
                            "t o (h d) -> t (o h) d", d=HD)
                        last = pool.tensor_copy(
                            QR[:, q % 2, :, at * HD:(at + times) * HD].rearrange("t h (r d) -> t h r d", d=HD),
                            src.unsqueeze(2).to_broadcast([T, 4, times, HD]))
                        at += times
                    last.then_inc(S["q_built"], 1)

                def negate(n, q):
                    pool.wait_ge(S["max_done"], n + 1)
                    pool.wait_ge(S["neg_turned"], n - 1) if not isinstance(n, int) or n >= 2 else None
                    link(pool.tensor_tensor(nm[:, q % 2, :, 0], mx[:, :], zero[:, :], ALU.add))
                    link(pool.tensor_tensor(mx[:, :], mx[:, :], nm[:, q % 2, :, 0], ALU.subtract))
                    link(pool.tensor_tensor(nm[:, q % 2, :, 1], mx[:, :], zero[:, :], ALU.add))
                    pool.tensor_tensor(nm[:, q % 2, :, 2], mx[:, :], nm[:, q % 2, :, 1],
                                       ALU.subtract).then_inc(S["neg_done"], 1)

                pool.wait_ge(S["parts_ready"], 1)
                for hf in range(2):
                    rest(0, hf)
                    third(0, hf)
                build_queries(0, 0)
                build_queries(0, 1)
                negate(0, 0)

                def body(b, known):
                    final = known == B - 1
                    for q in range(NQ):
                        n = NQ * b + q
                        if not final:
                            (rest if q % 2 == 0 else third)(b + 1, q // 2)
                        if not (final and q >= 2):
                            build_queries(b + (q + 2) // NQ, (q + 2) % NQ)
                        if not (final and q == 3):
                            negate(n + 1, (q + 1) % NQ)

                with pool.Fori(0, B - 1) as b:
                    link.loop(b, 3 * NQ)
                    body(b, 0)
                link.end(B - 1)
                body(B - 1, B - 1)

            @block.tensor
            def _(pe):
                def turn_queries(n, q):
                    pe.wait_ge(S["q_built"], n + 1)
                    pe.wait_ge(S["q_stacked"], n)
                    for j in range(4):
                        last = pe.transpose(TQ[0:STK, j * T:(j + 1) * T], QR[:, q % 2, j, :],
                                            K["identb"][0:T, 0:T])
                    last.then_inc(S["q_turned"], 1)

                def score_chunk(n, q, k):
                    j, part = divmod(k, 3)
                    if k == 0:
                        pe.wait_ge(S["q_stacked"], n + 1)
                    at = 12 * n + k
                    if not (isinstance(at, int) and at < 2):
                        pe.wait_ge(S["maxed"], at - 1)
                    lo, hi = CUTS[part:part + 2]
                    last = pe.matmul(SB[0:T, k % 2, 0:hi - lo], QS[0:STK, q, j, :], KS[0:STK, q, j, lo:hi],
                                     start=True, stop=(part < 2), skip_group_check=True)
                    if part == 2:
                        m = S2 - T
                        last = pe.matmul(SB[0:T, k % 2, m - lo:hi - lo], K["identb"][0:T, 0:T],
                                         mask[:, m - MASK0:S2 - MASK0], start=False, stop=True,
                                         skip_group_check=True)
                    last.then_inc(S["scores_ready"], 1)

                def turn_maxima(n, q, turned):
                    pe.wait_ge(S["neg_done"], n + 1)
                    pe.wait_ge(S["q_stacked"], turned)
                    for j in range(4):
                        last = pe.transpose(TQ[STK:ROWS, j * T:(j + 1) * T], nm[:, q % 2, j, :],
                                            K["identb"][0:T, 0:T])
                    last.then_inc(S["neg_turned"], 1)

                def score_set(n, q, k):
                    half, j = divmod(k, 4)
                    if k == 0:
                        pe.wait_ge(S["neg_stacked"], n + 1)
                    at = SETS * n + k
                    if not (isinstance(at, int) and at < 2):
                        pe.wait_ge(S["exp_done"], at - 1)
                    for i in range(HKB):
                        kb = half * HKB + i
                        dst = ST[0:KB, k % 2, i // 3, (i % 3) * T:(i % 3 + 1) * T]
                        masked = kb * KB >= MASK0
                        last = pe.matmul(dst, KS[:, q, j, kb * KB:(kb + 1) * KB], QS[:, q, j, :],
                                         start=True, stop=not masked, skip_group_check=True)
                        if masked:
                            at_mask = kb * KB - MASK0
                            last = pe.matmul(dst, mask[:, at_mask:at_mask + KB], K["identb"][0:T, 0:T], start=False, stop=True,
                                             skip_group_check=True)
                    last.then_inc(S["st_ready"], 1)

                def turn_out(n, q):
                    pe.wait_ge(S["ot_sb"], n + 1)
                    pe.wait_ge(S["added"], n)
                    pe.transpose(TO[0:T, :], OT[:, :], K["ident"][:, :]).then_inc(S["ot_turned"], 1)

                pe.wait_ge(S["zeroed"], 2)
                pe.wait_ge(mask_in, 16)
                turn_queries(0, 0)
                turn_queries(1, 1)
                pe.wait_ge(stack_in[0], 6 * 16)
                for k in range(12):
                    score_chunk(0, 0, k)
                turn_maxima(0, 0, 2)

                def body(b, known):
                    final, first = known == B - 1, known == -1
                    for q in range(NQ):
                        n = NQ * b + q
                        more = not (final and q == 3)
                        for k in range(SETS):
                            score_set(n, q, k)
                            if more and k < 6:
                                if k == 0:
                                    nb = b + (q + 1) // NQ
                                    pe.wait_ge(stack_in[(q + 1) % NQ], 6 * 16 * (nb + 1))
                                score_chunk(n + 1, (q + 1) % NQ, 2 * k)
                                score_chunk(n + 1, (q + 1) % NQ, 2 * k + 1)
                            if k < 4:
                                if not (first and q == 0):
                                    weigh(n - 1, (q - 1) % NQ, 1, k)
                            else:
                                if k == 4:
                                    pe.wait_ge(v_in[q], 16 * (b + 1))
                                    if not (first and q == 0):
                                        pe.wait_ge(S["ot_sb"], n)
                                weigh_first(n, q, k - 4)
                            if k == 5 and not (first and q == 0):
                                turn_out(n - 1, (q - 1) % NQ)
                            if k == 7 and not (final and q >= 2):
                                if not (first and q == 0):
                                    pe.wait_ge(S["added"], n)
                                turn_queries(n + 2, (q + 2) % NQ)
                        if more:
                            if not (first and q == 0):
                                pe.wait_ge(S["added"], n)
                            turn_maxima(n + 1, (q + 1) % NQ, min(n + 3, STEPS) if final else n + 3)

                def weigh_first(n, q, piece):
                    if piece == 0:
                        pe.wait_ge(S["exp_done"], SETS * n + 4)
                    for i in ((0, 1), (2,), (3, 4), (5,))[piece]:
                        products(q, 0, i, S["pv_done"] if i == 5 else None)

                def products(q, half, i, done):
                    kb = half * HKB + i
                    for j in range(4):
                        last = pe.matmul(OB[32 * j:32 * j + HD + 1, 0:T], V[:, q, kb, j, :],
                                         Pb[:, half, j, i * T:(i + 1) * T], start=(kb == 0),
                                         stop=(kb == NKB - 1), skip_group_check=True)
                    if done is not None:
                        last.then_inc(done, 1)

                def weigh(n, q, half, piece):
                    if piece == 0:
                        pe.wait_ge(S["exp_done"], SETS * (n + 1))
                    for i in ((0, 1), (2,), (3, 4), (5,))[piece]:
                        products(q, 1, i, S["pv_done"] if i == 5 else None)

                body(0, -1)
                with pe.Fori(1, B - 1) as b:
                    body(b, 0)
                body(B - 1, B - 1)
                n = STEPS - 1
                for piece in range(4):
                    weigh(n, 3, 1, piece)
                turn_out(n, 3)

            @block.scalar
            def _(act):
                def part1(b, hf):
                    act.wait_ge(kf_in[hf], 16 * (b + 1))
                    act.wait_ge(stack_in[2 * hf], 96 * b)
                    act.wait_ge(stack_in[2 * hf + 1], 96 * b)
                    act.activation(kp[:, hf, 0, :], kf[:, hf, :], ACT.Copy).then_inc(S["k1_done"], 1)

                def part2(b, hf):
                    act.wait_ge(S["r_done"], 2 * b + hf + 1)
                    act.activation(kp[:, hf, 1, :], kf[:, hf, :], ACT.Copy).then_inc(S["k2_done"], 1)

                def take_queries(n, q):
                    act.wait_ge(S["q_turned"], n + 1)
                    act.activation(QS[0:STK, q, :, :].rearrange("r h t -> r (h t)"), TQ[0:STK, 0:GT],
                                   ACT.Copy).then_inc(S["q_stacked"], 1)

                def take_maxima(n, q):
                    act.wait_ge(S["neg_turned"], n + 1)
                    act.activation(QS[STK:ROWS, q, :, :].rearrange("r h t -> r (h t)"), TQ[STK:ROWS, 0:GT],
                                   ACT.Copy).then_inc(S["neg_stacked"], 1)

                def exponential(n, k):
                    half, j = divmod(k, 4)
                    act.wait_ge(S["st_ready"], SETS * n + k + 1)
                    if j == 0 and not (isinstance(n, int) and n == 0):
                        act.wait_ge(S["pv_done"], 2 * n + half - 1)
                    act.activation(Pb[:, half, j, :].rearrange("k (c t) -> k c t", c=2), ST[0:KB, k % 2, :, 0:3 * T],
                                   ACT.Exp, scale=HD ** -0.5).then_inc(S["exp_done"], 1)

                for hf in range(2):
                    part1(0, hf)
                    part2(0, hf)
                take_queries(0, 0)
                take_queries(1, 1)
                take_maxima(0, 0)

                def body(b, known):
                    final = known == B - 1
                    for q in range(NQ):
                        n = NQ * b + q
                        for k in range(SETS):
                            exponential(n, k)
                            if k == 4 and not final:
                                (part1 if q % 2 == 0 else part2)(b + 1, q // 2)
                            if k == 7 and not (final and q >= 2):
                                take_queries(n + 2, (q + 2) % NQ)
                        if not (final and q == 3):
                            take_maxima(n + 1, (q + 1) % NQ)

                body(0, -1)
                with act.Fori(1, B - 1) as b:
                    body(b, 0)
                body(B - 1, B - 1)

            @block.vector
            def _(dve):
                link = Chain(dve, S["chain"])
                dve.memset(KS[STK:ROWS, :, :, :], 1.0).then_inc(S["zeroed"], 1)
                dve.memset(OB[:, :], 0.0).then_inc(S["zeroed"], 1)
                link(dve.memset(zero[:, :], 0.0))
                link(dve.tensor_copy(QP[:, 0, :, :], X[:, :, :]))
                link(dve.tensor_tensor(tmp[:, :, :], X[:, :, :], QP[:, 0, :, :], ALU.subtract))
                link(dve.tensor_copy(QP[:, 1, :, :], tmp[:, :, :]))
                dve.tensor_tensor(QP[:, 2, :, :], tmp[:, :, :], QP[:, 1, :, :],
                                  ALU.subtract).then_inc(S["parts_ready"], 1)

                def chunk(n, q, k):
                    j, part = divmod(k, 3)
                    dve.wait_ge(S["scores_ready"], 12 * n + k + 1)
                    dve.tensor_reduce(mx3[:, q % 2, j, part:part + 1],
                                      SB[0:T, k % 2, 0:CUTS[part + 1] - CUTS[part]], AX_X,
                                      ALU.max).then_inc(S["maxed"], 1)

                def maximum(n, q):
                    dve.wait_ge(S["maxed"], 12 * (n + 1))
                    dve.wait_ge(S["neg_done"], n)
                    dve.tensor_reduce(mx[:, :], mx3[:, q % 2, :, :], AX_X, ALU.max,
                                      negate=True).then_inc(S["max_done"], 1)

                def take_out(n, q):
                    dve.wait_ge(S["pv_done"], 2 * (n + 1))
                    dve.wait_ge(S["ot_turned"], n)
                    dve.tensor_copy(OT[:, :], OB[:, 0:T]).then_inc(S["ot_sb"], 1)

                def add_out(n, b, q):
                    dve.wait_ge(S["ot_turned"], n + 1)
                    o = TO[0:T, :].rearrange("t (j d) -> t j d", j=4)
                    link(dve.reciprocal(rz[:, :, :], o[:, :, HD:HD + 1]))
                    link(dve.tensor_tensor(on[:, :, :], o[:, :, 0:HD], rz[:, :, :].to_broadcast([T, 4, HD]),
                                           ALU.mult))
                    xb = X[:, bass.ds(b, 1), 4 * HD * q:4 * HD * (q + 1)].rearrange("t o (j d) -> t (o j) d", d=HD)
                    dve.tensor_tensor(xb, xb, on[:, :, :], ALU.add).then_inc(S["added"], 1)

                for k in range(12):
                    chunk(0, 0, k)
                maximum(0, 0)

                def body(b, known):
                    final, first = known == B - 1, known == -1
                    for q in range(NQ):
                        n = NQ * b + q
                        more = not (final and q == 3)
                        for k in range(SETS):
                            if more and k < 6:
                                chunk(n + 1, (q + 1) % NQ, 2 * k)
                                chunk(n + 1, (q + 1) % NQ, 2 * k + 1)
                            if k == 3 and not (first and q == 0):
                                take_out(n - 1, (q - 1) % NQ)
                            if k == 5 and more:
                                maximum(n + 1, (q + 1) % NQ)
                            if k == 6 and not (first and q == 0):
                                add_out(n - 1, b if q > 0 else b - 1, (q - 1) % NQ)

                body(0, -1)
                with dve.Fori(1, B - 1) as b:
                    link.loop(b - 1, 2 * NQ)
                    body(b, 0)
                link.end(B - 2)
                body(B - 1, B - 1)
                take_out(STEPS - 1, 3)
                add_out(STEPS - 1, B - 1, 3)



def latent_and_experts(c, X, A, K, a):
    nc = c.nc
    with ExitStack() as s:
        c.stage = "la"
        XT = c.sb(s, "XT", [P, DC, N])
        with ExitStack() as s2:
            w = weights(c, s2, a, "L0l_", {"wq": [P, DC, H * P], "wk": [P, DC, H * P], "wv": [P, DC, H * P],
                                         "wo": [P, H, D], "nw": [P, DC]})
            features_first(c, "lan", X, XT, K["ident"], rms=True, weight=w["nw"])
            copy_tokens(c, "lac", A, X)
            latent_attention(c, "laa", A, XT, K, w, (P + 64) ** -0.5)
        with ExitStack() as s2:
            c.stage = "moe"
            w = weights(c, s2, a, "L0m_", {"nw": [P, DC], "gate": [P, DC, E0], "wg": [P, DC, EC * P],
                                         "wu": [P, DC, EC * P], "wd": [P, EC, D], "sg": [P, DC, SHI],
                                         "su": [P, DC, SHI], "sd": [P, 3, D], "prio": [T, E0]})
            features_first(c, "moen", A, XT, K["ident"], rms=True, weight=w["nw"])
            sel = c.sb(s2, "sel", [96, EC * P], BF16)
            load(c, "moesel", [(sel[:, :], a["k_experts"])])
            WT = c.sb(s2, "WT", [96, N], BF16)
            route_top4(c, "rt", XT, WT, K, w)
            copy_tokens(c, "moec", X, A, add=True)
            experts(c, "moe", X, XT, WT, sel, w)
    layernorm(c, "ff0l", X)


def copy_tokens(c, name, dst, src, add=False):
    c.stage = name
    with c.nc.Block() as block:
        @block.gpsimd
        def _(pool):
            if add:
                pool.tensor_tensor(dst[:, :, :], dst[:, :, :], src[:, :, :], ALU.add)
            else:
                pool.tensor_copy(dst[:, :, :], src[:, :, :])


def first_of(link, dve, work, best, rank, pick, prio, n):
    wide = lambda t: t[:, :, :].to_broadcast([T, B, n])
    link(dve.tensor_reduce(best[:, :, 0], work[:, :, :], AX_X, ALU.max))
    link(dve.tensor_tensor(pick[:, :, :], work[:, :, :], wide(best), ALU.is_equal))
    link(dve.tensor_tensor(pick[:, :, :], pick[:, :, :], prio.unsqueeze(1).to_broadcast([T, B, n]), ALU.mult))
    link(dve.tensor_reduce(rank[:, :, 0], pick[:, :, :], AX_X, ALU.max))
    link(dve.tensor_tensor(pick[:, :, :], pick[:, :, :], wide(rank), ALU.is_equal))


def router_logits(pe, LG, XT, gate, n, done):
    for b in range(B):
        for ch in range(DC):
            last = pe.matmul(LG[0:T, b * n:(b + 1) * n], XT[:, ch, b * T:(b + 1) * T], gate[:, ch, :],
                             start=(ch == 0), stop=(ch == DC - 1))
    last.then_inc(done, 1)


def route_top4(c, name, XT, WT, K, w):
    c.stage = name
    nc = c.nc
    with ExitStack() as s:
        e, work, pick, chosen = (c.sb(s, n, [T, B, E0]) for n in ("e", "work", "pick", "chosen"))
        best, rank = c.sb(s, "best", [T, B, 1]), c.sb(s, "rank", [T, B, 1])
        WP = c.sb(s, "WP", [T, B, 96], BF16)
        LG = c.psum(s, "LG", [P, 512])
        WB = c.psum(s, "WB", [P, 4, 1024], BF16)
        chain, logits, shifted, exp_done, parts, turned = (c.sem(n) for n in (
            "chain", "logits", "shifted", "exp_done", "parts", "turned"))
        with nc.Block() as block:
            @block.tensor
            def _(pe):
                router_logits(pe, LG, XT, w["gate"], E0, logits)
                pe.wait_ge(parts, 1)
                for b in range(B):
                    last = pe.transpose(WB[0:96, b // 4, (b % 4) * T:(b % 4 + 1) * T], WP[:, b, :],
                                        K["identb"][0:T, 0:T])
                last.then_inc(turned, 1)

            @block.scalar
            def _(act):
                act.wait_ge(shifted, 1)
                act.activation(e[:, :, :], e[:, :, :], ACT.Exp).then_inc(exp_done, 1)
                act.wait_ge(turned, 1)
                act.activation(WT[:, :].rearrange("r (g t) -> r g t", g=G), WB[0:96, :, 0:GT], ACT.Copy)

            @block.vector
            def _(dve):
                link = Chain(dve, chain)
                link(dve.memset(WP[:, :, :], 0.0))
                link(dve.memset(chosen[:, :, :], 0.0))
                dve.wait_ge(logits, 1)
                lg = LG[0:T, 0:B * E0].rearrange("t (b e) -> t b e", b=B)
                wide = lambda t: t[:, :, :].to_broadcast([T, B, E0])
                link(dve.tensor_reduce(best[:, :, 0], lg, AX_X, ALU.max))
                dve.tensor_tensor(e[:, :, :], lg, wide(best), ALU.subtract).then_inc(shifted, 1)
                dve.wait_ge(exp_done, 1)
                link(dve.tensor_copy(work[:, :, :], e[:, :, :]))
                for k in range(TOPK):
                    first_of(link, dve, work, best, rank, pick, w["prio"][:, :], E0)
                    link(dve.tensor_tensor(chosen[:, :, :], chosen[:, :, :], pick[:, :, :], ALU.add))
                    if k < TOPK - 1:
                        link(dve.tensor_scalar(pick[:, :, :], pick[:, :, :], -4.0, None, ALU.mult))
                        link(dve.tensor_tensor(work[:, :, :], work[:, :, :], pick[:, :, :], ALU.add))
                link(dve.tensor_tensor(e[:, :, :], e[:, :, :], chosen[:, :, :], ALU.mult))
                link(dve.tensor_reduce(best[:, :, 0], e[:, :, :], AX_X, ALU.add))
                link(dve.reciprocal(best[:, :, :], best[:, :, :]))
                link(dve.tensor_tensor(e[:, :, :], e[:, :, :], wide(best), ALU.mult))
                link(dve.tensor_copy(WP[:, :, 0:E0], e[:, :, :]))
                link(dve.tensor_tensor(e[:, :, :], e[:, :, :], WP[:, :, 0:E0], ALU.subtract))
                link(dve.tensor_copy(WP[:, :, 32:32 + E0], e[:, :, :]))
                dve.tensor_tensor(WP[:, :, 64:64 + E0], e[:, :, :], WP[:, :, 32:32 + E0],
                                  ALU.subtract).then_inc(parts, 1)


def experts(c, name, X, XT, WT, sel, w):
    c.stage = name
    nc = c.nc
    NC = EC + 3
    width = lambda k: P if k < EC else min(P, SHI - (k - EC) * P)
    with ExitStack() as s:
        sg, hid = c.sb(s, "gated", [P, 2, GT]), c.sb(s, "hid", [P, 2, GT])
        HB = c.psum(s, "HB", [P, 2, 3, 512])
        OB = c.psum(s, "OB", [P, 2, 512])
        silu_done, up_done, hid_ready, gu_ready, chunk_done, out_ready, added = (c.sem(n) for n in (
            "silu_done", "up_done", "hid_ready", "gu_ready", "chunk_done", "out_ready", "added"))
        with nc.Block() as block:
            @block.tensor
            def _(pe):
                def up(g, k):
                    M = width(k)
                    n = g * NC + k
                    if k >= 2:
                        pe.wait_ge(hid_ready, n - 1)
                    elif not isinstance(g, int):
                        pe.wait_ge(out_ready, g)
                        pe.wait_ge(added, g)
                    tok = bass.ds(g * GT, GT)
                    mats = ("wg", "wu") if k < EC else ("sg", "su")
                    at = (k if k < EC else k - EC) * P
                    for i in range(2):
                        for ch in range(DC):
                            last = pe.matmul(HB[0:M, k % 2, i, 0:GT], w[mats[i]][:, ch, at:at + M], XT[:, ch, tok],
                                             start=(ch == 0), stop=(ch == DC - 1))
                    if k < EC:
                        last = pe.matmul(HB[0:M, k % 2, 2, 0:GT], sel[:, at:at + M], WT[:, tok],
                                         start=True, stop=True)
                    last.then_inc(gu_ready, 1)

                def down(g, k):
                    M = width(k)
                    pe.wait_ge(hid_ready, g * NC + k + 1)
                    wd = w["wd"][0:M, k, :] if k < EC else w["sd"][0:M, k - EC, :]
                    for b in range(GB):
                        last = pe.matmul(OB[0:T, b // 2, (b % 2) * D:(b % 2 + 1) * D], hid[0:M, k % 2, b * T:(b + 1) * T],
                                         wd, start=(k == 0 and b % 2 == 0), stop=(k == NC - 1),
                                         skip_group_check=True)
                    last.then_inc(chunk_done, 1)
                    if k == NC - 1:
                        pe.wait_ge(chunk_done, (g + 1) * NC)
                        pe.sem_inc(out_ready, 1)

                with pe.Fori(0, G) as g:
                    up(g, 0)
                    for k in range(NC):
                        if k + 1 < NC:
                            up(g, k + 1)
                        down(g, k)

            @block.scalar
            def _(act):
                with act.Fori(0, G) as g:
                    for k in range(NC):
                        M = width(k)
                        n = g * NC + k
                        act.wait_ge(gu_ready, n + 1)
                        if k >= 2:
                            act.wait_ge(up_done, n - 1)
                        else:
                            act.wait_ge(up_done, g * NC)
                        act.activation(sg[0:M, k % 2, :], HB[0:M, k % 2, 0, 0:GT], ACT.Silu).then_inc(silu_done, 1)

            @block.vector
            def _(dve):
                with dve.Fori(0, G) as g:
                    for k in range(NC):
                        M = width(k)
                        n = g * NC + k
                        dve.wait_ge(silu_done, n + 1)
                        if k >= 2:
                            dve.wait_ge(chunk_done, n - 1)
                        else:
                            dve.wait_ge(chunk_done, g * NC)
                        h = hid[0:M, k % 2, :]
                        ins = dve.tensor_tensor(h, HB[0:M, k % 2, 1, 0:GT], sg[0:M, k % 2, :], ALU.mult)
                        ins.then_inc(up_done, 1)
                        if k < EC:
                            dve.wait_ge(up_done, n + 1)
                            dve.tensor_tensor(h, h, HB[0:M, k % 2, 2, 0:GT], ALU.mult).then_inc(hid_ready, 1)
                        else:
                            dve.wait_ge(up_done, n + 1)
                            dve.sem_inc(hid_ready, 1)
                    dve.wait_ge(out_ready, g + 1)
                    xg = X[:, bass.ds(g * GB, GB), :].rearrange("t b d -> t (b d)").rearrange("t (i n) -> t i n", i=2)
                    dve.tensor_tensor(xg, xg, OB[0:T, :, :], ALU.add).then_inc(added, 1)
                    dve.wait_ge(added, g + 1)



def cross_attention_1(c, name, X, K, a):
    c.stage = name
    nc = c.nc
    LIM = 50.0 * HD ** 0.5
    MROWS = STK + 1
    XT = None
    with ExitStack() as s:
        A = c.sb(s, "A", [T, B, D])
        QP = c.sb(s, "QP", [T, PARTS, B, D], BF16)
        rs = c.sb(s, "rs", [T, 1])
        c.stage = name + "w"
        wo = c.sb(s, "wo", [P, DC, D])
        bo, bq, bv = (c.sb(s, n, [1, D]) for n in ("bo", "bq", "bv"))
        bk = c.sb(s, "bk", [P, 2])
        wk, wv = c.sb(s, "wk", [P, DC, D]), c.sb(s, "wv", [P, DC, D])
        load(c, name + "l", [(wk[:, :, :], a["L1x_wk"]), (wv[:, :, :], a["L1x_wv"]), (wo[:, :, :], a["L1x_wo"]),
                             (bo[:, :], a["L1x_bo"]), (bq[:, :], a["L1x_bq"]), (bv[:, :], a["L1x_bv"]),
                             (bk[:, :], a["L1x_bk"]), (rs[:, :], a["L1x_rs"])])
        query_parts(c, name + "q", X, A, QP, bq, K, a)
        mask_rows(c, name + "m", a)
        projected_context(c, name, A, QP, K, a, wk, wv, wo, bk, bv, bo, LIM, MROWS)
        with ExitStack() as s2:
            c.stage = name + "n"
            gamma, beta = c.sb(s2, "gamma", [T, D]), c.sb(s2, "beta", [T, D])
            load(c, name + "g", [(gamma[:, :], a["L1x_gamma"].partition_broadcast(T)),
                                 (beta[:, :], a["L1x_beta"].partition_broadcast(T))])
            clip_scale(c, name + "r", rs)
            layernorm(c, name + "d", A, gamma=gamma[:, :], beta=beta[:, :], scale=rs[:, 0:1])
        copy_tokens(c, name + "a", X, A, add=True)


def clip_scale(c, name, rs):
    c.stage = name
    with c.nc.Block() as block:
        @block.vector
        def _(dve):
            dve.tensor_scalar(rs[:, :], rs[:, :], 0.0, 0.3, ALU.max, ALU.min)


def query_parts(c, name, X, A, QP, bq, K, a):
    nc = c.nc
    with ExitStack() as s:
        c.stage = name
        XT = c.sb(s, "XT", [P, DC, N])
        wq = c.sb(s, "wq", [P, DC, D])
        load(c, name + "l", [(wq[:, :, :], a["L1x_wq"])])
        features_first(c, name + "t", X, XT, K["ident"])
        c.stage = name
        QB = c.psum(s, "QB", [P, 8, 512])
        chain, made = c.sem("chain"), c.sem("made")
        with nc.Block() as block:
            @block.tensor
            def _(pe):
                for n in range(B):
                    dst = QB[0:T, n // 2, (n % 2) * D:(n % 2 + 1) * D]
                    for ch in range(DC):
                        pe.matmul(dst, XT[:, ch, n * T:(n + 1) * T], wq[:, ch, :], start=(ch == 0), stop=False)
                    pe.matmul(dst, K["ones"][0:1, 0:T], bq[:, :], start=False, stop=True).then_inc(made, 1)

            @block.vector
            def _(dve):
                link = Chain(dve, chain)
                for n in range(8):
                    dve.wait_ge(made, 2 * n + 2)
                    last = dve.tensor_copy(A[:, 2 * n:2 * n + 2, :].rearrange("t b d -> t (b d)"), QB[0:T, n, :])
                link(last)
                link(dve.tensor_copy(QP[:, 0, :, :], A[:, :, :]))
                link(dve.tensor_tensor(A[:, :, :], A[:, :, :], QP[:, 0, :, :], ALU.subtract))
                link(dve.tensor_copy(QP[:, 1, :, :], A[:, :, :]))
                dve.tensor_tensor(QP[:, 2, :, :], A[:, :, :], QP[:, 1, :, :], ALU.subtract)


def mask_rows(c, name, a):
    c.stage = name
    nc = c.nc
    with ExitStack() as s:
        mi = c.sb(s, "mi", [B, S2P], I32)
        mf = c.sb(s, "mf", [B, S2P])
        mb = c.sb(s, "mb", [B, S2P], BF16)
        landed, chain, stored = c.sem("landed"), c.sem("chain"), c.sem("stored")
        with nc.Block() as block:
            @block.vector
            def _(dve):
                link = Chain(dve, chain)
                dve.wait_ge(landed, 16)
                link(dve.tensor_copy(mf[:, :], mi[:, :]))
                link(dve.tensor_scalar(mf[:, :], mf[:, :], 0.5, None, ALU.is_gt))
                link(dve.tensor_scalar(mb[:, :], mf[:, :], 1.0, -NEG, ALU.subtract, ALU.mult))

            @block.sync
            def _(sp):
                sp.dma_start(mi[:, :], a["mask"]).then_inc(landed, 16)
                sp.wait_ge(chain, 3)
                for h in range(4):
                    sp.dma_start(a["s_mask"][:, h, :], mb[:, :]).then_inc(stored, 16)
                sp.wait_ge(stored, 4 * 16)


def projected_context(c, name, A, QP, K, a, wk, wv, wo, bk, bv, bo, LIM, MROWS):
    c.stage = name
    nc = c.nc
    STEPS = B * NQ
    with ExitStack() as s:
        cx = c.sb(s, "cx", [P, DC, S2P])
        kf = c.sb(s, "kf", [P, S2P])
        kp = c.sb(s, "kp", [P, PARTS, S2P], BF16)
        KS = c.sb(s, "KS", [MROWS, NQ, 4, S2P], BF16)
        QS = c.sb(s, "QS", [MROWS, NQ, 4, T], BF16)
        QR = c.sb(s, "QR", [T, 2, 4, STK], BF16)
        V = c.sb(s, "V", [KB, NQ, NKB, 4, HD + 1])
        Cb = c.sb(s, "Cb", [KB, 2, HKB * T])
        Pb = c.sb(s, "Pb", [KB, 2, 4, HKB * T])
        OT = c.sb(s, "OT", [P, T])
        rz, sz, on = c.sb(s, "rz", [T, 4, 1]), c.sb(s, "sz", [T, 4, 1]), c.sb(s, "on", [T, D])
        oT = c.sb(s, "oT", [P, DC, T])
        PR = c.psum(s, "PR", [P, 2, 512])
        ST = c.psum(s, "ST", [P, 2, 2, 512])
        OB = c.psum(s, "OB", [P, 512])
        TB = c.psum(s, "TB", [P, 512])
        TQ, TO = TB[:, 0:3 * P].bitcast(BF16), TB[:, 3 * P:4 * P]
        names = ("chain kchain r_done k3_done k1_done k2_done q_built q_turned q_stacked st_ready clipped "
                 "exp_done pv_done ot_sb ot_turned normed zeroed made taken on_turned on_sb out_ready added "
                 "cx_used cx_in mask_in v_done kf_done").split()
        S = {n: c.sem(n) for n in names}
        stack_in = [c.sem(f"stack_in{q}") for q in range(NQ)]
        parts_in = S["zeroed"]
        NPR = 2 * 3 + NKB * 2

        with nc.Block() as block:
            @block.sync
            def _(sp):
                def load_context(b):
                    sp.dma_start(cx[:, :, :], a["ctxT1"][bass.ds(b, 1), :, :, :]
                                 .rearrange("o p c k -> (o p) c k")).then_inc(S["cx_in"], 16)

                def stack(b, q, parts):
                    sp.wait_ge(S["k3_done"], parts)
                    for r, part in enumerate((0, 1, 2, 0, 1, 0)):
                        sp.dma_start(KS[HD * r:HD * (r + 1), q, :, :], kp[64 * (q % 2):64 * (q % 2) + 64, part, :]
                                     ).then_inc(stack_in[q], 16)
                    sp.dma_start(KS[STK:MROWS, q, :, :], a["s_mask"][bass.ds(b, 1), :, :]).then_inc(stack_in[q], 16)

                load_context(0)
                for q in range(NQ):
                    stack(0, q, q // 2 + 1)
                sp.wait_ge(S["made"], NPR)
                load_context(1)
                def prepare(b, more):
                    b1 = sp.snap(b + 1) if more else b + 1
                    b2 = sp.snap(b + 2) if more else None
                    for q in range(NQ):
                        parts = fixed(sp, 2 * b + q // 2 + 3, f"{name}_parts{q}") if more else 2 * b + q // 2 + 3
                        sp.wait_ge(S["st_ready"], SETS * (NQ * b + q + 1))
                        stack(b1, q, parts)
                    if more:
                        sp.wait_ge(S["made"], NPR * (b + 2))
                        sp.wait_ge(S["cx_in"], 16)
                        load_context(b2)
                with sp.Fori(0, B - 2) as b:
                    prepare(b, True)
                prepare(B - 2, False)

            @block.gpsimd
            def _(pool):
                def rest(n):
                    pool.wait_ge(S["k1_done"], n + 1)
                    pool.tensor_tensor(kf[:, :], kf[:, :], kp[:, 0, :], ALU.subtract).then_inc(S["r_done"], 1)

                def third(n):
                    pool.wait_ge(S["k2_done"], n + 1)
                    pool.tensor_tensor(kp[:, 2, :], kf[:, :], kp[:, 1, :], ALU.subtract).then_inc(S["k3_done"], 1)

                def build_queries(b, q):
                    n = NQ * b + q
                    if not (isinstance(n, int) and n < 2):
                        pool.wait_ge(S["q_turned"], n - 1)
                    pool.wait_ge(parts_in, 1)
                    at = 0
                    for part, times in ((0, 3), (1, 2), (2, 1)):
                        src = QP[:, part, bass.ds(b, 1), 4 * HD * q:4 * HD * (q + 1)].rearrange(
                            "t o (h d) -> t (o h) d", d=HD)
                        last = pool.tensor_copy(
                            QR[:, q % 2, :, at * HD:(at + times) * HD].rearrange("t h (r d) -> t h r d", d=HD),
                            src.unsqueeze(2).to_broadcast([T, 4, times, HD]))
                        at += times
                    last.then_inc(S["q_built"], 1)

                build_queries(0, 0)
                build_queries(0, 1)
                for hf in range(2):
                    rest(hf)
                    third(hf)

                def body(b, final):
                    for q in range(NQ):
                        if not (final and q >= 2):
                            build_queries(b + (q + 2) // NQ, (q + 2) % NQ)
                        if not final and q >= 2:
                            rest(2 * (b + 1) + q - 2)
                            third(2 * (b + 1) + q - 2)
                with pool.Fori(0, B - 1) as b:
                    body(b, False)
                body(B - 1, True)

            @block.tensor
            def _(pe):
                def project_keys(b, hf):
                    for k in range(3):
                        n = NPR * b + (3 + NKB) * hf + k
                        if not (isinstance(n, int) and n < 2):
                            pe.wait_ge(S["taken"], n - 1)
                        lo, hi = CUTS[k:k + 2]
                        for ch in range(DC):
                            last = pe.matmul(PR[:, (3 + NKB) * hf + k & 1, 0:hi - lo], wk[:, ch, hf * P:(hf + 1) * P],
                                             cx[:, ch, lo:hi], start=(ch == 0), stop=(ch == DC - 1))
                        last.then_inc(S["made"], 1)

                def project_values(b, hf, blocks):
                    for k in blocks:
                        n = NPR * b + (3 + NKB) * hf + 3 + k
                        pe.wait_ge(S["taken"], n - 1)
                        dst = PR[0:KB, (3 + NKB) * hf + 3 + k & 1, 0:P]
                        for ch in range(DC):
                            pe.matmul(dst, cx[:, ch, k * KB:(k + 1) * KB], wv[:, ch, hf * P:(hf + 1) * P],
                                      start=(ch == 0), stop=False)
                        last = pe.matmul(dst, K["ones"][0:1, 0:KB], bv[:, hf * P:(hf + 1) * P], start=False, stop=True)
                        last.then_inc(S["made"], 1)

                def turn_queries(n, q):
                    pe.wait_ge(S["q_built"], n + 1)
                    pe.wait_ge(S["q_stacked"], n)
                    for j in range(4):
                        last = pe.transpose(TQ[0:STK, j * T:(j + 1) * T], QR[:, q % 2, j, :],
                                            K["identb"][0:T, 0:T])
                    last.then_inc(S["q_turned"], 1)

                def score_set(n, q, k):
                    half, j = divmod(k, 4)
                    if k == 0:
                        pe.wait_ge(S["q_stacked"], n + 1)
                    at = SETS * n + k
                    if not (isinstance(at, int) and at < 2):
                        pe.wait_ge(S["clipped"], at - 1)
                    for i in range(HKB):
                        kb = half * HKB + i
                        last = pe.matmul(ST[0:KB, k % 2, i // 3, (i % 3) * T:(i % 3 + 1) * T],
                                         KS[:, q, j, kb * KB:(kb + 1) * KB], QS[:, q, j, :],
                                         start=True, stop=True)
                    last.then_inc(S["st_ready"], 1)

                def weigh(n, q, half, piece):
                    if piece == 0:
                        pe.wait_ge(S["exp_done"], SETS * n + 4 * half + 4)
                    for i in ((0, 1), (2,), (3, 4), (5,))[piece]:
                        kb = half * HKB + i
                        for j in range(4):
                            last = pe.matmul(OB[32 * j:32 * j + HD + 1, 0:T], V[:, q, kb, j, :],
                                             Pb[:, half, j, i * T:(i + 1) * T], start=(kb == 0),
                                             stop=(kb == NKB - 1), skip_group_check=True)
                    if piece == 3:
                        last.then_inc(S["pv_done"], 1)

                def turn_out(n, q):
                    pe.wait_ge(S["ot_sb"], n + 1)
                    pe.transpose(TO[0:T, :], OT[:, :], K["ident"][:, :]).then_inc(S["ot_turned"], 1)

                pe.wait_ge(S["zeroed"], 3)
                turn_queries(0, 0)
                turn_queries(1, 1)
                pe.wait_ge(S["cx_in"], 16)
                for hf in range(2):
                    project_keys(0, hf)
                    project_values(0, hf, range(NKB))

                def body(b, first, final):
                    for q in range(NQ):
                        n = NQ * b + q
                        for k in range(SETS):
                            if k == 0:
                                pe.wait_ge(stack_in[q], 7 * 16 * (b + 1))
                            score_set(n, q, k)
                            if k < 4:
                                if not (first and q == 0):
                                    weigh(n - 1, (q - 1) % NQ, 1, k)
                            else:
                                if k == 4 and not (first and q == 0):
                                    pe.wait_ge(S["ot_sb"], n)
                                if k == 4 and q % 2 == 0:
                                    pe.wait_ge(S["taken"], NPR * b + (3 + NKB) * (q // 2 + 1))
                                weigh(n, q, 0, k - 4)
                            if k == 5 and not (first and q == 0):
                                turn_out(n - 1, (q - 1) % NQ)
                            if k == 7 and not (final and q >= 2):
                                if not (first and q == 0):
                                    pe.wait_ge(S["added"], n)
                                turn_queries(n + 2, (q + 2) % NQ)
                        if q == 0 and not first:
                            project_values(b, 1, range(NKB))
                        if not final:
                            if q == 2:
                                pe.wait_ge(S["cx_in"], 16 * (b + 2))
                                project_keys(b + 1, 0)
                                project_values(b + 1, 0, range(NKB))
                            if q == 3:
                                project_keys(b + 1, 1)
                body(0, True, False)
                with pe.Fori(1, B - 1) as b:
                    body(b, False, False)
                body(B - 1, False, True)
                n = STEPS - 1
                for piece in range(4):
                    weigh(n, 3, 1, piece)
                turn_out(n, 3)

            @block.scalar
            def _(act):
                def take_keys(b, hf):
                    n = 2 * b + hf
                    if not (isinstance(n, int) and n == 0):
                        act.wait_ge(S["k3_done"], n)
                    for k in range(3):
                        at = NPR * b + (3 + NKB) * hf + k
                        act.wait_ge(S["made"], at + 1)
                        lo, hi = CUTS[k:k + 2]
                        last = act.activation(kf[:, lo:hi], PR[:, (3 + NKB) * hf + k & 1, 0:hi - lo],
                                              ACT.Identity, bias=bk[:, hf:hf + 1])
                        last.then_inc(S["taken"], 1)
                    act.wait_ge(S["taken"], NPR * b + (3 + NKB) * hf + 3)
                    if not (isinstance(n, int) and n == 0):
                        for q in ((2, 3) if hf == 0 else (0, 1)):
                            act.wait_ge(stack_in[q], 112 * (b if hf == 0 else b + 1))
                    act.activation(kp[:, 0, :], kf[:, :], ACT.Copy).then_inc(S["k1_done"], 1)
                    act.wait_ge(S["r_done"], n + 1)
                    act.activation(kp[:, 1, :], kf[:, :], ACT.Copy).then_inc(S["k2_done"], 1)

                def take_values(b, hf):
                    if not (isinstance(b, int) and b == 0):
                        act.wait_ge(S["pv_done"], 2 * (NQ * (b - 1) + 2 * hf + 2))
                    for k in range(NKB):
                        at = NPR * b + (3 + NKB) * hf + 3 + k
                        rows = KB if k < NKB - 1 else LASTKB
                        act.wait_ge(S["made"], at + 1)
                        act.activation(V[0:rows, 2 * hf:2 * hf + 2, k, :, 0:HD],
                                       PR[0:rows, (3 + NKB) * hf + 3 + k & 1, 0:P]
                                       .rearrange("k (q h d) -> k q h d", q=2, h=4), ACT.Copy).then_inc(S["taken"], 1)

                def take_queries(n, q):
                    act.wait_ge(S["q_turned"], n + 1)
                    act.activation(QS[0:STK, q, :, :].rearrange("r h t -> r (h t)"), TQ[0:STK, 0:GT],
                                   ACT.Copy).then_inc(S["q_stacked"], 1)

                def exponential(n, k):
                    half, j = divmod(k, 4)
                    act.wait_ge(S["clipped"], SETS * n + k + 1)
                    if j == 0 and not (isinstance(n, int) and n == 0):
                        act.wait_ge(S["pv_done"], 2 * n + half - 1)
                    act.activation(Pb[:, half, j, :], Cb[:, k % 2, :], ACT.Exp, scale=HD ** -0.5
                                   ).then_inc(S["exp_done"], 1)

                act.wait_ge(S["zeroed"], 3)
                take_queries(0, 0)
                take_queries(1, 1)
                for hf in range(2):
                    take_keys(0, hf)
                    take_values(0, hf)

                def body(b, first, final):
                    for q in range(NQ):
                        n = NQ * b + q
                        for k in range(SETS):
                            exponential(n, k)
                            if k == 7 and not (final and q >= 2):
                                take_queries(n + 2, (q + 2) % NQ)
                        if q == 0 and not first:
                            take_values(b, 1)
                        if not final:
                            if q == 2:
                                take_keys(b + 1, 0)
                                take_values(b + 1, 0)
                            if q == 3:
                                take_keys(b + 1, 1)
                body(0, True, False)
                with act.Fori(1, B - 1) as b:
                    body(b, False, False)
                body(B - 1, False, True)

            @block.vector
            def _(dve):
                link = Chain(dve, S["chain"])
                link(dve.memset(V[:, :, :, :, :], 0.0))
                link(dve.memset(V[:, :, 0:NKB - 1, :, HD:HD + 1], 1.0))
                dve.memset(V[0:LASTKB, :, NKB - 1, :, HD:HD + 1], 1.0).then_inc(S["zeroed"], 1)
                link(dve.memset(kf[:, S2:S2P], 0.0))
                dve.memset(QS[STK:MROWS, :, :, :], 1.0).then_inc(S["zeroed"], 1)
                dve.memset(OB[:, :], 0.0).then_inc(S["zeroed"], 1)

                def clip(n, k):
                    at = SETS * n + k
                    dve.wait_ge(S["st_ready"], at + 1)
                    if not (isinstance(at, int) and at < 2):
                        dve.wait_ge(S["exp_done"], at - 1)
                    dve.tensor_scalar(Cb[:, k % 2, :].rearrange("k (c t) -> k c t", c=2), ST[0:KB, k % 2, :, 0:3 * T],
                                      LIM, -LIM, ALU.min, ALU.max).then_inc(S["clipped"], 1)

                def take_out(n, q):
                    dve.wait_ge(S["pv_done"], 2 * (n + 1))
                    dve.wait_ge(S["ot_turned"], n)
                    dve.tensor_copy(OT[:, :], OB[:, 0:T]).then_inc(S["ot_sb"], 1)

                def add_out(n, b, q):
                    dve.wait_ge(S["ot_turned"], n + 1)
                    o = TO[0:T, :].rearrange("t (j d) -> t j d", j=4)
                    link(dve.reciprocal(rz[:, :, :], o[:, :, HD:HD + 1]))
                    link(dve.tensor_tensor(sz[:, :, :], o[:, :, HD:HD + 1], rz[:, :, :], ALU.mult))
                    link(dve.tensor_scalar(sz[:, :, :], sz[:, :, :], 1e-8, None, ALU.add))
                    link(dve.reciprocal(sz[:, :, :], sz[:, :, :]))
                    link(dve.tensor_tensor(rz[:, :, :], rz[:, :, :], sz[:, :, :], ALU.mult))
                    xb = A[:, bass.ds(b, 1), 4 * HD * q:4 * HD * (q + 1)].rearrange("t o (j d) -> t (o j) d", d=HD)
                    dve.tensor_tensor(xb, o[:, :, 0:HD], rz[:, :, :].to_broadcast([T, 4, HD]),
                                      ALU.mult).then_inc(S["added"], 1)

                def body(b, first, final):
                    for q in range(NQ):
                        n = NQ * b + q
                        for k in range(SETS):
                            clip(n, k)
                            if k == 3 and not (first and q == 0):
                                take_out(n - 1, (q - 1) % NQ)
                            if k == 6 and not (first and q == 0):
                                add_out(n - 1, b if q > 0 else b - 1, (q - 1) % NQ)
                body(0, True, False)
                with dve.Fori(1, B - 1) as b:
                    link.loop(b - 1, 5 * NQ)
                    body(b, False, False)
                link.end(B - 2)
                body(B - 1, False, True)
                take_out(STEPS - 1, 3)
                add_out(STEPS - 1, B - 1, 3)
    project_out(c, name + "o", A, K, wo, bo)


def project_out(c, name, A, K, wo, bo):
    nc = c.nc
    with ExitStack() as s:
        c.stage = name
        AT = c.sb(s, "AT", [P, DC, N])
        features_first(c, name + "t", A, AT, K["ident"])
        c.stage = name
        QB = c.psum(s, "QB", [P, 8, 512])
        made = c.sem("made")
        with nc.Block() as block:
            @block.tensor
            def _(pe):
                for n in range(B):
                    dst = QB[0:T, n // 2, (n % 2) * D:(n % 2 + 1) * D]
                    for ch in range(DC):
                        pe.matmul(dst, AT[:, ch, n * T:(n + 1) * T], wo[:, ch, :], start=(ch == 0), stop=False)
                    pe.matmul(dst, K["ones"][0:1, 0:T], bo[:, :], start=False, stop=True).then_inc(made, 1)

            @block.vector
            def _(dve):
                for n in range(8):
                    dve.wait_ge(made, 2 * n + 2)
                    dve.tensor_copy(A[:, 2 * n:2 * n + 2, :].rearrange("t b d -> t (b d)"), QB[0:T, n, :])


def dispatched_experts(c, name, X, K, a):
    nc = c.nc
    with ExitStack() as s:
        c.stage = name
        XT = c.sb(s, "XT", [P, DC, N])
        w = weights(c, s, a, "L1f_", {"gate": [P, DC, E1], "tri": [T, T], "all": [T, T], "prio": [T, E1],
                                    "slot0": [T, E1], "oob": [T, B]})
        gatew, slot = c.sb(s, "gatew", [T, B]), c.sb(s, "slot", [T, B], I32)
        features_first(c, name + "t", X, XT, K["ident"])
        route_top1(c, name + "r", X, XT, K, w, gatew, slot, a)
        scatter_tokens(c, name + "s", X, slot, a)
        Y = c.sb(s, "Y", [T, B, D])
        c.stage = name + "y"
        load(c, name + "d", [(Y[:, :, :], a["s_in"].rearrange("(b t) d -> t b d", t=T))])
        features_first(c, name + "u", Y, XT, K["ident"])
        expert_pairs(c, name + "e", XT, a)
        gather_tokens(c, name + "g", X, Y, slot, gatew, a)


def route_top1(c, name, X, XT, K, w, gatew, slot, a):
    c.stage = name
    nc = c.nc
    with ExitStack() as s:
        e, work, pick, loc, t2 = (c.sb(s, n, [T, B, E1]) for n in ("e", "work", "pick", "loc", "t2"))
        best, rank, z = (c.sb(s, n, [T, B, 1]) for n in ("best", "rank", "z"))
        valid, sf = c.sb(s, "valid", [T, B]), c.sb(s, "sf", [T, B])
        LG, CB, TB = (c.psum(s, n, [P, 512]) for n in ("LG", "CB", "TB"))
        chain, logits, shifted, exp_done, picked, counted = (c.sem(n) for n in (
            "chain", "logits", "shifted", "exp_done", "picked", "counted"))
        with nc.Block() as block:
            @block.tensor
            def _(pe):
                router_logits(pe, LG, XT, w["gate"], E1, logits)
                pe.wait_ge(picked, 1)
                ones = pick[:, :, :].rearrange("t b e -> t (b e)")
                pe.matmul(CB[0:T, 0:B * E1], w["tri"][:, :], ones, start=True, stop=True)
                pe.matmul(TB[0:T, 0:B * E1], w["all"][:, :], ones, start=True, stop=True).then_inc(counted, 1)

            @block.scalar
            def _(act):
                act.wait_ge(shifted, 1)
                act.activation(e[:, :, :], e[:, :, :], ACT.Exp).then_inc(exp_done, 1)

            @block.vector
            def _(dve):
                link = Chain(dve, chain)
                dve.wait_ge(logits, 1)
                lg = LG[0:T, 0:B * E1].rearrange("t (b e) -> t b e", b=B)
                wide = lambda t: t[:, :, :].to_broadcast([T, B, E1])
                link(dve.tensor_reduce(best[:, :, 0], lg, AX_X, ALU.max))
                dve.tensor_tensor(e[:, :, :], lg, wide(best), ALU.subtract).then_inc(shifted, 1)
                dve.wait_ge(exp_done, 1)
                link(dve.tensor_reduce(z[:, :, 0], e[:, :, :], AX_X, ALU.add))
                link(dve.reciprocal(z[:, :, :], z[:, :, :]))
                link(dve.tensor_tensor(e[:, :, :], e[:, :, :], wide(z), ALU.mult))
                first_of(link, dve, e, best, rank, pick, w["prio"][:, :], E1)
                dve.sem_inc(picked, 1)
                dve.wait_ge(counted, 1)
                link(dve.tensor_copy(loc[:, :, :], CB[0:T, 0:B * E1].rearrange("t (b e) -> t b e", b=B)))
                link(dve.tensor_copy(t2[:, :, :], TB[0:T, 0:B * E1].rearrange("t (b e) -> t b e", b=B)))
                link(dve.memset(work[:, :, :], 0.0))
                for b in range(1, B):
                    link(dve.tensor_tensor(work[:, b, :], work[:, b - 1, :], t2[:, b - 1, :], ALU.add))
                link(dve.tensor_tensor(loc[:, :, :], loc[:, :, :], work[:, :, :], ALU.add))
                link(dve.tensor_scalar(t2[:, :, :], loc[:, :, :], float(CAP), None, ALU.is_lt))
                link(dve.tensor_tensor(pick[:, :, :], pick[:, :, :], t2[:, :, :], ALU.mult))
                link(dve.tensor_reduce(valid[:, :], pick[:, :, :], AX_X, ALU.add))
                link(dve.tensor_tensor(e[:, :, :], e[:, :, :], pick[:, :, :], ALU.mult))
                link(dve.tensor_reduce(gatew[:, :], e[:, :, :], AX_X, ALU.add))
                link(dve.tensor_tensor(loc[:, :, :], loc[:, :, :],
                                       w["slot0"][:, :].unsqueeze(1).to_broadcast([T, B, E1]), ALU.add))
                link(dve.tensor_tensor(loc[:, :, :], loc[:, :, :], pick[:, :, :], ALU.mult))
                link(dve.tensor_reduce(sf[:, :], loc[:, :, :], AX_X, ALU.add))
                link(dve.tensor_scalar(valid[:, :], valid[:, :], -1.0, 1.0, ALU.mult, ALU.add))
                link(dve.tensor_tensor(valid[:, :], valid[:, :], w["oob"][:, :], ALU.mult))
                link(dve.tensor_tensor(sf[:, :], sf[:, :], valid[:, :], ALU.add))
                link(dve.tensor_copy(slot[:, :], sf[:, :]))


def scatter_tokens(c, name, X, slot, a):
    c.stage = name
    nc = c.nc
    with ExitStack() as s:
        Z = c.sb(s, "Z", [T, B, D])
        zeroed, cleared, placed = c.sem("zeroed"), c.sem("cleared"), c.sem("placed")
        with nc.Block() as block:
            @block.vector
            def _(dve):
                dve.memset(Z[:, :, :], 0.0).then_inc(zeroed, 1)

            @block.sync
            def _(sp):
                sp.wait_ge(zeroed, 1)
                sp.dma_start(a["s_in"].rearrange("(b t) d -> t b d", t=T), Z[:, :, :]).then_inc(cleared, 16)

            @block.gpsimd
            def _(pool):
                pool.wait_ge(cleared, 16)
                for b in range(B):
                    pool.indirect_dma_start(
                        out=a["s_in"], out_offset=bass.IndirectOffsetOnAxis(ap=slot[:, b:b + 1], axis=0),
                        in_=X[:, b, :], in_offset=None, bounds_check=N - 1, oob_is_err=False).then_inc(placed, 16)
                pool.wait_ge(placed, 16 * B)


def expert_pairs(c, name, XT, a):
    c.stage = name
    nc = c.nc
    FC = F1 // P
    with ExitStack() as s:
        w1 = c.sb(s, "w1", [P, 2, DC, F1])
        w2 = c.sb(s, "w2", [P, 2, FC, D])
        h = c.sb(s, "h", [P, 2, FC, CAP])
        O = c.sb(s, "O", [T, 2, 2, D])
        HB = c.psum(s, "HB", [P, 4, 512])
        OB = c.psum(s, "OB", [P, 2, 512])
        w_in = [c.sem(f"w_in{i}") for i in range(2)]
        o_out = [c.sem(f"o_out{i}") for i in range(2)]
        made, gelu_done, out_ready, o_sb = (c.sem(n) for n in ("made", "gelu_done", "out_ready", "o_sb"))
        with nc.Block() as block:
            @block.sync
            def _(sp):
                def load_expert(e, i):
                    sp.dma_start(w1[:, i, :, :], a["L1f_w1"][bass.ds(e, 1), :, :, :].rearrange("o p c f -> (o p) c f")
                                 ).then_inc(w_in[i], 16)
                    sp.dma_start(w2[:, i, :, :], a["L1f_w2"][bass.ds(e, 1), :, :, :].rearrange("o p c f -> (o p) c f")
                                 ).then_inc(w_in[i], 16)

                def store(e, i):
                    sp.wait_ge(o_sb, e + 1)
                    sp.dma_start(a["s_out"][bass.ds(e * CAP, CAP), :].rearrange("(i t) d -> t i d", t=T),
                                 O[:, i, :, :]).then_inc(o_out[i], 16)
                for i in range(2):
                    load_expert(i, i)
                with sp.Fori(0, E1 // 2 - 1) as p:
                    for i in range(2):
                        sp.wait_ge(out_ready, 2 * p + i + 1)
                        load_expert(2 * p + i + 2, i)
                        store(2 * p + i, i)
                for i in range(2):
                    store(E1 - 2 + i, i)
                for i in range(2):
                    sp.wait_ge(o_out[i], 16 * E1 // 2)

            @block.tensor
            def _(pe):
                with pe.Fori(0, E1 // 2) as p:
                    for i in range(2):
                        e = 2 * p + i
                        pe.wait_ge(w_in[i], 32 * (p + 1))
                        pe.wait_ge(gelu_done, 4 * e)
                        for k in range(FC):
                            for ch in range(DC):
                                last = pe.matmul(HB[:, k // 2, (k % 2) * CAP:(k % 2 + 1) * CAP],
                                                 w1[:, i, ch, k * P:(k + 1) * P], XT[:, ch, bass.ds(e * CAP, CAP)],
                                                 start=(ch == 0), stop=(ch == DC - 1))
                            if k % 2:
                                last.then_inc(made, 1)
                        pe.wait_ge(o_sb, e)
                        for k in range(FC):
                            pe.wait_ge(gelu_done, 4 * e + k // 2 + 1)
                            for j in range(2):
                                last = pe.matmul(OB[0:T, j, 0:D], h[:, i, k, j * T:(j + 1) * T], w2[:, i, k, :],
                                                 start=(k == 0), stop=(k == FC - 1))
                        last.then_inc(out_ready, 1)

            @block.scalar
            def _(act):
                with act.Fori(0, E1 // 2) as p:
                    for i in range(2):
                        e = 2 * p + i
                        if i == 1:
                            act.wait_ge(out_ready, e - 1)
                        else:
                            act.wait_ge(out_ready, 2 * p)
                        for k in range(FC // 2):
                            act.wait_ge(made, 4 * e + k + 1)
                            act.activation(h[:, i, 2 * k:2 * k + 2, :].rearrange("p c n -> p (c n)"),
                                           HB[:, k, 0:2 * CAP], ACT.Gelu_apprx_tanh).then_inc(gelu_done, 1)

            @block.vector
            def _(dve):
                with dve.Fori(0, E1 // 2) as p:
                    for i in range(2):
                        e = 2 * p + i
                        dve.wait_ge(out_ready, e + 1)
                        dve.wait_ge(o_out[i], 16 * p)
                        dve.tensor_copy(O[:, i, :, :], OB[0:T, :, 0:D]).then_inc(o_sb, 1)


def gather_tokens(c, name, X, Y, slot, gatew, a):
    c.stage = name
    nc = c.nc
    with ExitStack() as s:
        zeroed, came = c.sem("zeroed"), c.sem("came")
        with nc.Block() as block:
            @block.gpsimd
            def _(pool):
                pool.wait_ge(zeroed, 1)
                for b in range(B):
                    pool.indirect_dma_start(
                        out=Y[:, b, :], out_offset=None, in_=a["s_out"],
                        in_offset=bass.IndirectOffsetOnAxis(ap=slot[:, b:b + 1], axis=0),
                        bounds_check=N - 1, oob_is_err=False).then_inc(came, 16)

            @block.vector
            def _(dve):
                dve.memset(Y[:, :, :], 0.0).then_inc(zeroed, 1)
                dve.wait_ge(came, 16 * B)
                for b in range(B):
                    dve.scalar_tensor_tensor(out=X[:, b, :], in0=Y[:, b, :], scalar=gatew[:, b:b + 1],
                                             in1=X[:, b, :], op0=ALU.mult, op1=ALU.add)


def decoder(nc, a, out, stages=(1, 2, 3, 4, 5, 6)):
    with ExitStack() as ctx:
        c = Core(nc, ctx)
        c.stage = "all"
        a = dict(a)
        a["s_mask"] = nc.dram_tensor("s_mask", (B, 4, S2P), BF16, kind="Internal").ap()
        a["s_in"] = nc.dram_tensor("s_in", (N, D), F32, kind="Internal").ap()
        a["s_out"] = nc.dram_tensor("s_out", (N, D), F32, kind="Internal").ap()
        X = c.sb(ctx, "X", [T, B, D])
        K = {"ident": c.sb(ctx, "ident", [P, P]), "identb": c.sb(ctx, "identb", [P, P], BF16),
             "causal": c.sb(ctx, "causal", [T, GT], BF16), "headrows": c.sb(ctx, "headrows", [P, HH]),
             "ones": c.sb(ctx, "ones", [1, P])}
        load(c, "first", [(X[:, :, :], a["x"].rearrange("b t d -> t b d"))]
             + [(K[k][:, :], a["k_" + k]) for k in K])

        if 1 in stages:
            with ExitStack() as s:
                c.stage = "sa0"
                XT = c.sb(s, "XT", [P, DC, N])
                w = weights(c, s, a, "L0a_", {"wq": [P, DC, D], "wk": [P, DC, D], "wv": [P, DC, D], "wo": [P, 4, D],
                                            "bq": [P, DC], "bk": [P, DC], "bv": [1, D], "bo": [1, D], "nw": [P, DC]})
                features_first(c, "sa0n", X, XT, K["ident"], rms=True, weight=w["nw"])
                narrow_attention(c, "sa0a", X, XT, K, w, HD ** -0.5, bias=True)
            layernorm(c, "sa0l", X)
            c.clear_sems()
        if 2 in stages:
            cross_attention_0(c, "xa0", X, K, a)
            layernorm(c, "xa0l", X)
            c.clear_sems()
        if 3 in stages:
            c.stage = "ff0"
            with ExitStack() as s:
                A = c.sb(s, "A", [T, B, D])
                latent_and_experts(c, X, A, K, a)
            c.clear_sems()
        if 4 in stages:
            with ExitStack() as s:
                c.stage = "sa1"
                XT = c.sb(s, "XT", [P, DC, N])
                rope = c.sb(s, "rope", [P, 2, T])
                w = weights(c, s, a, "L1a_", {"wq": [P, DC, D], "wk": [P, DC, D], "wqs": [P, DC, D],
                                            "wks": [P, DC, D], "wv": [P, DC, D], "wo": [P, 4, D]},
                            [(rope[:, :, :], a["k_rope"])])
                features_first(c, "sa1n", X, XT, K["ident"])
                narrow_attention(c, "sa1a", X, XT, K, w, HD ** -0.5, rope=rope)
            layernorm(c, "sa1l", X)
            c.clear_sems()
        if 5 in stages:
            cross_attention_1(c, "xa1", X, K, a)
            layernorm(c, "xa1l", X)
            c.clear_sems()
        if 6 in stages:
            dispatched_experts(c, "ff1", X, K, a)
            layernorm(c, "ff1l", X)

        c.stage = "end"
        stored = c.sem("stored")
        with nc.Block() as block:
            @block.sync
            def _(sp):
                sp.dma_start(out.rearrange("b t d -> t b d"), X[:, :, :]).then_inc(stored, 16)
                sp.wait_ge(stored, 16)


def weights(c, s, a, prefix, shapes, more=()):
    w = {k: c.sb(s, k, shape) for k, shape in shapes.items()}
    whole = lambda t: t[tuple(slice(None) for _ in t.shape)]
    load(c, c.stage + "w", [(whole(t), a[prefix + k]) for k, t in w.items()] + list(more))
    return w


def layouts(i):
    import numpy as np
    f32, bf = np.float32, mybir.dt.np(BF16)
    i = {k: np.asarray(v) for k, v in i.items()}
    rows = lambda wt: np.ascontiguousarray(wt.reshape(-1, P, wt.shape[1]).transpose(1, 0, 2))
    cols = lambda v: np.ascontiguousarray(v.reshape(-1, P).T)
    row = lambda v: v.reshape(1, -1)
    a = {"x": i["x"]}

    def padded_heads(wt):
        o = np.zeros((4, 32, 4, wt.shape[1]), f32)
        o[:, :HD] = wt.reshape(4, 4, HD, -1).transpose(1, 2, 0, 3)
        return o.reshape(P, 4, -1)

    for k in ("wq", "wk", "wv"):
        a["L0a_" + k] = rows(i["L0_attn_" + k].T)
    a["L0a_wo"] = padded_heads(i["L0_attn_wo"].T)
    a["L0a_nw"] = cols(i["L0_attn_norm_w"])
    for k in ("bq", "bk"):
        a["L0a_" + k] = cols(i["L0_attn_" + k])
    for k in ("bv", "bo"):
        a["L0a_" + k] = row(i["L0_attn_" + k])

    def swapped(wt):
        return wt.reshape(D, H, 2, HD // 2)[:, :, ::-1].reshape(D, D)

    a["L1a_wq"], a["L1a_wk"], a["L1a_wv"] = (rows(i["L1_attn_" + k].T) for k in ("Wq", "Wk", "Wv"))
    a["L1a_wqs"], a["L1a_wks"] = (rows(swapped(i["L1_attn_" + k].T)) for k in ("Wq", "Wk"))
    a["L1a_wo"] = padded_heads(i["L1_attn_Wo"].T)

    a["k_ident"], a["k_identb"] = np.eye(P, dtype=f32), np.eye(P, dtype=bf)
    q, k = np.arange(T)[:, None], np.arange(T)[None, :]
    a["k_causal"] = np.tile(np.where(k <= q, 0.0, NEG), (1, GB)).astype(bf)
    a["k_headrows"] = (np.arange(P)[:, None] // HD == np.arange(HH)[None, :]).astype(f32)
    a["k_ones"] = np.ones((1, P), f32)
    inv = (1.0 / 10000.0 ** (np.arange(0, HD, 2, dtype=f32) / HD)).astype(f32)
    freqs = np.arange(T, dtype=f32)[None, :] * inv[:, None]
    sin, cos = np.sin(freqs), np.cos(freqs)
    head = np.stack([np.concatenate([sin, sin]), np.concatenate([-cos, cos])], 1)
    a["k_rope"] = np.tile(head, (HH, 1, 1)).astype(f32)
    more_layouts(i, a, rows, cols, row, padded_heads)
    return a


def more_layouts(i, a, rows, cols, row, padded_heads):
    import numpy as np
    f32, bf = np.float32, mybir.dt.np(BF16)
    ctx = np.zeros((B, S2P, D), f32)
    ctx[:, :S2] = i["ctx_2048"]
    a["ctxT0"] = ctx.reshape(B, S2P, 2, 2, 4, HD).transpose(0, 2, 3, 5, 4, 1).reshape(B, 2, P, S2P)
    v = np.zeros((B, NQ, KB, NKB, 4, HD + 1), f32)
    v[..., :HD] = ctx.reshape(B, NKB, KB, NQ, 4, HD).transpose(0, 3, 2, 1, 4, 5)
    v[..., HD] = 1.0
    a["ctxV0"] = v.reshape(B, NQ, KB, -1)
    qw = i["L0_ffn_q_w"].reshape(H, P + 64, D)[:, :P].reshape(H * P, D)
    kv = i["L0_ffn_kv_w"]
    a["L0l_wq"], a["L0l_wk"], a["L0l_wv"] = rows(qw.T), rows(kv[:H * P].T), rows(kv[H * P:2 * H * P].T)
    a["L0l_wo"] = rows(i["L0_ffn_o_w"].T)
    a["L0l_nw"], a["L0m_nw"] = cols(i["L0_ffn_ln1_w"]), cols(i["L0_ffn_ln2_w"])
    a["L0m_gate"] = rows(i["L0_ffn_gate_w"].T)
    w1 = i["L0_ffn_w1"]
    a["L0m_wg"], a["L0m_wu"] = (rows(x.reshape(E0 * I0, D).T) for x in (w1[:, :I0], w1[:, I0:]))
    a["L0m_wd"] = rows(i["L0_ffn_w2"].transpose(0, 2, 1).reshape(E0 * I0, D))
    a["L0m_sg"], a["L0m_su"] = (rows(x.T) for x in (i["L0_ffn_sh_gu_w"][:SHI], i["L0_ffn_sh_gu_w"][SHI:]))
    sd = np.zeros((3 * P, D), f32)
    sd[:SHI] = i["L0_ffn_sh_down_w"].T
    a["L0m_sd"] = rows(sd)
    a["L0m_prio"] = np.tile(np.arange(E0, 0, -1, dtype=f32), (T, 1))
    r = np.arange(96)[:, None]
    a["k_experts"] = ((r % 32 < E0) & (r % 32 == np.arange(E0 * I0)[None, :] // I0)).astype(bf)
    a["ctxT1"] = ctx.reshape(B, S2P, DC, P).transpose(0, 3, 2, 1)
    a["L1x_wq"], a["L1x_wv"], a["L1x_wo"] = (rows(i["L1_xattn_" + k].T) for k in ("Wq", "Wv", "Wo"))
    quads = lambda v: v.reshape(2, 2, 4, HD, *v.shape[1:]).swapaxes(2, 3).reshape(v.shape)
    a["L1x_wk"] = rows(quads(i["L1_xattn_Wk"]).T)
    a["L1x_bk"] = cols(quads(i["L1_xattn_bk"]))
    for k in ("bq", "bv", "bo"):
        a["L1x_" + k] = row(i["L1_xattn_" + k])
    a["L1x_gamma"], a["L1x_beta"] = i["L1_xattn_ln_gamma"], i["L1_xattn_ln_beta"]
    a["L1x_rs"] = np.tile(i["L1_xattn_residual_scale"].reshape(1, 1), (T, 1))
    a["mask"] = np.zeros((B, S2P), np.int32)
    a["mask"][:, :S2] = i["mask_BxS2_ik0"]
    a["L1f_gate"] = rows(i["L1_ffn_w_gate"])
    a["L1f_w1"] = i["L1_ffn_w1"].reshape(E1, DC, P, F1).transpose(0, 2, 1, 3)
    a["L1f_w2"] = i["L1_ffn_w2"].reshape(E1, F1 // P, P, D).transpose(0, 2, 1, 3)
    t = np.arange(T)
    a["L1f_tri"] = (t[:, None] < t[None, :]).astype(f32)
    a["L1f_all"] = np.ones((T, T), f32)
    a["L1f_prio"] = np.tile(np.arange(E1, 0, -1, dtype=f32), (T, 1))
    a["L1f_slot0"] = np.tile(np.arange(E1, dtype=f32) * CAP, (T, 1))
    a["L1f_oob"] = (N + np.arange(B)[None, :] * T + t[:, None]).astype(f32)
    key, q = np.arange(MASK0, S2P)[None, :], np.arange(T)[:, None]
    a["k_mask0"] = np.where(key <= q + S2 - T, 0.0, NEG).astype(bf)


def kernel(**inputs):
    import numpy as np
    import concourse.bacc as bacc
    from concourse.bass_utils import run_bass_kernel_spmd

    nc = bacc.Bacc("TRN2", target_bir_lowering=False, num_devices=1)
    arrays = {f"in_{k}": np.ascontiguousarray(v) for k, v in layouts(inputs).items()}
    a = {k[3:]: nc.dram_tensor(k, v.shape, mybir.dt.from_np(v.dtype), kind="ExternalInput").ap()
         for k, v in arrays.items()}
    out = nc.dram_tensor("out_x", (B, T, D), F32, kind="ExternalOutput").ap()
    decoder(nc, a, out)
    r = run_bass_kernel_spmd(nc, [arrays], core_ids=[0])
    return r.results[0]["out_x"]
```

```python
from contextlib import ExitStack

import concourse.bass as bass
from concourse import mybir

F32 = mybir.dt.float32
BF16 = mybir.dt.bfloat16
I32 = mybir.dt.int32
ALU = mybir.AluOpType
ACT = mybir.ActivationFunctionType
AX_X = mybir.AxisListType.X

P = 128
B, T, D = 16, 100, 256
DC = D // P
H, HD = 16, 16
HH = 8
GB = 4
G = B // GB
GT = GB * T
N = B * T
S2 = 1444
KB, NKB = P, 12
S2P = KB * NKB
LASTKB = S2 - KB * (NKB - 1)
CUTS = (0, 482, 964, S2)
MASK0 = S2P - 2 * KB
PARTS = 3
STK = 6 * HD
E0, TOPK, I0 = 16, 4, 176
EC = E0 * I0 // P
SHI = 2 * I0
E1, F1 = 8, 1024
CAP = N // E1
NEG = -1.0e30


class Chain:

    def __init__(self, eng, sem):
        self.eng, self.sem, self.base, self.n = eng, sem, 0, 0

    def __call__(self, ins):
        self.n += 1
        ins.then_inc(self.sem, 1)
        self.eng.wait_ge(self.sem, self.base + self.n)

    def loop(self, i, per):
        self.start = self.n if isinstance(self.base, int) else self.start
        self.base, self.n, self.per = self.start + i * per, 0, per

    def end(self, steps):
        assert self.n == self.per, (self.n, self.per)
        self.base, self.n = 0, self.start + steps * self.per


def fixed(eng, value, name):
    reg = eng.alloc_register(name)
    eng.reg_mov(reg, value)
    return eng.snap(reg)


class Core:
    def __init__(self, nc, ctx):
        self.nc, self.ctx, self.stage = nc, ctx, ""
        self.sems = []

    def sem(self, name):
        self.sems.append(self.nc.alloc_semaphore(name=f"{self.stage}_{name}"))
        return self.sems[-1]

    def clear_sems(self):
        with self.nc.Block() as block:
            @block.sync
            def _(sp):
                for s in self.sems:
                    sp.sem_clear(s)
        for s in self.sems:
            self.nc.release_semaphore(s)
        self.sems = []

    def psum(self, ctx, name, shape, dt=F32):
        return ctx.enter_context(self.nc.psum_tensor(f"{self.stage}_{name}", shape, dt))

    def sb(self, ctx, name, shape, dt=F32):
        return ctx.enter_context(self.nc.sbuf_tensor(f"{self.stage}_{name}", shape, dt))


def statistics(dve, link, src, st, mv):
    for b in range(B):
        last = dve.bn_stats(st[:, b, :], src[:, b, :])
    link(last)
    for b in range(B):
        last = dve.bn_aggr(mv[:, b, :], st[:, b, :])
    link(last)


def layernorm(c, name, X, gamma=None, beta=None, into=None, eps=1e-5, scale=None):
    c.stage = name
    nc = c.nc
    with ExitStack() as s:
        st, mv, rstd = (c.sb(s, n, [T, B, k]) for n, k in (("st", 6), ("mv", 2), ("rstd", 1)))
        chain, have_var, have_rstd = c.sem("chain"), c.sem("have_var"), c.sem("have_rstd")
        with nc.Block() as block:
            @block.vector
            def _(dve):
                link = Chain(dve, chain)
                if scale is not None:
                    link(dve.tensor_scalar(scale, scale, 0.0, 0.3, ALU.max, ALU.min))
                    link(dve.tensor_scalar(X[:, :, :], X[:, :, :], scale, None, ALU.mult))
                statistics(dve, link, X, st, mv)
                dve.tensor_scalar(rstd[:, :, :], mv[:, :, 1:2], eps, None, ALU.add).then_inc(have_var, 1)
                dve.wait_ge(have_rstd, 1)
                link(dve.reciprocal(rstd[:, :, :], rstd[:, :, :]))
                for b in range(B):
                    last = dve.tensor_scalar(X[:, b, :], X[:, b, :], mv[:, b, 0:1], rstd[:, b, :],
                                             ALU.subtract, ALU.mult)
                link(last)
                if gamma is not None:
                    link(dve.tensor_tensor(X[:, :, :], X[:, :, :], over_seqs(gamma), ALU.mult))
                    link(dve.tensor_tensor(X[:, :, :], X[:, :, :], over_seqs(beta), ALU.add))
                if into is not None:
                    link(dve.tensor_tensor(into[:, :, :], into[:, :, :], X[:, :, :], ALU.add))

            @block.scalar
            def _(act):
                act.wait_ge(have_var, 1)
                act.activation(rstd[:, :, :], rstd[:, :, :], ACT.Sqrt).then_inc(have_rstd, 1)


def over_seqs(row):
    return row.unsqueeze(1).to_broadcast([T, B, D])


def features_first(c, name, X, XT, ident, rms=False, weight=None, copy=None):
    c.stage = name
    nc = c.nc
    with ExitStack() as s:
        st, mv, ms = (c.sb(s, n, [T, B, k]) for n, k in (("st", 6), ("mv", 2), ("ms", 1)))
        xn = c.sb(s, "xn", [T, B, D]) if rms else X
        banks = c.psum(s, "banks", [P, 8, 512])
        chain, have_ms, have_rms, have_xn = (c.sem(n) for n in ("chain", "have_ms", "have_rms", "have_xn"))
        turned = c.sem("turned")
        with nc.Block() as block:
            if copy is not None:
                @block.gpsimd
                def _(pool):
                    pool.tensor_copy(copy[:, :, :], X[:, :, :])

            if rms:
                @block.vector
                def _(dve):
                    link = Chain(dve, chain)
                    statistics(dve, link, X, st, mv)
                    link(dve.tensor_tensor(ms[:, :, :], mv[:, :, 0:1], mv[:, :, 0:1], ALU.mult))
                    link(dve.tensor_tensor(ms[:, :, :], ms[:, :, :], mv[:, :, 1:2], ALU.add))
                    dve.tensor_scalar(ms[:, :, :], ms[:, :, :], 1e-6, None, ALU.add).then_inc(have_ms, 1)
                    dve.wait_ge(have_rms, 1)
                    link(dve.reciprocal(ms[:, :, :], ms[:, :, :]))
                    for b in range(B):
                        dve.tensor_scalar(xn[:, b, :], X[:, b, :], ms[:, b, :], None, ALU.mult).then_inc(have_xn, 1)

            @block.tensor
            def _(pe):
                for g in range(G):
                    if rms:
                        pe.wait_ge(have_xn, GB * (g + 1))
                    for ch in range(DC):
                        for j in range(GB):
                            last = pe.transpose(banks[:, g * DC + ch, j * T:(j + 1) * T],
                                                xn[:, g * GB + j, ch * P:(ch + 1) * P], ident[0:T, 0:T])
                        last.then_inc(turned, 1)

            @block.scalar
            def _(act):
                if rms:
                    act.wait_ge(have_ms, 1)
                    act.activation(ms[:, :, :], ms[:, :, :], ACT.Sqrt).then_inc(have_rms, 1)
                for g in range(G):
                    for ch in range(DC):
                        act.wait_ge(turned, g * DC + ch + 1)
                        act.activation(XT[:, ch, g * GT:(g + 1) * GT], banks[:, g * DC + ch, 0:GT], ACT.Copy,
                                       scale=1.0 if weight is None else weight[:, ch:ch + 1])


def load(c, name, pairs):
    c.stage = name
    landed = c.sem("landed")
    with c.nc.Block() as block:
        @block.sync
        def _(sp):
            for dst, src in pairs[0::2]:
                sp.dma_start(dst, src).then_inc(landed, 16)
            sp.wait_ge(landed, 16 * len(pairs))

        @block.scalar
        def _(act):
            for dst, src in pairs[1::2]:
                act.dma_start(dst, src).then_inc(landed, 16)


def start_load(c, name, pairs):
    c.stage = name
    landed = c.sem("landed")
    with c.nc.Block() as block:
        @block.sync
        def _(sp):
            for dst, src in pairs:
                sp.dma_start(dst, src).then_inc(landed, 16)
    return landed, 16 * len(pairs)


def end_load(c, started):
    with c.nc.Block() as block:
        @block.sync
        def _(sp):
            sp.wait_ge(*started)


def narrow_attention(c, name, X, XT, K, w, scale, rope=None, bias=None):
    c.stage = name
    nc = c.nc
    with ExitStack() as s:
        xg = c.sb(s, "xg", [P, DC, GT])
        qT, kT = c.sb(s, "qT", [P, DC, GT]), c.sb(s, "kT", [P, DC, GT])
        rot = c.sb(s, "rot", [P, 4, GT]) if rope else None
        kD = c.sb(s, "kD", [P, 2, DC, HH, T])
        V = c.sb(s, "V", [T, GB, H, 32])
        Pm = c.sb(s, "Pm", [T, 2, H, T])
        mx, sm = c.sb(s, "mx", [T, H, 1]), c.sb(s, "sm", [T, H, 1])
        PT = c.sb(s, "PT", [T, H, T])
        OT = c.sb(s, "OT", [P, 4, T])
        SB, TB = c.psum(s, "SB", [P, 4, 512]), c.psum(s, "TB", [P, 4, 512])
        (chain, xg_ready, zeroed, proj_ready, qk_done, v_ready, v_taken, spread, scores_ready,
         shifted, exp_done, sums, scaled, turned, turned_sb, mixed, mixed_sb, out_ready, out_added) = (
            c.sem(n) for n in (
                "chain", "xg_ready", "zeroed", "proj_ready", "qk_done", "v_ready", "v_taken",
                "spread", "scores_ready", "shifted", "exp_done", "sums", "scaled", "turned", "turned_sb",
                "mixed", "mixed_sb", "out_ready", "out_added"))
        banks_read, turned_sb2 = c.sem("banks_read"), c.sem("turned_sb2")
        Sv = SB[0:T, :, 0:GT].rearrange("q j (i k) -> q j i k", k=T)
        NPROJ = 8 if rope else 4
        QK = 1 if rope else 4

        with nc.Block() as block:
            @block.gpsimd
            def _(pool):
                pool.memset(V[:, :, :, :], 0.0).then_inc(zeroed, 1)

                def spread_keys(g, u):
                    if u == 0:
                        pool.wait_ge(qk_done, QK * (g + 1))
                    if u >= 2:
                        pool.wait_ge(scores_ready, g * GB + u - 1)
                    for m in range(DC):
                        pool.tensor_tensor(kD[:, u % 2, m, :, :],
                                           kT[:, m, u * T:(u + 1) * T].unsqueeze(1).to_broadcast([P, HH, T]),
                                           K["headrows"][:, :].unsqueeze(2).to_broadcast([P, HH, T]),
                                           ALU.mult).then_inc(spread, 1)

                with pool.Fori(0, G) as g:
                    spread_keys(g, 0)
                    for u in range(GB):
                        if u + 1 < GB:
                            spread_keys(g, u + 1)
                        pool.wait_ge(sums, g * GB + u + 1)
                        for h in range(0, H, HH):
                            pool.tensor_tensor(Pm[:, u % 2, h:h + HH, :], Pm[:, u % 2, h:h + HH, :],
                                               sm[:, h:h + HH, :].to_broadcast([T, HH, T]),
                                               ALU.mult).then_inc(scaled, 1)

            @block.tensor
            def _(pe):
                def project(g):
                    pe.wait_ge(xg_ready, g + 1)
                    pe.wait_ge(shifted, g * GB)
                    for i, mats in enumerate((("wq", "wqs"), ("wk", "wks")) if rope else (("wq", "wk"),)):
                        if i == 1:
                            pe.wait_ge(banks_read, 2 * g + 1)
                        for j in range(4):
                            for ch in range(DC):
                                m = j % 2
                                last = pe.matmul(SB[:, j, 0:GT], w[mats[j // 2]][:, ch, m * P:(m + 1) * P],
                                                 xg[:, ch, :], start=(ch == 0), stop=(ch == DC - 1))
                            last.then_inc(proj_ready, 1)

                def values(g):
                    pe.wait_ge(out_added, g * GB)
                    for b in range(GB):
                        for ch in range(DC):
                            last = pe.matmul(TB[0:T, b, 0:D], xg[:, ch, b * T:(b + 1) * T], w["wv"][:, ch, :],
                                             start=(ch == 0), stop=(ch == DC - 1 and not bias))
                        if bias:
                            last = pe.matmul(TB[0:T, b, 0:D], K["ones"][0:1, 0:T], w["bv"][:, :],
                                             start=False, stop=True)
                        last.then_inc(v_ready, 1)

                def scores(g, u):
                    pe.wait_ge(shifted, g * GB + u)
                    pe.wait_ge(qk_done, QK * (g + 1))
                    pe.wait_ge(spread, 2 * (g * GB + u + 1))
                    for j in range(4):
                        pe.matmul(SB[0:T, j, 0:GT], K["identb"][0:T, 0:T], K["causal"][:, :],
                                  start=True, stop=False, skip_group_check=True)
                        h = 4 * (j % 2)
                        last = pe.matmul(SB[0:T, j, 0:GT], qT[:, j // 2, u * T:(u + 1) * T],
                                         kD[:, u % 2, j // 2, h:h + 4, :].rearrange("p h k -> p (h k)"),
                                         start=False, stop=True, skip_group_check=True)
                    last.then_inc(scores_ready, 1)

                def mix(g, u):
                    U = g * GB + u
                    pe.wait_ge(out_added, U)
                    pe.wait_ge(v_taken, 4 * (g + 1))
                    for j in range(4):
                        if j % 2 == 0:
                            pe.wait_ge(scaled, 2 * U + j // 2 + 1)
                        for i in range(4):
                            last = pe.transpose(TB[0:T, j, i * T:(i + 1) * T], Pm[:, u % 2, 4 * j + i, :],
                                                K["ident"][0:T, 0:T])
                        last.then_inc(turned, 1)
                    pe.wait_ge(turned_sb, U + 1)
                    for q in range(4):
                        if q == 2:
                            pe.wait_ge(turned_sb2, U + 1)
                        for j in range(4):
                            last = pe.matmul(TB[32 * j:32 * j + 32, 0, q * T:(q + 1) * T], V[:, u, 4 * q + j, :],
                                             PT[:, 4 * q + j, :], start=(q == 0), stop=True,
                                             skip_group_check=True)
                    last.then_inc(mixed, 1)
                    pe.wait_ge(mixed_sb, U + 1)
                    for q in range(4):
                        last = pe.matmul(TB[0:T, 1, 0:D], OT[:, q, :], w["wo"][:, q, :],
                                         start=(q == 0), stop=(q == 3 and not bias))
                    if bias:
                        last = pe.matmul(TB[0:T, 1, 0:D], K["ones"][0:1, 0:T], w["bo"][:, :],
                                         start=False, stop=True)
                    last.then_inc(out_ready, 1)

                def body(g, final):
                    values(g)
                    for u in range(GB):
                        if u + 1 < GB:
                            scores(g, u + 1)
                        elif not final:
                            project(g + 1)
                        mix(g, u)
                    if not final:
                        scores(g + 1, 0)

                project(0)
                scores(0, 0)
                with pe.Fori(0, G - 1) as g:
                    body(g, False)
                body(G - 1, True)

            @block.scalar
            def _(act):
                def exponentials(g, u):
                    act.wait_ge(shifted, g * GB + u + 1)
                    act.activation(Pm[:, u % 2, :, :], Pm[:, u % 2, :, :], ACT.Exp,
                                   scale=scale).then_inc(exp_done, 1)

                act.wait_ge(zeroed, 1)
                def take_group(g):
                    act.activation(xg[:, :, :], XT[:, :, bass.ds(g * GT, GT)], ACT.Copy).then_inc(xg_ready, 1)

                def take_projections(g):
                    if not rope:
                        act.wait_ge(scores_ready, g * GB)
                        act.wait_ge(spread, 2 * g * GB)
                        for j in range(4):
                            act.wait_ge(proj_ready, 4 * g + j + 1)
                            act.activation((qT if j < 2 else kT)[:, j % 2, :], SB[:, j, 0:GT], ACT.Identity,
                                           bias=w["bq" if j < 2 else "bk"][:, j % 2:j % 2 + 1]).then_inc(qk_done, 1)

                def body(g, final):
                    act.wait_ge(mixed, g * GB)
                    for b in range(GB):
                        act.wait_ge(v_ready, 4 * g + b + 1)
                        act.activation(V[:, b, :, 0:HD], TB[0:T, b, 0:D].rearrange("t (h d) -> t h d", d=HD),
                                       ACT.Copy).then_inc(v_taken, 1)
                    exponentials(g, 0)
                    if not final:
                        take_group(g + 1)
                    for u in range(GB):
                        U = g * GB + u
                        if u + 1 == GB and not final:
                            take_projections(g + 1)
                        act.wait_ge(turned, 4 * U + 2)
                        act.wait_ge(mixed, U)
                        act.activation(PT[:, 0:8, :].rearrange("k (j i) q -> k j (i q)", j=2),
                                       TB[0:T, 0:2, 0:GT], ACT.Copy).then_inc(turned_sb, 1)
                        act.wait_ge(mixed, U + 1)
                        act.wait_ge(out_ready, U)
                        act.activation(OT[:, :, :].rearrange("p q t -> p (q t)"), TB[:, 0, 0:GT],
                                       ACT.Copy).then_inc(mixed_sb, 1)
                        if u + 1 < GB:
                            exponentials(g, u + 1)

                take_group(0)
                take_projections(0)
                with act.Fori(0, G - 1) as g:
                    body(g, False)
                body(G - 1, True)

            @block.vector
            def _(dve):
                link = Chain(dve, chain)

                def rotate(g):
                    dve.wait_ge(scores_ready, g * GB)
                    dve.wait_ge(spread, 2 * g * GB)
                    tab = [rope[:, t, :].unsqueeze(1).to_broadcast([P, GB, T]) for t in range(2)]
                    cut = lambda a: a.rearrange("p (b t) -> p b t", t=T)
                    for i, dst in enumerate((qT, kT)):
                        dve.wait_ge(proj_ready, g * NPROJ + 4 * (i + 1))
                        for m in range(2):
                            dve.tensor_tensor(cut(dst[:, m, :]), cut(SB[:, m, 0:GT]), tab[0], ALU.mult)
                            last = dve.tensor_tensor(cut(rot[:, 2 * i + m, :]), cut(SB[:, 2 + m, 0:GT]), tab[1],
                                                     ALU.mult)
                        last.then_inc(banks_read, 1)
                        dve.wait_ge(banks_read, 2 * g + i + 1)
                        last = dve.tensor_tensor(dst[:, :, :], dst[:, :, :], rot[:, 2 * i:2 * i + 2, :], ALU.add)
                    last.then_inc(qk_done, 1)

                def maxima(g, u):
                    dve.wait_ge(scores_ready, g * GB + u + 1)
                    link(dve.tensor_reduce(mx[:, :, :].rearrange("q (j i) o -> q j (i o)", j=4), Sv, AX_X, ALU.max))

                def shift(g, u):
                    dve.tensor_tensor(Pm[:, u % 2, :, :].rearrange("q (j i) k -> q j i k", j=4), Sv,
                                      mx[:, :, :].rearrange("q (j i) o -> q j i o", j=4).to_broadcast([T, 4, 4, T]),
                                      ALU.subtract).then_inc(shifted, 1)

                def add_up(g, u):
                    U = g * GB + u
                    dve.wait_ge(exp_done, U + 1)
                    dve.wait_ge(scaled, 2 * U)
                    link(dve.tensor_reduce(sm[:, :, :].rearrange("q h o -> q (h o)"), Pm[:, u % 2, :, :],
                                           AX_X, ALU.add))
                    dve.reciprocal(sm[:, :, :], sm[:, :, :]).then_inc(sums, 1)

                def body(g, final):
                    maxima(g, 0)
                    shift(g, 0)
                    add_up(g, 0)
                    for u in range(GB):
                        U = g * GB + u
                        if u + 1 < GB:
                            maxima(g, u + 1)
                        elif rope and not final:
                            rotate(g + 1)
                        dve.wait_ge(turned, 4 * U + 4)
                        dve.wait_ge(mixed, U)
                        dve.tensor_copy(PT[:, 8:16, :].rearrange("k (j i) q -> k j (i q)", j=2),
                                        TB[0:T, 2:4, 0:GT]).then_inc(turned_sb2, 1)
                        if u + 1 < GB:
                            shift(g, u + 1)
                            add_up(g, u + 1)
                        dve.wait_ge(out_ready, U + 1)
                        xb = X[:, bass.ds(g * GB + u, 1), :]
                        dve.tensor_tensor(xb, xb, TB[0:T, 1:2, 0:D], ALU.add).then_inc(out_added, 1)

                if rope:
                    rotate(0)
                with dve.Fori(0, G - 1) as g:
                    link.loop(g, 2 * GB)
                    body(g, False)
                link.end(G - 1)
                body(G - 1, True)


def latent_attention(c, name, A, XT, K, w, scale):
    c.stage = name
    nc = c.nc
    with ExitStack() as s:
        xg = c.sb(s, "xg", [P, DC, GT])
        qT, kT = c.sb(s, "qT", [P, 4, GT]), c.sb(s, "kT", [P, 4, GT])
        V = c.sb(s, "V", [T, 2, GB, 4, P])
        Pm = c.sb(s, "Pm", [T, 16, T])
        mx, sm = c.sb(s, "mx", [T, 16, 1]), c.sb(s, "sm", [T, 16, 1])
        PT = c.sb(s, "PT", [T, 16, T])
        OT = c.sb(s, "OT", [P, 4, GT])
        SB, TB = c.psum(s, "SB", [P, 4, 512]), c.psum(s, "TB", [P, 4, 512])
        (chain, xg_ready, proj_ready, qk_done, v_ready, v_taken, scores_ready, shifted, exp_done,
         sums, scaled, turned, turned_sb, mixed, mixed_sb, out_ready, out_added) = (
            c.sem(n) for n in (
                "chain", "xg_ready", "proj_ready", "qk_done", "v_ready", "v_taken",
                "scores_ready", "shifted", "exp_done", "sums", "scaled", "turned", "turned_sb", "mixed",
                "mixed_sb", "out_ready", "out_added"))
        Sv = SB[0:T, :, 0:GT].rearrange("q j (i k) -> q j i k", k=T)
        HQ = 4

        with nc.Block() as block:
            @block.gpsimd
            def _(pool):
                with pool.Fori(0, G) as g:
                    for u in range(HQ):
                        pool.wait_ge(sums, g * HQ + u + 1)
                        pool.tensor_tensor(Pm[:, :, :], Pm[:, :, :], sm[:, :, :].to_broadcast([T, 16, T]),
                                           ALU.mult).then_inc(scaled, 1)

            @block.tensor
            def _(pe):
                def project(g, u, pieces):
                    U = g * HQ + u
                    if 0 in pieces:
                        pe.wait_ge(shifted, U)
                    for n in pieces:
                        if n >= 4:
                            pe.wait_ge(qk_done, 8 * U + n - 3)
                        wm = w["wq" if n < 4 else "wk"]
                        h = 4 * u + n % 4
                        for ch in range(DC):
                            last = pe.matmul(SB[:, n % 4, 0:GT], wm[:, ch, h * P:(h + 1) * P], xg[:, ch, :],
                                             start=(ch == 0), stop=(ch == DC - 1))
                        last.then_inc(proj_ready, 1)

                def values(g, u, before):
                    pe.wait_ge(xg_ready, g + 1)
                    if before is not None:
                        pe.wait_ge(out_added, before)
                    for b in range(GB):
                        for ch in range(DC):
                            last = pe.matmul(TB[0:T, b, :], xg[:, ch, b * T:(b + 1) * T],
                                             w["wv"][:, ch, 4 * u * P:4 * (u + 1) * P],
                                             start=(ch == 0), stop=(ch == DC - 1))
                        last.then_inc(v_ready, 1)

                def scores(g, u):
                    U = g * HQ + u
                    pe.wait_ge(qk_done, 8 * (U + 1))
                    for j in range(4):
                        pe.matmul(SB[0:T, j, 0:GT], K["identb"][0:T, 0:T], K["causal"][:, :],
                                  start=True, stop=False, skip_group_check=True)
                        for b in range(GB):
                            t = slice(b * T, (b + 1) * T)
                            last = pe.matmul(SB[0:T, j, t], qT[:, j, t], kT[:, j, t], start=False,
                                             stop=(b == GB - 1), skip_group_check=True)
                    last.then_inc(scores_ready, 1)

                def turn(g, u, taken):
                    U = g * HQ + u
                    pe.wait_ge(scaled, U + 1)
                    pe.wait_ge(v_taken, taken)
                    for j in range(4):
                        for b in range(GB):
                            last = pe.transpose(TB[0:T, j, b * T:(b + 1) * T], Pm[:, 4 * j + b, :],
                                                K["ident"][0:T, 0:T])
                        last.then_inc(turned, 1)

                def mix(g, u):
                    U = g * HQ + u
                    pe.wait_ge(turned_sb, 2 * (U + 1))
                    for j in range(4):
                        for b in range(GB):
                            last = pe.matmul(TB[:, j, b * T:(b + 1) * T], V[:, u % 2, b, j, :], PT[:, 4 * j + b, :],
                                             start=True, stop=True)
                        last.then_inc(mixed, 1)

                def project_out(g, u):
                    U = g * HQ + u
                    pe.wait_ge(mixed_sb, 4 * (U + 1))
                    for b in range(GB):
                        for j in range(4):
                            last = pe.matmul(TB[0:T, b, 0:D], OT[:, j, b * T:(b + 1) * T],
                                             w["wo"][:, 4 * u + j, :], start=(j == 0), stop=(j == 3))
                    last.then_inc(out_ready, 1)

                def body(g, final):
                    for u in range(HQ):
                        U = g * HQ + u
                        following = (g, u + 1) if u + 1 < HQ else (g + 1, 0)
                        more = not (final and u + 1 == HQ)
                        if more:
                            values(*following, U)
                            project(*following, range(5))
                        turn(g, u, 4 * (U + 2) if more else 4 * (U + 1))
                        if more:
                            project(*following, (5, 6))
                        mix(g, u)
                        if more:
                            project(*following, (7,))
                        project_out(g, u)
                        if more:
                            scores(*following)

                values(0, 0, None)
                project(0, 0, range(8))
                scores(0, 0)
                with pe.Fori(0, G - 1) as g:
                    body(g, False)
                body(G - 1, True)

            @block.scalar
            def _(act):
                def take_group(g):
                    tokens = bass.ds(g * GT, GT)
                    act.activation(xg[:, :, :], XT[:, :, tokens], ACT.Copy).then_inc(xg_ready, 1)

                def take_projections(g, u, pieces):
                    U = g * HQ + u
                    if 0 in pieces:
                        act.wait_ge(scores_ready, U)
                    for n in pieces:
                        act.wait_ge(proj_ready, 8 * U + n + 1)
                        act.activation((qT if n < 4 else kT)[:, n % 4, :], SB[:, n % 4, 0:GT],
                                       ACT.Copy).then_inc(qk_done, 1)

                def take_values(g, u, blocks, mixed_before=None):
                    U = g * HQ + u
                    if mixed_before is not None:
                        act.wait_ge(mixed, mixed_before)
                    for b in blocks:
                        act.wait_ge(v_ready, 4 * U + b + 1)
                        act.activation(V[:, u % 2, b, :, :].rearrange("t h d -> t (h d)"), TB[0:T, b, :],
                                       ACT.Copy).then_inc(v_taken, 1)

                def body(g, final):
                    for u in range(HQ):
                        U = g * HQ + u
                        following = (g, u + 1) if u + 1 < HQ else (g + 1, 0)
                        more = not (final and u + 1 == HQ)
                        if more:
                            take_values(*following, (0, 1), 4 * U)
                        act.wait_ge(shifted, U + 1)
                        act.activation(Pm[:, :, :], Pm[:, :, :], ACT.Exp, scale=scale).then_inc(exp_done, 1)
                        if more:
                            take_values(*following, (2, 3))
                            take_projections(*following, range(5))
                        act.wait_ge(turned, 4 * U + 2)
                        act.wait_ge(mixed, 4 * U)
                        act.activation(PT[:, 0:8, :].rearrange("k (j i) q -> k j (i q)", j=2),
                                       TB[0:T, 0:2, 0:GT], ACT.Copy).then_inc(turned_sb, 1)
                        if more:
                            take_projections(*following, (5, 6))
                        for j in range(4):
                            act.wait_ge(mixed, 4 * U + j + 1)
                            if j == 0:
                                act.wait_ge(out_ready, U)
                            act.activation(OT[:, j, :], TB[:, j, 0:GT], ACT.Copy).then_inc(mixed_sb, 1)
                        if more:
                            take_projections(*following, (7,))
                        if u == HQ - 2 and not final:
                            take_group(g + 1)

                take_group(0)
                take_values(0, 0, range(GB))
                take_projections(0, 0, range(8))
                with act.Fori(0, G - 1) as g:
                    body(g, False)
                body(G - 1, True)

            @block.vector
            def _(dve):
                link = Chain(dve, chain)
                with dve.Fori(0, G) as g:
                    link.loop(g, 2 * HQ)
                    for u in range(HQ):
                        U = g * HQ + u
                        dve.wait_ge(scores_ready, U + 1)
                        link(dve.tensor_reduce(mx[:, :, :].rearrange("q (j i) o -> q j (i o)", j=4), Sv,
                                               AX_X, ALU.max))
                        dve.tensor_tensor(Pm[:, :, :].rearrange("q (j i) k -> q j i k", j=4), Sv,
                                          mx[:, :, :].rearrange("q (j i) o -> q j i o", j=4)
                                          .to_broadcast([T, 4, 4, T]), ALU.subtract).then_inc(shifted, 1)
                        dve.wait_ge(exp_done, U + 1)
                        link(dve.tensor_reduce(sm[:, :, :].rearrange("q h o -> q (h o)"), Pm[:, :, :],
                                               AX_X, ALU.add))
                        dve.reciprocal(sm[:, :, :], sm[:, :, :]).then_inc(sums, 1)
                        dve.wait_ge(turned, 4 * U + 4)
                        dve.wait_ge(mixed, 4 * U)
                        dve.tensor_copy(PT[:, 8:16, :].rearrange("k (j i) q -> k j (i q)", j=2),
                                        TB[0:T, 2:4, 0:GT]).then_inc(turned_sb, 1)
                        dve.wait_ge(out_ready, U + 1)
                        ag = A[:, bass.ds(g * GB, GB), :]
                        dve.tensor_tensor(ag, ag, TB[0:T, 0:GB, 0:D], ALU.add).then_inc(out_added, 1)
                        dve.wait_ge(out_added, U + 1)
                link.end(G)



NQ = 4
ROWS = STK + PARTS
SETS = 8
HKB = NKB // 2
CHUNKS_AT = ((6,), (7, 8), (9, 10), (11,), (0,), (1, 2), (3, 4), (5,))


def quad_rows(kp, part, q):
    return kp[64 * (q % 2):64 * (q % 2) + 64, q // 2, part, :]


def cross_attention_0(c, name, X, K, a):
    c.stage = name
    nc = c.nc
    STEPS = B * NQ
    with ExitStack() as s:
        mask = c.sb(s, "mask", [T, 2 * KB], BF16)
        QP = c.sb(s, "QP", [T, PARTS, B, D], BF16)
        tmp = c.sb(s, "tmp", [T, B, D])
        kf = c.sb(s, "kf", [P, 2, S2P])
        kp = c.sb(s, "kp", [P, 2, PARTS, S2P], BF16)
        KS = c.sb(s, "KS", [ROWS, NQ, 4, S2P], BF16)
        QS = c.sb(s, "QS", [ROWS, NQ, 4, T], BF16)
        QR = c.sb(s, "QR", [T, 2, 4, STK], BF16)
        V = c.sb(s, "V", [KB, NQ, NKB, 4, HD + 1])
        Pb = c.sb(s, "Pb", [KB, 2, 4, HKB * T])
        mx3, mx = c.sb(s, "mx3", [T, 2, 4, 3]), c.sb(s, "mx", [T, 4])
        nm, zero = c.sb(s, "nm", [T, 2, 4, PARTS], BF16), c.sb(s, "zero", [T, 4])
        OT, rz, on = c.sb(s, "OT", [P, T]), c.sb(s, "rz", [T, 4, 1]), c.sb(s, "on", [T, 4, HD])
        SB = c.psum(s, "SB", [P, 2, 512])
        ST = c.psum(s, "ST", [P, 2, 2, 512])
        OB = c.psum(s, "OB", [P, 512])
        TB = c.psum(s, "TB", [P, 512])
        TQ, TO = TB[:, 0:3 * P].bitcast(BF16), TB[:, 3 * P:4 * P]
        names = ("chain pchain parts_ready k1_done r_done k2_done k3_done q_built "
                 "q_turned q_stacked scores_ready maxed max_done neg_done neg_turned neg_stacked st_ready "
                 "exp_done pv_done ot_sb ot_turned added zeroed").split()
        S = {n: c.sem(n) for n in names}
        stack_in = [c.sem(f"stack_in{q}") for q in range(NQ)]
        v_in = [c.sem(f"v_in{q}") for q in range(NQ)]
        kf_in = [c.sem(f"kf_in{h}") for h in range(2)]
        mask_in = c.sem("mask_in")
        parts_in = S["parts_ready"]

        with nc.Block() as block:
            @block.sync
            def _(sp):
                sp.dma_start(mask[:, :], a["k_mask0"]).then_inc(mask_in, 16)
                sp.dma_start(KS[STK:ROWS, :, :, :], a["k_one_rows"]).then_inc(mask_in, 16)

                def load_keys(b, hf):
                    sp.dma_start(kf[:, hf, :], a["ctxT0"][bass.ds(b, 1), hf, :, :]
                                 .rearrange("o p k -> (o p) k")).then_inc(kf_in[hf], 16)

                def load_values(b, q):
                    sp.dma_start(V[:, q, :, :, :].rearrange("k n h d -> k (n h d)"),
                                 a["ctxV0"][bass.ds(b, 1), q, :, :].rearrange("o k n -> (o k) n")
                                 ).then_inc(v_in[q], 16)

                def stack(parts, q):
                    sp.wait_ge(S["k3_done"], parts)
                    for r, part in enumerate((0, 1, 2, 0, 1, 0)):
                        sp.dma_start(KS[HD * r:HD * (r + 1), q, :, :], quad_rows(kp, part, q)
                                     ).then_inc(stack_in[q], 16)

                def prepare(b, known):
                    last = known == B - 2
                    b2 = None if last else sp.snap(b + 2)
                    b1 = b + 1 if last else sp.snap(b + 1)
                    for q in range(NQ):
                        parts = 2 * b + q // 2 + 3 if last else fixed(sp, 2 * b + q // 2 + 3, f"{name}_parts{q}")
                        sp.wait_ge(S["st_ready"], SETS * (NQ * b + q + 1))
                        stack(parts, q)
                        if q % 2 == 0 and not last:
                            load_keys(b2, q // 2)
                        sp.wait_ge(S["pv_done"], 2 * (NQ * b + q + 1))
                        load_values(b1, q)

                for hf in range(2):
                    load_keys(0, hf)
                for hf in range(2):
                    for q in (2 * hf, 2 * hf + 1):
                        stack(hf + 1, q)
                    load_keys(1, hf)
                for q in range(NQ):
                    load_values(0, q)
                with sp.Fori(0, B - 2) as b:
                    prepare(b, None)
                prepare(B - 2, B - 2)

            @block.gpsimd
            def _(pool):
                link = Chain(pool, S["pchain"])
                def rest(b, hf):
                    pool.wait_ge(S["k1_done"], 2 * b + hf + 1)
                    pool.tensor_tensor(kf[:, hf, :], kf[:, hf, :], kp[:, hf, 0, :],
                                       ALU.subtract).then_inc(S["r_done"], 1)

                def third(b, hf):
                    pool.wait_ge(S["k2_done"], 2 * b + hf + 1)
                    pool.tensor_tensor(kp[:, hf, 2, :], kf[:, hf, :], kp[:, hf, 1, :],
                                       ALU.subtract).then_inc(S["k3_done"], 1)

                def build_queries(b, q):
                    n = NQ * b + q
                    if not (isinstance(n, int) and n < 2):
                        pool.wait_ge(S["q_turned"], n - 1)
                    pool.wait_ge(parts_in, 1)
                    at = 0
                    for part, times in ((0, 3), (1, 2), (2, 1)):
                        src = QP[:, part, bass.ds(b, 1), 4 * HD * q:4 * HD * (q + 1)].rearrange(
                            "t o (h d) -> t (o h) d", d=HD)
                        last = pool.tensor_copy(
                            QR[:, q % 2, :, at * HD:(at + times) * HD].rearrange("t h (r d) -> t h r d", d=HD),
                            src.unsqueeze(2).to_broadcast([T, 4, times, HD]))
                        at += times
                    last.then_inc(S["q_built"], 1)

                def negate(n, q):
                    pool.wait_ge(S["max_done"], n + 1)
                    pool.wait_ge(S["neg_turned"], n - 1) if not isinstance(n, int) or n >= 2 else None
                    link(pool.tensor_tensor(nm[:, q % 2, :, 0], mx[:, :], zero[:, :], ALU.add))
                    link(pool.tensor_tensor(mx[:, :], mx[:, :], nm[:, q % 2, :, 0], ALU.subtract))
                    link(pool.tensor_tensor(nm[:, q % 2, :, 1], mx[:, :], zero[:, :], ALU.add))
                    pool.tensor_tensor(nm[:, q % 2, :, 2], mx[:, :], nm[:, q % 2, :, 1],
                                       ALU.subtract).then_inc(S["neg_done"], 1)

                def parts(b, q, known):
                    if known != B - 1 and not (known == B - 2 and q == 3):
                        (third, rest, third, rest)[q](b + (q + 5) // 4, (0, 1, 1, 0)[q])

                for split in (rest, third):
                    for hf in range(2):
                        split(0, hf)
                build_queries(0, 0)
                build_queries(0, 1)
                build_queries(0, 2)
                negate(0, 0)
                rest(1, 0)

                def body(b, known):
                    final = known == B - 1
                    for q in range(NQ):
                        n = NQ * b + q
                        parts(b, q, known)
                        if not (final and q == 3):
                            negate(n + 1, (q + 1) % NQ)
                        if not (final and q >= 1):
                            build_queries(b + (q + 3) // NQ, (q + 3) % NQ)

                with pool.Fori(0, B - 2) as b:
                    link.loop(b, 3 * NQ)
                    body(b, None)
                link.end(B - 2)
                body(B - 2, B - 2)
                body(B - 1, B - 1)

            @block.tensor
            def _(pe):
                def turn_queries(n, q):
                    pe.wait_ge(S["q_built"], n + 1)
                    pe.wait_ge(S["q_stacked"], n)
                    for j in range(4):
                        last = pe.transpose(TQ[0:STK, j * T:(j + 1) * T], QR[:, q % 2, j, :],
                                            K["identb"][0:T, 0:T])
                    last.then_inc(S["q_turned"], 1)

                def score_chunk(n, q, k):
                    j, part = divmod(k, 3)
                    if k == 0:
                        pe.wait_ge(S["q_stacked"], n + 1)
                    at = 12 * n + k
                    if not (isinstance(at, int) and at < 2):
                        pe.wait_ge(S["maxed"], at - 1)
                    lo, hi = CUTS[part:part + 2]
                    last = pe.matmul(SB[0:T, k % 2, 0:hi - lo], QS[0:STK, q, j, :], KS[0:STK, q, j, lo:hi],
                                     start=True, stop=(part < 2), skip_group_check=True)
                    if part == 2:
                        m = S2 - T
                        last = pe.matmul(SB[0:T, k % 2, m - lo:hi - lo], K["identb"][0:T, 0:T],
                                         mask[:, m - MASK0:S2 - MASK0], start=False, stop=True,
                                         skip_group_check=True)
                    last.then_inc(S["scores_ready"], 1)

                def turn_maxima(n, q):
                    pe.wait_ge(S["neg_done"], n + 1)
                    for j in range(4):
                        last = pe.transpose(TQ[STK:ROWS, j * T:(j + 1) * T], nm[:, q % 2, j, :],
                                            K["identb"][0:T, 0:T])
                    last.then_inc(S["neg_turned"], 1)

                def score_set(n, q, k):
                    half, j = divmod(k, 4)
                    if k == 0:
                        pe.wait_ge(S["neg_stacked"], n + 1)
                    at = SETS * n + k
                    if not (isinstance(at, int) and at < 2):
                        pe.wait_ge(S["exp_done"], at - 1)
                    for i in range(HKB):
                        kb = half * HKB + i
                        dst = ST[0:KB, k % 2, i // 3, (i % 3) * T:(i % 3 + 1) * T]
                        masked = kb * KB >= MASK0
                        last = pe.matmul(dst, KS[:, q, j, kb * KB:(kb + 1) * KB], QS[:, q, j, :],
                                         start=True, stop=not masked, skip_group_check=True)
                        if masked:
                            at_mask = kb * KB - MASK0
                            last = pe.matmul(dst, mask[:, at_mask:at_mask + KB], K["identb"][0:T, 0:T], start=False, stop=True,
                                             skip_group_check=True)
                    last.then_inc(S["st_ready"], 1)

                def turn_out(n, q):
                    pe.wait_ge(S["ot_sb"], n + 1)
                    pe.wait_ge(S["added"], n)
                    pe.transpose(TO[0:T, :], OT[:, :], K["ident"][:, :]).then_inc(S["ot_turned"], 1)

                def weigh(n, q, half, piece):
                    if piece == 0:
                        pe.wait_ge(S["exp_done"], SETS * n + 4 * half + 4)
                    for i in (2 * piece, 2 * piece + 1):
                        kb = half * HKB + i
                        for j in range(4):
                            last = pe.matmul(OB[32 * j:32 * j + HD + 1, 0:T], V[:, q, kb, j, :],
                                             Pb[:, half, j, i * T:(i + 1) * T], start=(kb == 0),
                                             stop=(kb == NKB - 1), skip_group_check=True)
                    if piece == 2:
                        last.then_inc(S["pv_done"], 1)

                pe.wait_ge(mask_in, 32)
                turn_queries(0, 0)
                turn_queries(1, 1)
                for n, chunks in ((0, 12), (1, 6)):
                    pe.wait_ge(stack_in[n], 6 * 16)
                    for k in range(chunks):
                        score_chunk(n, n, k)
                turn_maxima(0, 0)
                pe.wait_ge(S["zeroed"], 1)

                def body(b, known):
                    final, first = known == B - 1, known == -1
                    for q in range(NQ):
                        n = NQ * b + q
                        before = not (first and q == 0)
                        for k in range(SETS):
                            score_set(n, q, k)
                            if k == 4 and not (final and q >= 2):
                                pe.wait_ge(stack_in[(q + 2) % NQ], 96 * (b + (q + 2) // NQ + 1))
                            ahead = 1 if k < 4 else 2
                            chunks = () if final and q + ahead >= NQ else CHUNKS_AT[k]
                            for chunk in chunks[:1]:
                                score_chunk(n + ahead, (q + ahead) % NQ, chunk)
                            if 1 <= k < 4 and before:
                                weigh(n - 1, (q - 1) % NQ, 1, k - 1)
                            if k >= 5:
                                if k == 5:
                                    pe.wait_ge(v_in[q], 16 * (b + 1))
                                    if before:
                                        pe.wait_ge(S["ot_sb"], n)
                                weigh(n, q, 0, k - 5)
                            for chunk in chunks[1:]:
                                score_chunk(n + ahead, (q + ahead) % NQ, chunk)
                            if k == 1 and not (final and q >= 2):
                                if not (first and q < 2):
                                    pe.wait_ge(S["added"], n - 1)
                                turn_queries(n + 2, (q + 2) % NQ)
                            if k == 4 and before:
                                pe.wait_ge(S["q_stacked"], STEPS if final and q >= 2 else n + 3)
                                turn_out(n - 1, (q - 1) % NQ)
                            if k == 6 and not (final and q == 3):
                                if before:
                                    pe.wait_ge(S["added"], n)
                                turn_maxima(n + 1, (q + 1) % NQ)

                body(0, -1)
                with pe.Fori(1, B - 1) as b:
                    body(b, 0)
                body(B - 1, B - 1)
                for piece in range(3):
                    weigh(STEPS - 1, 3, 1, piece)
                turn_out(STEPS - 1, 3)

            @block.scalar
            def _(act):
                def part1(b, hf):
                    act.wait_ge(kf_in[hf], 16 * (b + 1))
                    act.wait_ge(stack_in[2 * hf], 96 * b)
                    act.wait_ge(stack_in[2 * hf + 1], 96 * b)
                    act.activation(kp[:, hf, 0, :], kf[:, hf, :], ACT.Copy).then_inc(S["k1_done"], 1)

                def part2(b, hf):
                    act.wait_ge(S["r_done"], 2 * b + hf + 1)
                    act.activation(kp[:, hf, 1, :], kf[:, hf, :], ACT.Copy).then_inc(S["k2_done"], 1)

                def take_queries(n, q):
                    act.wait_ge(S["q_turned"], n + 1)
                    act.activation(QS[0:STK, q, :, :].rearrange("r h t -> r (h t)"), TQ[0:STK, 0:GT],
                                   ACT.Copy).then_inc(S["q_stacked"], 1)

                def take_maxima(n, q):
                    act.wait_ge(S["neg_turned"], n + 1)
                    act.activation(QS[STK:ROWS, q, :, :].rearrange("r h t -> r (h t)"), TQ[STK:ROWS, 0:GT],
                                   ACT.Copy).then_inc(S["neg_stacked"], 1)

                def exponential(n, k):
                    half, j = divmod(k, 4)
                    act.wait_ge(S["st_ready"], SETS * n + k + 1)
                    if j == 0 and not (isinstance(n, int) and n == 0):
                        act.wait_ge(S["pv_done"], 2 * n + half - 1)
                    act.activation(Pb[:, half, j, :].rearrange("k (c t) -> k c t", c=2), ST[0:KB, k % 2, :, 0:3 * T],
                                   ACT.Exp, scale=HD ** -0.5).then_inc(S["exp_done"], 1)

                for split in (part1, part2):
                    for hf in range(2):
                        split(0, hf)
                take_queries(0, 0)
                take_queries(1, 1)
                part1(1, 0)
                take_maxima(0, 0)

                def parts(b, q, known):
                    if known != B - 1 and not (known == B - 2 and q == 3):
                        (part2, part1, part2, part1)[q](b + (q + 5) // 4, (0, 1, 1, 0)[q])

                def body(b, known):
                    final = known == B - 1
                    for q in range(NQ):
                        n = NQ * b + q
                        for k in range(SETS):
                            exponential(n, k)
                            if k == 0:
                                parts(b, q, known)
                            if k == 1 and not (final and q >= 2):
                                take_queries(n + 2, (q + 2) % NQ)
                            if k == 6 and not (final and q == 3):
                                take_maxima(n + 1, (q + 1) % NQ)

                body(0, -1)
                with act.Fori(1, B - 2) as b:
                    body(b, None)
                body(B - 2, B - 2)
                body(B - 1, B - 1)

            @block.vector
            def _(dve):
                link = Chain(dve, S["chain"])
                dve.memset(OB[:, :], 0.0).then_inc(S["zeroed"], 1)
                link(dve.memset(zero[:, :], 0.0))
                link(dve.tensor_copy(QP[:, 0, :, :], X[:, :, :]))
                link(dve.tensor_tensor(tmp[:, :, :], X[:, :, :], QP[:, 0, :, :], ALU.subtract))
                link(dve.tensor_copy(QP[:, 1, :, :], tmp[:, :, :]))
                dve.tensor_tensor(QP[:, 2, :, :], tmp[:, :, :], QP[:, 1, :, :],
                                  ALU.subtract).then_inc(S["parts_ready"], 1)

                def chunk(n, q, k):
                    j, part = divmod(k, 3)
                    dve.wait_ge(S["scores_ready"], 12 * n + k + 1)
                    dve.tensor_reduce(mx3[:, q % 2, j, part:part + 1],
                                      SB[0:T, k % 2, 0:CUTS[part + 1] - CUTS[part]], AX_X,
                                      ALU.max).then_inc(S["maxed"], 1)

                def maximum(n, q):
                    dve.wait_ge(S["maxed"], 12 * (n + 1))
                    dve.wait_ge(S["neg_done"], n)
                    dve.tensor_reduce(mx[:, :], mx3[:, q % 2, :, :], AX_X, ALU.max,
                                      negate=True).then_inc(S["max_done"], 1)

                def take_out(n, q):
                    dve.wait_ge(S["pv_done"], 2 * (n + 1))
                    dve.wait_ge(S["ot_turned"], n)
                    dve.tensor_copy(OT[:, :], OB[:, 0:T]).then_inc(S["ot_sb"], 1)

                def add_out(n, b, q):
                    dve.wait_ge(S["ot_turned"], n + 1)
                    o = TO[0:T, :].rearrange("t (j d) -> t j d", j=4)
                    link(dve.reciprocal(rz[:, :, :], o[:, :, HD:HD + 1]))
                    link(dve.tensor_tensor(on[:, :, :], o[:, :, 0:HD], rz[:, :, :].to_broadcast([T, 4, HD]),
                                           ALU.mult))
                    xb = X[:, bass.ds(b, 1), 4 * HD * q:4 * HD * (q + 1)].rearrange("t o (j d) -> t (o j) d", d=HD)
                    dve.tensor_tensor(xb, xb, on[:, :, :], ALU.add).then_inc(S["added"], 1)

                for k in range(12):
                    chunk(0, 0, k)
                maximum(0, 0)
                for k in range(6):
                    chunk(1, 1, k)

                def body(b, known):
                    final, first = known == B - 1, known == -1
                    for q in range(NQ):
                        n = NQ * b + q
                        before = not (first and q == 0)
                        for k in range(SETS):
                            ahead = 1 if k < 4 else 2
                            if not (final and q + ahead >= NQ):
                                for piece in CHUNKS_AT[k]:
                                    chunk(n + ahead, (q + ahead) % NQ, piece)
                            if k == 3:
                                if not (final and q == 3):
                                    maximum(n + 1, (q + 1) % NQ)
                                if before:
                                    take_out(n - 1, (q - 1) % NQ)
                            if k == 5 and before:
                                add_out(n - 1, b if q > 0 else b - 1, (q - 1) % NQ)

                body(0, -1)
                with dve.Fori(1, B - 1) as b:
                    link.loop(b - 1, 2 * NQ)
                    body(b, 0)
                link.end(B - 2)
                body(B - 1, B - 1)
                take_out(STEPS - 1, 3)
                add_out(STEPS - 1, B - 1, 3)



def latent_and_experts(c, X, A, K, a):
    nc = c.nc
    with ExitStack() as s:
        c.stage = "la"
        XT = c.sb(s, "XT", [P, DC, N])
        nw = c.sb(s, "nw", [P, 2, DC])
        load(c, "lanw", [(nw[:, 0, :], a["L0l_nw"]), (nw[:, 1, :], a["L0m_nw"])])
        with ExitStack() as s2:
            c.stage = "law"
            w, started = later_weights(c, s2, a, "L0l_", {"wq": [P, DC, H * P], "wk": [P, DC, H * P],
                                                        "wv": [P, DC, H * P], "wo": [P, H, D]})
            features_first(c, "lan", X, XT, K["ident"], rms=True, weight=nw[:, 0, :], copy=A)
            end_load(c, started)
            latent_attention(c, "laa", A, XT, K, w, (P + 64) ** -0.5)
        with ExitStack() as s2:
            c.stage = "moe"
            w0 = weights(c, s2, a, "L0m_", {"gate": [P, DC, E0], "prio": [T, E0]})
            sel = c.sb(s2, "sel", [96, EC * P], BF16)
            load(c, "moesel", [(sel[:, :], a["k_experts"])])
            c.stage = "moew"
            w, started = later_weights(c, s2, a, "L0m_", {"wg": [P, DC, EC * P], "wu": [P, DC, EC * P],
                                                        "wd": [P, EC, D], "sg": [P, DC, SHI],
                                                        "su": [P, DC, SHI], "sd": [P, 3, D]})
            features_first(c, "moen", A, XT, K["ident"], rms=True, weight=nw[:, 1, :])
            WT = c.sb(s2, "WT", [96, N], BF16)
            route_top4(c, "rt", XT, WT, K, w0, X, A)
            end_load(c, started)
            experts(c, "moe", X, XT, WT, sel, w)
    layernorm(c, "ff0l", X)


def first_of(link, dve, work, best, rank, pick, prio, n):
    wide = lambda t: t[:, :, :].to_broadcast([T, B, n])
    link(dve.tensor_reduce(best[:, :, 0], work[:, :, :], AX_X, ALU.max))
    link(dve.tensor_tensor(pick[:, :, :], work[:, :, :], wide(best), ALU.is_equal))
    link(dve.tensor_tensor(pick[:, :, :], pick[:, :, :], prio.unsqueeze(1).to_broadcast([T, B, n]), ALU.mult))
    link(dve.tensor_reduce(rank[:, :, 0], pick[:, :, :], AX_X, ALU.max))
    link(dve.tensor_tensor(pick[:, :, :], pick[:, :, :], wide(rank), ALU.is_equal))


def router_logits(pe, LG, XT, gate, n, done):
    for b in range(B):
        for ch in range(DC):
            last = pe.matmul(LG[0:T, b * n:(b + 1) * n], XT[:, ch, b * T:(b + 1) * T], gate[:, ch, :],
                             start=(ch == 0), stop=(ch == DC - 1))
    last.then_inc(done, 1)


def route_top4(c, name, XT, WT, K, w, X, A):
    c.stage = name
    nc = c.nc
    with ExitStack() as s:
        e, work, pick, chosen = (c.sb(s, n, [T, B, E0]) for n in ("e", "work", "pick", "chosen"))
        best, rank = c.sb(s, "best", [T, B, 1]), c.sb(s, "rank", [T, B, 1])
        WP = c.sb(s, "WP", [T, B, 96], BF16)
        LG = c.psum(s, "LG", [P, 512])
        WB = c.psum(s, "WB", [P, 4, 1024], BF16)
        chain, logits, shifted, exp_done, parts, turned = (c.sem(n) for n in (
            "chain", "logits", "shifted", "exp_done", "parts", "turned"))
        with nc.Block() as block:
            @block.gpsimd
            def _(pool):
                pool.tensor_tensor(X[:, :, :], X[:, :, :], A[:, :, :], ALU.add)

            @block.tensor
            def _(pe):
                router_logits(pe, LG, XT, w["gate"], E0, logits)
                pe.wait_ge(parts, 1)
                for b in range(B):
                    last = pe.transpose(WB[0:96, b // 4, (b % 4) * T:(b % 4 + 1) * T], WP[:, b, :],
                                        K["identb"][0:T, 0:T])
                last.then_inc(turned, 1)

            @block.scalar
            def _(act):
                act.wait_ge(shifted, 1)
                act.activation(e[:, :, :], e[:, :, :], ACT.Exp).then_inc(exp_done, 1)
                act.wait_ge(turned, 1)
                act.activation(WT[:, :].rearrange("r (g t) -> r g t", g=G), WB[0:96, :, 0:GT], ACT.Copy)

            @block.vector
            def _(dve):
                link = Chain(dve, chain)
                link(dve.memset(WP[:, :, :], 0.0))
                link(dve.memset(chosen[:, :, :], 0.0))
                dve.wait_ge(logits, 1)
                lg = LG[0:T, 0:B * E0].rearrange("t (b e) -> t b e", b=B)
                wide = lambda t: t[:, :, :].to_broadcast([T, B, E0])
                link(dve.tensor_reduce(best[:, :, 0], lg, AX_X, ALU.max))
                dve.tensor_tensor(e[:, :, :], lg, wide(best), ALU.subtract).then_inc(shifted, 1)
                dve.wait_ge(exp_done, 1)
                link(dve.tensor_copy(work[:, :, :], e[:, :, :]))
                for k in range(TOPK):
                    first_of(link, dve, work, best, rank, pick, w["prio"][:, :], E0)
                    link(dve.tensor_tensor(chosen[:, :, :], chosen[:, :, :], pick[:, :, :], ALU.add))
                    if k < TOPK - 1:
                        link(dve.tensor_scalar(pick[:, :, :], pick[:, :, :], -4.0, None, ALU.mult))
                        link(dve.tensor_tensor(work[:, :, :], work[:, :, :], pick[:, :, :], ALU.add))
                link(dve.tensor_tensor(e[:, :, :], e[:, :, :], chosen[:, :, :], ALU.mult))
                link(dve.tensor_reduce(best[:, :, 0], e[:, :, :], AX_X, ALU.add))
                link(dve.reciprocal(best[:, :, :], best[:, :, :]))
                link(dve.tensor_tensor(e[:, :, :], e[:, :, :], wide(best), ALU.mult))
                link(dve.tensor_copy(WP[:, :, 0:E0], e[:, :, :]))
                link(dve.tensor_tensor(e[:, :, :], e[:, :, :], WP[:, :, 0:E0], ALU.subtract))
                link(dve.tensor_copy(WP[:, :, 32:32 + E0], e[:, :, :]))
                dve.tensor_tensor(WP[:, :, 64:64 + E0], e[:, :, :], WP[:, :, 32:32 + E0],
                                  ALU.subtract).then_inc(parts, 1)


def experts(c, name, X, XT, WT, sel, w):
    c.stage = name
    nc = c.nc
    NC = EC + 3
    width = lambda k: P if k < EC else min(P, SHI - (k - EC) * P)
    with ExitStack() as s:
        sg, hid = c.sb(s, "gated", [P, 2, GT]), c.sb(s, "hid", [P, 2, GT])
        HB = c.psum(s, "HB", [P, 2, 3, 512])
        OB = c.psum(s, "OB", [P, 2, 512])
        silu_done, up_done, hid_ready, gu_ready, chunk_done, out_ready, added = (c.sem(n) for n in (
            "silu_done", "up_done", "hid_ready", "gu_ready", "chunk_done", "out_ready", "added"))
        with nc.Block() as block:
            @block.tensor
            def _(pe):
                def up(g, k):
                    M = width(k)
                    n = g * NC + k
                    if k >= 2:
                        pe.wait_ge(hid_ready, n - 1)
                    elif not isinstance(g, int):
                        pe.wait_ge(out_ready, g)
                        pe.wait_ge(added, g)
                    tok = bass.ds(g * GT, GT)
                    mats = ("wg", "wu") if k < EC else ("sg", "su")
                    at = (k if k < EC else k - EC) * P
                    for i in range(2):
                        for ch in range(DC):
                            last = pe.matmul(HB[0:M, k % 2, i, 0:GT], w[mats[i]][:, ch, at:at + M], XT[:, ch, tok],
                                             start=(ch == 0), stop=(ch == DC - 1))
                    if k < EC:
                        last = pe.matmul(HB[0:M, k % 2, 2, 0:GT], sel[:, at:at + M], WT[:, tok],
                                         start=True, stop=True)
                    last.then_inc(gu_ready, 1)

                def down(g, k):
                    M = width(k)
                    pe.wait_ge(hid_ready, g * NC + k + 1)
                    wd = w["wd"][0:M, k, :] if k < EC else w["sd"][0:M, k - EC, :]
                    for b in range(GB):
                        last = pe.matmul(OB[0:T, b // 2, (b % 2) * D:(b % 2 + 1) * D], hid[0:M, k % 2, b * T:(b + 1) * T],
                                         wd, start=(k == 0 and b % 2 == 0), stop=(k == NC - 1),
                                         skip_group_check=True)
                    last.then_inc(chunk_done, 1)
                    if k == NC - 1:
                        pe.wait_ge(chunk_done, (g + 1) * NC)
                        pe.sem_inc(out_ready, 1)

                with pe.Fori(0, G) as g:
                    up(g, 0)
                    for k in range(NC):
                        if k + 1 < NC:
                            up(g, k + 1)
                        down(g, k)

            @block.scalar
            def _(act):
                with act.Fori(0, G) as g:
                    for k in range(NC):
                        M = width(k)
                        n = g * NC + k
                        act.wait_ge(gu_ready, n + 1)
                        if k >= 2:
                            act.wait_ge(up_done, n - 1)
                        else:
                            act.wait_ge(up_done, g * NC)
                        act.activation(sg[0:M, k % 2, :], HB[0:M, k % 2, 0, 0:GT], ACT.Silu).then_inc(silu_done, 1)

            @block.vector
            def _(dve):
                with dve.Fori(0, G) as g:
                    for k in range(NC):
                        M = width(k)
                        n = g * NC + k
                        dve.wait_ge(silu_done, n + 1)
                        if k >= 2:
                            dve.wait_ge(chunk_done, n - 1)
                        else:
                            dve.wait_ge(chunk_done, g * NC)
                        h = hid[0:M, k % 2, :]
                        ins = dve.tensor_tensor(h, HB[0:M, k % 2, 1, 0:GT], sg[0:M, k % 2, :], ALU.mult)
                        ins.then_inc(up_done, 1)
                        if k < EC:
                            dve.wait_ge(up_done, n + 1)
                            dve.tensor_tensor(h, h, HB[0:M, k % 2, 2, 0:GT], ALU.mult).then_inc(hid_ready, 1)
                        else:
                            dve.wait_ge(up_done, n + 1)
                            dve.sem_inc(hid_ready, 1)
                    dve.wait_ge(out_ready, g + 1)
                    xg = X[:, bass.ds(g * GB, GB), :].rearrange("t b d -> t (b d)").rearrange("t (i n) -> t i n", i=2)
                    dve.tensor_tensor(xg, xg, OB[0:T, :, :], ALU.add).then_inc(added, 1)
                    dve.wait_ge(added, g + 1)



def cross_attention_1(c, name, X, K, a):
    c.stage = name
    nc = c.nc
    LIM = 50.0 * HD ** 0.5
    MROWS = STK + 1
    with ExitStack() as s:
        A = c.sb(s, "A", [T, B, D])
        QP = c.sb(s, "QP", [T, PARTS, B, D], BF16)
        rs = c.sb(s, "rs", [T, 1])
        c.stage = name + "w"
        wo = c.sb(s, "wo", [P, DC, D])
        bo, bv = (c.sb(s, n, [T, D]) for n in ("bo", "bv"))
        gamma, beta = c.sb(s, "gamma", [T, D]), c.sb(s, "beta", [T, D])
        bk = c.sb(s, "bk", [P, 2])
        wk, wv = c.sb(s, "wk", [P, DC, D]), c.sb(s, "wv", [P, DC, D])
        needed_later = [(wk[:, :, :], a["L1x_wk"]), (wv[:, :, :], a["L1x_wv"]), (wo[:, :, :], a["L1x_wo"]),
                             (bo[:, :], a["L1x_bo"].partition_broadcast(T)),
                             (bv[:, :], a["L1x_bv"].partition_broadcast(T)),
                             (bk[:, :], a["L1x_bk"]), (rs[:, :], a["L1x_rs"]),
                             (gamma[:, :], a["L1x_gamma"].partition_broadcast(T)),
                             (beta[:, :], a["L1x_beta"].partition_broadcast(T))]
        started = query_parts(c, name + "q", X, A, QP, K, a, needed_later)
        end_load(c, started)
        projected_context(c, name, A, QP, K, a, wk, wv, bk, bv, LIM, MROWS)
        project_out(c, name + "o", A, K, wo, bo)
        layernorm(c, name + "d", A, gamma=gamma[:, :], beta=beta[:, :], into=X, scale=rs[:, 0:1])


def query_parts(c, name, X, A, QP, K, a, needed_later):
    nc = c.nc
    with ExitStack() as s:
        c.stage = name
        XT = c.sb(s, "XT", [P, DC, N])
        wq = c.sb(s, "wq", [P, DC, D])
        bq = c.sb(s, "bq", [T, D])
        mi, mf, mb = c.sb(s, "mi", [B, S2P], I32), c.sb(s, "mf", [B, S2P]), c.sb(s, "mb", [B, S2P], BF16)
        load(c, name + "l", [(wq[:, :, :], a["L1x_wq"]), (bq[:, :], a["L1x_bq"].partition_broadcast(T)),
                             (mi[:, :], a["mask"])])
        started = start_load(c, name + "s", needed_later)
        features_first(c, name + "t", X, XT, K["ident"])
        c.stage = name
        QB = c.psum(s, "QB", [P, 8, 512])
        chain, made, bias_made, stored = (c.sem(n) for n in ("chain", "made", "bias_made", "stored"))
        with nc.Block() as block:
            @block.sync
            def _(sp):
                sp.wait_ge(bias_made, 1)
                for h in range(4):
                    sp.dma_start(a["s_mask"][:, h, :], mb[:, :]).then_inc(stored, 16)
                sp.wait_ge(stored, 4 * 16)

            @block.tensor
            def _(pe):
                for n in range(B):
                    dst = QB[0:T, n // 2, (n % 2) * D:(n % 2 + 1) * D]
                    for ch in range(DC):
                        last = pe.matmul(dst, XT[:, ch, n * T:(n + 1) * T], wq[:, ch, :], start=(ch == 0),
                                         stop=(ch == DC - 1))
                    last.then_inc(made, 1)

            @block.vector
            def _(dve):
                link = Chain(dve, chain)
                link(dve.tensor_copy(mf[:, :], mi[:, :]))
                link(dve.tensor_scalar(mf[:, :], mf[:, :], 0.5, None, ALU.is_gt))
                dve.tensor_scalar(mb[:, :], mf[:, :], 1.0, -NEG, ALU.subtract, ALU.mult).then_inc(bias_made, 1)
                for n in range(8):
                    dve.wait_ge(made, 2 * n + 2)
                    last = dve.tensor_tensor(A[:, 2 * n:2 * n + 2, :], QB[0:T, n, :].rearrange("t (b d) -> t b d", b=2),
                                             bq[:, :].unsqueeze(1).to_broadcast([T, 2, D]), ALU.add)
                link(last)
                link(dve.tensor_copy(QP[:, 0, :, :], A[:, :, :]))
                link(dve.tensor_tensor(A[:, :, :], A[:, :, :], QP[:, 0, :, :], ALU.subtract))
                link(dve.tensor_copy(QP[:, 1, :, :], A[:, :, :]))
                dve.tensor_tensor(QP[:, 2, :, :], A[:, :, :], QP[:, 1, :, :], ALU.subtract)
    return started


LATE, EARLY = {}, {}
for _k in range(SETS):
    LATE[0, _k] = [("v", 0, 8 + _k)] if _k < 4 else [("v", 1, _k - 4)]
    LATE[1, _k] = [("v", 1, 4 + _k)]
    EARLY[2, _k] = [] if _k < 2 else [("k", 0, _k - 2)] if _k < 5 else [("v", 0, _k - 5)]
    EARLY[3, _k] = [("v", 0, 3 + _k)] if _k < 4 else [("k", 1, _k - 4)] if _k < 7 else [("v", 0, 7)]
PROJECTIONS = [t for table, steps in ((EARLY, (2, 3)), (LATE, (0, 1))) for q in steps for k in range(SETS)
               for t in table[q, k]]
NPR = len(PROJECTIONS)


def projected_context(c, name, A, QP, K, a, wk, wv, bk, bv, LIM, MROWS):
    c.stage = name
    nc = c.nc
    STEPS = B * NQ
    with ExitStack() as s:
        cx = c.sb(s, "cx", [P, DC, S2P])
        kf = c.sb(s, "kf", [P, S2P])
        kp = c.sb(s, "kp", [P, PARTS, S2P], BF16)
        KS = c.sb(s, "KS", [MROWS, NQ, 4, S2P], BF16)
        QS = c.sb(s, "QS", [MROWS, NQ, 4, T], BF16)
        QR = c.sb(s, "QR", [T, 2, 4, STK], BF16)
        V = c.sb(s, "V", [KB, NQ, NKB, 4, HD + 1])
        Cb = c.sb(s, "Cb", [KB, 2, HKB * T])
        Pb = c.sb(s, "Pb", [KB, 2, 4, HKB * T])
        OT = c.sb(s, "OT", [P, T])
        rz, sz, on = c.sb(s, "rz", [T, 4, 1]), c.sb(s, "sz", [T, 4, 1]), c.sb(s, "on", [T, 4, HD])
        PR = c.psum(s, "PR", [P, 2, 512])
        ST = c.psum(s, "ST", [P, 2, 2, 512])
        OB = c.psum(s, "OB", [P, 512])
        TB = c.psum(s, "TB", [P, 512])
        TQ, TO = TB[:, 0:3 * P].bitcast(BF16), TB[:, 3 * P:4 * P]
        names = ("chain r_done k3_done k1_done k2_done q_built q_turned q_stacked st_ready clipped "
                 "exp_done pv_done ot_sb ot_turned zeroed made taken added").split()
        S = {n: c.sem(n) for n in names}
        stack_in = [c.sem(f"stack_in{q}") for q in range(NQ)]
        cx_in = [c.sem(f"cx_in{i}") for i in range(3)]
        number = {t: i for i, t in enumerate(PROJECTIONS)}
        KEYS_TAKEN = [number["k", hf, 2] + 1 for hf in range(2)]

        with nc.Block() as block:
            @block.sync
            def _(sp):
                def load_context(b, i):
                    cols = slice(i * S2P // 3, (i + 1) * S2P // 3)
                    sp.dma_start(cx[:, :, cols], a["ctxT1"][bass.ds(b, 1), :, :, cols]
                                 .rearrange("o p c k -> (o p) c k")).then_inc(cx_in[i], 16)

                def stack(b, q, parts):
                    sp.wait_ge(S["k3_done"], parts)
                    for r, part in enumerate((0, 1, 2, 0, 1, 0)):
                        sp.dma_start(KS[HD * r:HD * (r + 1), q, :, :], kp[64 * (q % 2):64 * (q % 2) + 64, part, :]
                                     ).then_inc(stack_in[q], 16)
                    sp.dma_start(KS[STK:MROWS, q, :, :], a["s_mask"][bass.ds(b, 1), :, :]).then_inc(stack_in[q], 16)

                def second_half(b, known):
                    parts = 2 * b + 2 if known else fixed(sp, 2 * b + 2, f"{name}_parts1")
                    for q in (2, 3):
                        if not (known and b == 0):
                            sp.wait_ge(S["st_ready"], SETS * (NQ * (b - 1) + q + 1))
                        stack(b, q, parts)

                def next_context(b, known):
                    b1 = b + 1 if known else sp.snap(b + 1)
                    parts = 2 * b + 3 if known else fixed(sp, 2 * b + 3, f"{name}_parts0")
                    for i in range(3):
                        sp.wait_ge(S["made"], NPR * b + number["v", 1, 4 * i + 3] + 1)
                        load_context(b1, i)
                    for q in (0, 1):
                        sp.wait_ge(S["st_ready"], SETS * (NQ * b + q + 1))
                        stack(b1, q, parts)

                for i in range(3):
                    load_context(0, i)
                for q in (0, 1):
                    stack(0, q, 1)
                second_half(0, True)
                next_context(0, True)
                with sp.Fori(1, B - 1) as b:
                    second_half(b, False)
                    next_context(b, False)
                second_half(B - 1, True)

            @block.gpsimd
            def _(pool):
                def rest(n):
                    pool.wait_ge(S["k1_done"], n + 1)
                    pool.tensor_tensor(kf[:, :], kf[:, :], kp[:, 0, :], ALU.subtract).then_inc(S["r_done"], 1)

                def third(n):
                    pool.wait_ge(S["k2_done"], n + 1)
                    pool.tensor_tensor(kp[:, 2, :], kf[:, :], kp[:, 1, :], ALU.subtract).then_inc(S["k3_done"], 1)

                def build_queries(b, q):
                    n = NQ * b + q
                    if not (isinstance(n, int) and n < 2):
                        pool.wait_ge(S["q_turned"], n - 1)
                    at = 0
                    for part, times in ((0, 3), (1, 2), (2, 1)):
                        src = QP[:, part, bass.ds(b, 1), 4 * HD * q:4 * HD * (q + 1)].rearrange(
                            "t o (h d) -> t (o h) d", d=HD)
                        last = pool.tensor_copy(
                            QR[:, q % 2, :, at * HD:(at + times) * HD].rearrange("t h (r d) -> t h r d", d=HD),
                            src.unsqueeze(2).to_broadcast([T, 4, times, HD]))
                        at += times
                    last.then_inc(S["q_built"], 1)

                build_queries(0, 0)
                build_queries(0, 1)
                rest(0)
                third(0)

                def body(b, final):
                    for q in range(NQ):
                        if not (final and q >= 2):
                            build_queries(b + (q + 2) // NQ, (q + 2) % NQ)
                        if q == 0 or (q == 2 and not final):
                            rest(2 * b + 1 + q // 2)
                            third(2 * b + 1 + q // 2)
                with pool.Fori(0, B - 1) as b:
                    body(b, False)
                body(B - 1, True)

            @block.tensor
            def _(pe):
                def project(b, tasks):
                    for kind, hf, k in tasks:
                        at = number[kind, hf, k]
                        if (kind, hf) == ("k", 0):
                            pe.wait_ge(cx_in[k], 16 * (b + 1))
                        if not (isinstance(b, int) and b == 0 and at < 2):
                            pe.wait_ge(S["taken"], NPR * b + at - 1)
                        heads = slice(hf * P, (hf + 1) * P)
                        lo, hi = CUTS[k:k + 2] if kind == "k" else (k * KB, (k + 1) * KB)
                        for ch in range(DC):
                            if kind == "k":
                                last = pe.matmul(PR[:, at % 2, 0:hi - lo], wk[:, ch, heads], cx[:, ch, lo:hi],
                                                 start=(ch == 0), stop=(ch == DC - 1))
                            else:
                                last = pe.matmul(PR[0:KB, at % 2, 0:P], cx[:, ch, lo:hi], wv[:, ch, heads],
                                                 start=(ch == 0), stop=(ch == DC - 1))
                        last.then_inc(S["made"], 1)

                def turn_queries(n, q):
                    pe.wait_ge(S["q_built"], n + 1)
                    pe.wait_ge(S["q_stacked"], n)
                    for j in range(4):
                        last = pe.transpose(TQ[0:STK, j * T:(j + 1) * T], QR[:, q % 2, j, :],
                                            K["identb"][0:T, 0:T])
                    last.then_inc(S["q_turned"], 1)

                def score_set(n, q, k):
                    half, j = divmod(k, 4)
                    if k == 0:
                        pe.wait_ge(S["q_stacked"], n + 1)
                    at = SETS * n + k
                    if not (isinstance(at, int) and at < 2):
                        pe.wait_ge(S["clipped"], at - 1)
                    for i in range(HKB):
                        kb = half * HKB + i
                        last = pe.matmul(ST[0:KB, k % 2, i // 3, (i % 3) * T:(i % 3 + 1) * T],
                                         KS[:, q, j, kb * KB:(kb + 1) * KB], QS[:, q, j, :],
                                         start=True, stop=True)
                    last.then_inc(S["st_ready"], 1)

                def weigh(n, q, half, piece):
                    if piece == 0:
                        pe.wait_ge(S["exp_done"], SETS * n + 4 * half + 4)
                    for i in (2 * piece, 2 * piece + 1):
                        kb = half * HKB + i
                        for j in range(4):
                            last = pe.matmul(OB[32 * j:32 * j + HD + 1, 0:T], V[:, q, kb, j, :],
                                             Pb[:, half, j, i * T:(i + 1) * T], start=(kb == 0),
                                             stop=(kb == NKB - 1), skip_group_check=True)
                    if piece == 2:
                        last.then_inc(S["pv_done"], 1)

                def turn_out(n, q):
                    pe.wait_ge(S["ot_sb"], n + 1)
                    pe.transpose(TO[0:T, :], OT[:, :], K["ident"][:, :]).then_inc(S["ot_turned"], 1)

                pe.wait_ge(S["zeroed"], 3)
                turn_queries(0, 0)
                turn_queries(1, 1)
                for q in (2, 3):
                    for k in range(SETS):
                        project(0, EARLY[q, k])

                def body(b, first, final):
                    for q in range(NQ):
                        n = NQ * b + q
                        for k in range(SETS):
                            if k == 0:
                                pe.wait_ge(stack_in[q], 7 * 16 * (b + 1))
                            score_set(n, q, k)
                            if k == 1 and q % 2 == 1:
                                pe.wait_ge(S["taken"], NPR * b + number["v", q // 2, NKB - 1] + 1)
                            if 1 <= k < 4 and not (first and q == 0):
                                weigh(n - 1, (q - 1) % NQ, 1, k - 1)
                            if k >= 5:
                                if k == 5 and not (first and q == 0):
                                    pe.wait_ge(S["ot_sb"], n)
                                if k == 5 and q % 2 == 0:
                                    pe.wait_ge(S["taken"], NPR * b + number["v", q // 2, HKB - 1] + 1)
                                weigh(n, q, 0, k - 5)
                            if k == 5 and not (first and q == 0):
                                turn_out(n - 1, (q - 1) % NQ)
                            if k == 7 and not (final and q >= 2):
                                if not (first and q == 0):
                                    pe.wait_ge(S["added"], n)
                                turn_queries(n + 2, (q + 2) % NQ)
                            if q < 2:
                                project(b, LATE[q, k])
                            elif not final:
                                project(b + 1, EARLY[q, k])
                body(0, True, False)
                with pe.Fori(1, B - 1) as b:
                    body(b, False, False)
                body(B - 1, False, True)
                n = STEPS - 1
                for piece in range(3):
                    weigh(n, 3, 1, piece)
                turn_out(n, 3)

            @block.scalar
            def _(act):
                def take(b, tasks):
                    for kind, hf, k in tasks:
                        at = number[kind, hf, k]
                        start = isinstance(b, int) and b == 0
                        if kind == "k":
                            lo, hi = CUTS[k:k + 2]
                            if k == 0 and not (start and hf == 0):
                                act.wait_ge(S["k3_done"], 2 * b + hf)
                            act.wait_ge(S["made"], NPR * b + at + 1)
                            act.activation(kf[:, lo:hi], PR[:, at % 2, 0:hi - lo], ACT.Identity,
                                           bias=bk[:, hf:hf + 1]).then_inc(S["taken"], 1)
                        else:
                            rows = KB if k < NKB - 1 else LASTKB
                            if k == 0 and not start:
                                act.wait_ge(S["pv_done"], 2 * (NQ * (b - 1) + 2 * hf + 2))
                            act.wait_ge(S["made"], NPR * b + at + 1)
                            act.activation(V[0:rows, 2 * hf:2 * hf + 2, k, :, 0:HD],
                                           PR[0:rows, at % 2, 0:P].rearrange("k (q h d) -> k q h d", q=2, h=4),
                                           ACT.Copy).then_inc(S["taken"], 1)

                def part1(b, hf):
                    act.wait_ge(S["taken"], NPR * b + KEYS_TAKEN[hf])
                    if not (isinstance(b, int) and b == 0 and hf == 0):
                        for q in ((2, 3) if hf == 0 else (0, 1)):
                            act.wait_ge(stack_in[q], 112 * (b if hf == 0 else b + 1))
                    act.activation(kp[:, 0, :], kf[:, :], ACT.Copy).then_inc(S["k1_done"], 1)

                def part2(b, hf):
                    act.wait_ge(S["r_done"], 2 * b + hf + 1)
                    act.activation(kp[:, 1, :], kf[:, :], ACT.Copy).then_inc(S["k2_done"], 1)

                def take_queries(n, q):
                    act.wait_ge(S["q_turned"], n + 1)
                    act.activation(QS[0:STK, q, :, :].rearrange("r h t -> r (h t)"), TQ[0:STK, 0:GT],
                                   ACT.Copy).then_inc(S["q_stacked"], 1)

                def exponential(n, k):
                    half, j = divmod(k, 4)
                    act.wait_ge(S["clipped"], SETS * n + k + 1)
                    if j == 0 and not (isinstance(n, int) and n == 0):
                        act.wait_ge(S["pv_done"], 2 * n + half - 1)
                    act.activation(Pb[:, half, j, :], Cb[:, k % 2, :], ACT.Exp, scale=HD ** -0.5
                                   ).then_inc(S["exp_done"], 1)

                act.wait_ge(S["zeroed"], 3)
                take_queries(0, 0)
                take_queries(1, 1)
                for q in (2, 3):
                    for k in range(SETS):
                        take(0, EARLY[q, k])
                        if (q, k) == (2, 4):
                            part1(0, 0)
                        if (q, k) == (3, 0):
                            part2(0, 0)

                def body(b, first, final):
                    for q in range(NQ):
                        n = NQ * b + q
                        for k in range(SETS):
                            exponential(n, k)
                            if k == 7 and not (final and q >= 2):
                                take_queries(n + 2, (q + 2) % NQ)
                            if q < 2:
                                take(b, LATE[q, k])
                            elif not final:
                                take(b + 1, EARLY[q, k])
                            if q == 0 and k == 1:
                                part1(b, 1)
                            if q == 0 and k == 5:
                                part2(b, 1)
                            if q == 2 and k == 4 and not final:
                                part1(b + 1, 0)
                            if q == 3 and k == 0 and not final:
                                part2(b + 1, 0)
                body(0, True, False)
                with act.Fori(1, B - 1) as b:
                    body(b, False, False)
                body(B - 1, False, True)

            @block.vector
            def _(dve):
                link = Chain(dve, S["chain"])
                link(dve.memset(V[:, :, :, :, :], 0.0))
                link(dve.memset(V[:, :, 0:NKB - 1, :, HD:HD + 1], 1.0))
                dve.memset(V[0:LASTKB, :, NKB - 1, :, HD:HD + 1], 1.0).then_inc(S["zeroed"], 1)
                link(dve.memset(kf[:, S2:S2P], 0.0))
                dve.memset(QS[STK:MROWS, :, :, :], 1.0).then_inc(S["zeroed"], 1)
                dve.memset(OB[:, :], 0.0).then_inc(S["zeroed"], 1)

                def clip(n, k):
                    at = SETS * n + k
                    dve.wait_ge(S["st_ready"], at + 1)
                    if not (isinstance(at, int) and at < 2):
                        dve.wait_ge(S["exp_done"], at - 1)
                    dve.tensor_scalar(Cb[:, k % 2, :].rearrange("k (c t) -> k c t", c=2), ST[0:KB, k % 2, :, 0:3 * T],
                                      LIM, -LIM, ALU.min, ALU.max).then_inc(S["clipped"], 1)

                def take_out(n, q):
                    dve.wait_ge(S["pv_done"], 2 * (n + 1))
                    dve.wait_ge(S["ot_turned"], n)
                    dve.tensor_copy(OT[:, :], OB[:, 0:T]).then_inc(S["ot_sb"], 1)

                def add_out(n, b, q):
                    dve.wait_ge(S["ot_turned"], n + 1)
                    o = TO[0:T, :].rearrange("t (j d) -> t j d", j=4)
                    link(dve.reciprocal(rz[:, :, :], o[:, :, HD:HD + 1]))
                    link(dve.tensor_tensor(sz[:, :, :], o[:, :, HD:HD + 1], rz[:, :, :], ALU.mult))
                    link(dve.tensor_scalar(sz[:, :, :], sz[:, :, :], 1e-8, None, ALU.add))
                    link(dve.reciprocal(sz[:, :, :], sz[:, :, :]))
                    link(dve.tensor_tensor(rz[:, :, :], rz[:, :, :], sz[:, :, :], ALU.mult))
                    xb = A[:, bass.ds(b, 1), 4 * HD * q:4 * HD * (q + 1)].rearrange("t o (j d) -> t (o j) d", d=HD)
                    link(dve.tensor_tensor(on[:, :, :], bv[:, 4 * HD * q:4 * HD * (q + 1)]
                                           .rearrange("t (j d) -> t j d", d=HD),
                                           o[:, :, HD:HD + 1].to_broadcast([T, 4, HD]), ALU.mult))
                    link(dve.tensor_tensor(on[:, :, :], on[:, :, :], o[:, :, 0:HD], ALU.add))
                    dve.tensor_tensor(xb, on[:, :, :], rz[:, :, :].to_broadcast([T, 4, HD]),
                                      ALU.mult).then_inc(S["added"], 1)

                def body(b, first, final):
                    for q in range(NQ):
                        n = NQ * b + q
                        for k in range(SETS):
                            clip(n, k)
                            if k == 3 and not (first and q == 0):
                                take_out(n - 1, (q - 1) % NQ)
                            if k == 6 and not (first and q == 0):
                                add_out(n - 1, b if q > 0 else b - 1, (q - 1) % NQ)
                body(0, True, False)
                with dve.Fori(1, B - 1) as b:
                    link.loop(b - 1, 7 * NQ)
                    body(b, False, False)
                link.end(B - 2)
                body(B - 1, False, True)
                take_out(STEPS - 1, 3)
                add_out(STEPS - 1, B - 1, 3)


def project_out(c, name, A, K, wo, bo):
    nc = c.nc
    with ExitStack() as s:
        c.stage = name
        AT = c.sb(s, "AT", [P, DC, N])
        features_first(c, name + "t", A, AT, K["ident"])
        c.stage = name
        QB = c.psum(s, "QB", [P, 8, 512])
        made = c.sem("made")
        with nc.Block() as block:
            @block.tensor
            def _(pe):
                for n in range(B):
                    dst = QB[0:T, n // 2, (n % 2) * D:(n % 2 + 1) * D]
                    for ch in range(DC):
                        last = pe.matmul(dst, AT[:, ch, n * T:(n + 1) * T], wo[:, ch, :], start=(ch == 0),
                                         stop=(ch == DC - 1))
                    last.then_inc(made, 1)

            @block.vector
            def _(dve):
                for n in range(8):
                    dve.wait_ge(made, 2 * n + 2)
                    dve.tensor_tensor(A[:, 2 * n:2 * n + 2, :], QB[0:T, n, :].rearrange("t (b d) -> t b d", b=2),
                                      bo[:, :].unsqueeze(1).to_broadcast([T, 2, D]), ALU.add)


def dispatched_experts(c, name, X, K, a):
    nc = c.nc
    with ExitStack() as s:
        c.stage = name
        XT = c.sb(s, "XT", [P, DC, N])
        w = weights(c, s, a, "L1f_", {"gate": [P, DC, E1], "tri": [T, T], "all": [T, T], "prio": [T, E1],
                                    "slot0": [T, E1], "oob": [T, B]})
        gatew, slot = c.sb(s, "gatew", [T, B]), c.sb(s, "slot", [T, B], I32)
        zeros = c.sb(s, "zeros", [T, B, D])
        w1, w2 = c.sb(s, "w1", [P, 2, DC, F1]), c.sb(s, "w2", [P, 2, F1 // P, D])
        cleared = clear_rows(c, name + "z", zeros, a)
        features_first(c, name + "t", X, XT, K["ident"])
        route_top1(c, name + "r", X, XT, K, w, gatew, slot, a)
        w_in = first_experts(c, name + "w", w1, w2, a)
        scatter_tokens(c, name + "s", X, slot, cleared, a)
        Y = zeros
        c.stage = name + "y"
        load(c, name + "d", [(Y[:, :, :], a["s_in"].rearrange("(b t) d -> t b d", t=T))])
        features_first(c, name + "u", Y, XT, K["ident"])
        expert_pairs(c, name + "e", XT, w1, w2, w_in, a)
        gather_tokens(c, name + "g", X, Y, slot, gatew, a)


def route_top1(c, name, X, XT, K, w, gatew, slot, a):
    c.stage = name
    nc = c.nc
    with ExitStack() as s:
        e, work, pick, loc, t2 = (c.sb(s, n, [T, B, E1]) for n in ("e", "work", "pick", "loc", "t2"))
        best, rank, z = (c.sb(s, n, [T, B, 1]) for n in ("best", "rank", "z"))
        valid, sf = c.sb(s, "valid", [T, B]), c.sb(s, "sf", [T, B])
        LG, CB, TB = (c.psum(s, n, [P, 512]) for n in ("LG", "CB", "TB"))
        chain, logits, shifted, exp_done, picked, counted = (c.sem(n) for n in (
            "chain", "logits", "shifted", "exp_done", "picked", "counted"))
        with nc.Block() as block:
            @block.tensor
            def _(pe):
                router_logits(pe, LG, XT, w["gate"], E1, logits)
                pe.wait_ge(picked, 1)
                ones = pick[:, :, :].rearrange("t b e -> t (b e)")
                pe.matmul(CB[0:T, 0:B * E1], w["tri"][:, :], ones, start=True, stop=True)
                pe.matmul(TB[0:T, 0:B * E1], w["all"][:, :], ones, start=True, stop=True).then_inc(counted, 1)

            @block.scalar
            def _(act):
                act.wait_ge(shifted, 1)
                act.activation(e[:, :, :], e[:, :, :], ACT.Exp).then_inc(exp_done, 1)

            @block.vector
            def _(dve):
                link = Chain(dve, chain)
                dve.wait_ge(logits, 1)
                lg = LG[0:T, 0:B * E1].rearrange("t (b e) -> t b e", b=B)
                wide = lambda t: t[:, :, :].to_broadcast([T, B, E1])
                link(dve.tensor_reduce(best[:, :, 0], lg, AX_X, ALU.max))
                dve.tensor_tensor(e[:, :, :], lg, wide(best), ALU.subtract).then_inc(shifted, 1)
                dve.wait_ge(exp_done, 1)
                link(dve.tensor_reduce(z[:, :, 0], e[:, :, :], AX_X, ALU.add))
                link(dve.reciprocal(z[:, :, :], z[:, :, :]))
                link(dve.tensor_tensor(e[:, :, :], e[:, :, :], wide(z), ALU.mult))
                first_of(link, dve, e, best, rank, pick, w["prio"][:, :], E1)
                dve.sem_inc(picked, 1)
                dve.wait_ge(counted, 1)
                link(dve.tensor_copy(loc[:, :, :], CB[0:T, 0:B * E1].rearrange("t (b e) -> t b e", b=B)))
                link(dve.tensor_copy(t2[:, :, :], TB[0:T, 0:B * E1].rearrange("t (b e) -> t b e", b=B)))
                link(dve.memset(work[:, :, :], 0.0))
                for b in range(1, B):
                    link(dve.tensor_tensor(work[:, b, :], work[:, b - 1, :], t2[:, b - 1, :], ALU.add))
                link(dve.tensor_tensor(loc[:, :, :], loc[:, :, :], work[:, :, :], ALU.add))
                link(dve.tensor_scalar(t2[:, :, :], loc[:, :, :], float(CAP), None, ALU.is_lt))
                link(dve.tensor_tensor(pick[:, :, :], pick[:, :, :], t2[:, :, :], ALU.mult))
                link(dve.tensor_reduce(valid[:, :], pick[:, :, :], AX_X, ALU.add))
                link(dve.tensor_tensor(e[:, :, :], e[:, :, :], pick[:, :, :], ALU.mult))
                link(dve.tensor_reduce(gatew[:, :], e[:, :, :], AX_X, ALU.add))
                link(dve.tensor_tensor(loc[:, :, :], loc[:, :, :],
                                       w["slot0"][:, :].unsqueeze(1).to_broadcast([T, B, E1]), ALU.add))
                link(dve.tensor_tensor(loc[:, :, :], loc[:, :, :], pick[:, :, :], ALU.mult))
                link(dve.tensor_reduce(sf[:, :], loc[:, :, :], AX_X, ALU.add))
                link(dve.tensor_scalar(valid[:, :], valid[:, :], -1.0, 1.0, ALU.mult, ALU.add))
                link(dve.tensor_tensor(valid[:, :], valid[:, :], w["oob"][:, :], ALU.mult))
                link(dve.tensor_tensor(sf[:, :], sf[:, :], valid[:, :], ALU.add))
                link(dve.tensor_copy(slot[:, :], sf[:, :]))


def clear_rows(c, name, zeros, a):
    c.stage = name
    zeroed, cleared = c.sem("zeroed"), c.sem("cleared")
    with c.nc.Block() as block:
        @block.vector
        def _(dve):
            dve.memset(zeros[:, :, :], 0.0).then_inc(zeroed, 1)

        @block.sync
        def _(sp):
            sp.wait_ge(zeroed, 1)
            sp.dma_start(a["s_in"].rearrange("(b t) d -> t b d", t=T), zeros[:, :, :]).then_inc(cleared, 16)
    return cleared


def scatter_tokens(c, name, X, slot, cleared, a):
    c.stage = name
    nc = c.nc
    with ExitStack():
        placed = c.sem("placed")
        with nc.Block() as block:
            @block.gpsimd
            def _(pool):
                pool.wait_ge(cleared, 16)
                for b in range(B):
                    pool.indirect_dma_start(
                        out=a["s_in"], out_offset=bass.IndirectOffsetOnAxis(ap=slot[:, b:b + 1], axis=0),
                        in_=X[:, b, :], in_offset=None, bounds_check=N - 1, oob_is_err=False).then_inc(placed, 16)
                pool.wait_ge(placed, 16 * B)


def load_expert(sp, w1, w2, e, i, w_in, a):
    for w, src in ((w1, a["L1f_w1"]), (w2, a["L1f_w2"])):
        sp.dma_start(w[:, i, :, :], src[bass.ds(e, 1), :, :, :].rearrange("o p c f -> (o p) c f")
                     ).then_inc(w_in[i], 16)


def first_experts(c, name, w1, w2, a):
    c.stage = name
    w_in = [c.sem(f"w_in{i}") for i in range(2)]
    with c.nc.Block() as block:
        @block.sync
        def _(sp):
            for i in range(2):
                load_expert(sp, w1, w2, i, i, w_in, a)
    return w_in


def expert_pairs(c, name, XT, w1, w2, w_in, a):
    c.stage = name
    nc = c.nc
    FC = F1 // P
    with ExitStack() as s:
        h = c.sb(s, "h", [P, 2, FC, CAP])
        O = c.sb(s, "O", [T, 2, 2, D])
        HB = c.psum(s, "HB", [P, 4, 512])
        OB = c.psum(s, "OB", [P, 2, 512])
        o_out = [c.sem(f"o_out{i}") for i in range(2)]
        made, gelu_done, out_ready, o_sb = (c.sem(n) for n in ("made", "gelu_done", "out_ready", "o_sb"))
        with nc.Block() as block:
            @block.sync
            def _(sp):
                def store(e, i):
                    sp.wait_ge(o_sb, e + 1)
                    sp.dma_start(a["s_out"][bass.ds(e * CAP, CAP), :].rearrange("(i t) d -> t i d", t=T),
                                 O[:, i, :, :]).then_inc(o_out[i], 16)
                with sp.Fori(0, E1 // 2 - 1) as p:
                    for i in range(2):
                        sp.wait_ge(out_ready, 2 * p + i + 1)
                        load_expert(sp, w1, w2, 2 * p + i + 2, i, w_in, a)
                        store(2 * p + i, i)
                for i in range(2):
                    store(E1 - 2 + i, i)
                for i in range(2):
                    sp.wait_ge(o_out[i], 16 * E1 // 2)

            @block.tensor
            def _(pe):
                with pe.Fori(0, E1 // 2) as p:
                    for i in range(2):
                        e = 2 * p + i
                        pe.wait_ge(w_in[i], 32 * (p + 1))
                        pe.wait_ge(gelu_done, 4 * e)
                        for k in range(FC):
                            for ch in range(DC):
                                last = pe.matmul(HB[:, k // 2, (k % 2) * CAP:(k % 2 + 1) * CAP],
                                                 w1[:, i, ch, k * P:(k + 1) * P], XT[:, ch, bass.ds(e * CAP, CAP)],
                                                 start=(ch == 0), stop=(ch == DC - 1))
                            if k % 2:
                                last.then_inc(made, 1)
                        pe.wait_ge(o_sb, e)
                        for k in range(FC):
                            pe.wait_ge(gelu_done, 4 * e + k // 2 + 1)
                            for j in range(2):
                                last = pe.matmul(OB[0:T, j, 0:D], h[:, i, k, j * T:(j + 1) * T], w2[:, i, k, :],
                                                 start=(k == 0), stop=(k == FC - 1))
                        last.then_inc(out_ready, 1)

            @block.scalar
            def _(act):
                with act.Fori(0, E1 // 2) as p:
                    for i in range(2):
                        e = 2 * p + i
                        if i == 1:
                            act.wait_ge(out_ready, e - 1)
                        else:
                            act.wait_ge(out_ready, 2 * p)
                        for k in range(FC // 2):
                            act.wait_ge(made, 4 * e + k + 1)
                            act.activation(h[:, i, 2 * k:2 * k + 2, :].rearrange("p c n -> p (c n)"),
                                           HB[:, k, 0:2 * CAP], ACT.Gelu_apprx_tanh).then_inc(gelu_done, 1)

            @block.vector
            def _(dve):
                with dve.Fori(0, E1 // 2) as p:
                    for i in range(2):
                        e = 2 * p + i
                        dve.wait_ge(out_ready, e + 1)
                        dve.wait_ge(o_out[i], 16 * p)
                        dve.tensor_copy(O[:, i, :, :], OB[0:T, :, 0:D]).then_inc(o_sb, 1)


def gather_tokens(c, name, X, Y, slot, gatew, a):
    c.stage = name
    nc = c.nc
    with ExitStack() as s:
        zeroed, came = c.sem("zeroed"), c.sem("came")
        with nc.Block() as block:
            @block.gpsimd
            def _(pool):
                pool.wait_ge(zeroed, 1)
                for b in range(B):
                    pool.indirect_dma_start(
                        out=Y[:, b, :], out_offset=None, in_=a["s_out"],
                        in_offset=bass.IndirectOffsetOnAxis(ap=slot[:, b:b + 1], axis=0),
                        bounds_check=N - 1, oob_is_err=False).then_inc(came, 16)

            @block.vector
            def _(dve):
                dve.memset(Y[:, :, :], 0.0).then_inc(zeroed, 1)
                dve.wait_ge(came, 16 * B)
                for b in range(B):
                    dve.scalar_tensor_tensor(out=X[:, b, :], in0=Y[:, b, :], scalar=gatew[:, b:b + 1],
                                             in1=X[:, b, :], op0=ALU.mult, op1=ALU.add)


def decoder(nc, a, out, stages=(1, 2, 3, 4, 5, 6)):
    with ExitStack() as ctx:
        c = Core(nc, ctx)
        c.stage = "all"
        a = dict(a)
        a["s_mask"] = nc.dram_tensor("s_mask", (B, 4, S2P), BF16, kind="Internal").ap()
        a["s_in"] = nc.dram_tensor("s_in", (N, D), F32, kind="Internal").ap()
        a["s_out"] = nc.dram_tensor("s_out", (N, D), F32, kind="Internal").ap()
        X = c.sb(ctx, "X", [T, B, D])
        K = {"ident": c.sb(ctx, "ident", [P, P]), "identb": c.sb(ctx, "identb", [P, P], BF16),
             "causal": c.sb(ctx, "causal", [T, GT], BF16), "headrows": c.sb(ctx, "headrows", [P, HH]),
             "ones": c.sb(ctx, "ones", [1, P])}
        nw = c.sb(ctx, "nw", [P, DC])
        load(c, "first", [(X[:, :, :], a["x"].rearrange("b t d -> t b d")), (nw[:, :], a["L0a_nw"])]
             + [(K[k][:, :], a["k_" + k]) for k in K])

        if 1 in stages:
            with ExitStack() as s:
                c.stage = "sa0"
                XT = c.sb(s, "XT", [P, DC, N])
                w, started = later_weights(c, s, a, "L0a_", {"wq": [P, DC, D], "wk": [P, DC, D], "wv": [P, DC, D],
                                                           "wo": [P, 4, D], "bq": [P, DC], "bk": [P, DC],
                                                           "bv": [1, D], "bo": [1, D]})
                features_first(c, "sa0n", X, XT, K["ident"], rms=True, weight=nw)
                end_load(c, started)
                narrow_attention(c, "sa0a", X, XT, K, w, HD ** -0.5, bias=True)
            layernorm(c, "sa0l", X)
            c.clear_sems()
        if 2 in stages:
            cross_attention_0(c, "xa0", X, K, a)
            layernorm(c, "xa0l", X)
            c.clear_sems()
        if 3 in stages:
            c.stage = "ff0"
            with ExitStack() as s:
                A = c.sb(s, "A", [T, B, D])
                latent_and_experts(c, X, A, K, a)
            c.clear_sems()
        if 4 in stages:
            with ExitStack() as s:
                c.stage = "sa1"
                XT = c.sb(s, "XT", [P, DC, N])
                w, started = later_weights(c, s, a, "L1a_", {"wq": [P, DC, D], "wk": [P, DC, D], "wqs": [P, DC, D],
                                                           "wks": [P, DC, D], "wv": [P, DC, D], "wo": [P, 4, D],
                                                           "rope": [P, 2, T]})
                rope = w["rope"]
                features_first(c, "sa1n", X, XT, K["ident"])
                end_load(c, started)
                narrow_attention(c, "sa1a", X, XT, K, w, HD ** -0.5, rope=rope)
            layernorm(c, "sa1l", X)
            c.clear_sems()
        if 5 in stages:
            cross_attention_1(c, "xa1", X, K, a)
            layernorm(c, "xa1l", X)
            c.clear_sems()
        if 6 in stages:
            dispatched_experts(c, "ff1", X, K, a)
            layernorm(c, "ff1l", X)

        c.stage = "end"
        stored = c.sem("stored")
        with nc.Block() as block:
            @block.sync
            def _(sp):
                sp.dma_start(out.rearrange("b t d -> t b d"), X[:, :, :]).then_inc(stored, 16)
                sp.wait_ge(stored, 16)


def weights(c, s, a, prefix, shapes):
    w = {k: c.sb(s, k, shape) for k, shape in shapes.items()}
    whole = lambda t: t[tuple(slice(None) for _ in t.shape)]
    load(c, c.stage + "w", [(whole(t), a[prefix + k]) for k, t in w.items()])
    return w


def later_weights(c, s, a, prefix, shapes):
    w = {k: c.sb(s, k, shape) for k, shape in shapes.items()}
    whole = lambda t: t[tuple(slice(None) for _ in t.shape)]
    return w, start_load(c, c.stage + "w", [(whole(t), a[prefix + k]) for k, t in w.items()])


def layouts(i):
    import numpy as np
    f32, bf = np.float32, mybir.dt.np(BF16)
    i = {k: np.asarray(v) for k, v in i.items()}
    rows = lambda wt: np.ascontiguousarray(wt.reshape(-1, P, wt.shape[1]).transpose(1, 0, 2))
    cols = lambda v: np.ascontiguousarray(v.reshape(-1, P).T)
    row = lambda v: v.reshape(1, -1)
    a = {"x": i["x"]}

    def padded_heads(wt):
        o = np.zeros((4, 32, 4, wt.shape[1]), f32)
        o[:, :HD] = wt.reshape(4, 4, HD, -1).transpose(1, 2, 0, 3)
        return o.reshape(P, 4, -1)

    for k in ("wq", "wk", "wv"):
        a["L0a_" + k] = rows(i["L0_attn_" + k].T)
    a["L0a_wo"] = padded_heads(i["L0_attn_wo"].T)
    a["L0a_nw"] = cols(i["L0_attn_norm_w"])
    for k in ("bq", "bk"):
        a["L0a_" + k] = cols(i["L0_attn_" + k])
    for k in ("bv", "bo"):
        a["L0a_" + k] = row(i["L0_attn_" + k])

    def swapped(wt):
        return wt.reshape(D, H, 2, HD // 2)[:, :, ::-1].reshape(D, D)

    a["L1a_wq"], a["L1a_wk"], a["L1a_wv"] = (rows(i["L1_attn_" + k].T) for k in ("Wq", "Wk", "Wv"))
    a["L1a_wqs"], a["L1a_wks"] = (rows(swapped(i["L1_attn_" + k].T)) for k in ("Wq", "Wk"))
    a["L1a_wo"] = padded_heads(i["L1_attn_Wo"].T)

    a["k_ident"], a["k_identb"] = np.eye(P, dtype=f32), np.eye(P, dtype=bf)
    q, k = np.arange(T)[:, None], np.arange(T)[None, :]
    a["k_causal"] = np.tile(np.where(k <= q, 0.0, NEG), (1, GB)).astype(bf)
    a["k_headrows"] = (np.arange(P)[:, None] // HD == np.arange(HH)[None, :]).astype(f32)
    a["k_ones"] = np.ones((1, P), f32)
    inv = (1.0 / 10000.0 ** (np.arange(0, HD, 2, dtype=f32) / HD)).astype(f32)
    freqs = np.arange(T, dtype=f32)[None, :] * inv[:, None]
    sin, cos = np.sin(freqs), np.cos(freqs)
    head = np.stack([np.concatenate([sin, sin]), np.concatenate([-cos, cos])], 1)
    a["L1a_rope"] = np.tile(head, (HH, 1, 1)).astype(f32)
    more_layouts(i, a, rows, cols, row, padded_heads)
    return a


def more_layouts(i, a, rows, cols, row, padded_heads):
    import numpy as np
    f32, bf = np.float32, mybir.dt.np(BF16)
    ctx = np.zeros((B, S2P, D), f32)
    ctx[:, :S2] = i["ctx_2048"]
    a["ctxT0"] = ctx.reshape(B, S2P, 2, 2, 4, HD).transpose(0, 2, 3, 5, 4, 1).reshape(B, 2, P, S2P)
    v = np.zeros((B, NQ, KB, NKB, 4, HD + 1), f32)
    v[..., :HD] = ctx.reshape(B, NKB, KB, NQ, 4, HD).transpose(0, 3, 2, 1, 4, 5)
    v[..., HD] = 1.0
    a["ctxV0"] = v.reshape(B, NQ, KB, -1)
    qw = i["L0_ffn_q_w"].reshape(H, P + 64, D)[:, :P].reshape(H * P, D)
    kv = i["L0_ffn_kv_w"]
    a["L0l_wq"], a["L0l_wk"], a["L0l_wv"] = rows(qw.T), rows(kv[:H * P].T), rows(kv[H * P:2 * H * P].T)
    a["L0l_wo"] = rows(i["L0_ffn_o_w"].T)
    a["L0l_nw"], a["L0m_nw"] = cols(i["L0_ffn_ln1_w"]), cols(i["L0_ffn_ln2_w"])
    a["L0m_gate"] = rows(i["L0_ffn_gate_w"].T)
    w1 = i["L0_ffn_w1"]
    a["L0m_wg"], a["L0m_wu"] = (rows(x.reshape(E0 * I0, D).T) for x in (w1[:, :I0], w1[:, I0:]))
    a["L0m_wd"] = rows(i["L0_ffn_w2"].transpose(0, 2, 1).reshape(E0 * I0, D))
    a["L0m_sg"], a["L0m_su"] = (rows(x.T) for x in (i["L0_ffn_sh_gu_w"][:SHI], i["L0_ffn_sh_gu_w"][SHI:]))
    sd = np.zeros((3 * P, D), f32)
    sd[:SHI] = i["L0_ffn_sh_down_w"].T
    a["L0m_sd"] = rows(sd)
    a["L0m_prio"] = np.tile(np.arange(E0, 0, -1, dtype=f32), (T, 1))
    r = np.arange(96)[:, None]
    a["k_experts"] = ((r % 32 < E0) & (r % 32 == np.arange(E0 * I0)[None, :] // I0)).astype(bf)
    a["ctxT1"] = ctx.reshape(B, S2P, DC, P).transpose(0, 3, 2, 1)
    a["L1x_wq"], a["L1x_wv"], a["L1x_wo"] = (rows(i["L1_xattn_" + k].T) for k in ("Wq", "Wv", "Wo"))
    quads = lambda v: v.reshape(2, 2, 4, HD, *v.shape[1:]).swapaxes(2, 3).reshape(v.shape)
    a["L1x_wk"] = rows(quads(i["L1_xattn_Wk"]).T)
    a["L1x_bk"] = cols(quads(i["L1_xattn_bk"]))
    for k in ("bq", "bv", "bo"):
        a["L1x_" + k] = i["L1_xattn_" + k]
    a["L1x_gamma"], a["L1x_beta"] = i["L1_xattn_ln_gamma"], i["L1_xattn_ln_beta"]
    a["L1x_rs"] = np.tile(i["L1_xattn_residual_scale"].reshape(1, 1), (T, 1))
    a["mask"] = np.zeros((B, S2P), np.int32)
    a["mask"][:, :S2] = i["mask_BxS2_ik0"]
    a["L1f_gate"] = rows(i["L1_ffn_w_gate"])
    a["L1f_w1"] = i["L1_ffn_w1"].reshape(E1, DC, P, F1).transpose(0, 2, 1, 3)
    a["L1f_w2"] = i["L1_ffn_w2"].reshape(E1, F1 // P, P, D).transpose(0, 2, 1, 3)
    t = np.arange(T)
    a["L1f_tri"] = (t[:, None] < t[None, :]).astype(f32)
    a["L1f_all"] = np.ones((T, T), f32)
    a["L1f_prio"] = np.tile(np.arange(E1, 0, -1, dtype=f32), (T, 1))
    a["L1f_slot0"] = np.tile(np.arange(E1, dtype=f32) * CAP, (T, 1))
    a["L1f_oob"] = (N + np.arange(B)[None, :] * T + t[:, None]).astype(f32)
    key, q = np.arange(MASK0, S2P)[None, :], np.arange(T)[:, None]
    a["k_one_rows"] = np.ones((PARTS, NQ, 4, S2P), bf)
    a["k_mask0"] = np.where(key <= q + S2 - T, 0.0, NEG).astype(bf)


def kernel(**inputs):
    import numpy as np
    import concourse.bacc as bacc
    from concourse.bass_utils import run_bass_kernel_spmd

    nc = bacc.Bacc("TRN2", target_bir_lowering=False, num_devices=1)
    arrays = {f"in_{k}": np.ascontiguousarray(v) for k, v in layouts(inputs).items()}
    a = {k[3:]: nc.dram_tensor(k, v.shape, mybir.dt.from_np(v.dtype), kind="ExternalInput").ap()
         for k, v in arrays.items()}
    out = nc.dram_tensor("out_x", (B, T, D), F32, kind="ExternalOutput").ap()
    decoder(nc, a, out)
    r = run_bass_kernel_spmd(nc, [arrays], core_ids=[0])
    return r.results[0]["out_x"]
```
